# Optimizing a Trainium2 kernel written in Bass

```python
import numpy as np
import jax
import jax.numpy as jnp

def _softmax(x, axis=-1):
    return jax.nn.softmax(x, axis=axis)

def _gelu(x):
    return jax.nn.gelu(x, approximate=True)

def _silu(x):
    return jax.nn.silu(x)

def _sigmoid(x):
    return jax.nn.sigmoid(x)

def _layernorm(x, axis=-1, eps=1e-05):
    m = jnp.mean(x, axis=axis, keepdims=True)
    v = jnp.var(x, axis=axis, keepdims=True)
    return (x - m) / jnp.sqrt(v + eps)

def _scatter_add(tgt, idx, src, axis=0):
    return tgt.at[idx].add(src)

def _segment_sum(src, seg, n):
    return jax.ops.segment_sum(src, seg, n)
kernel_name = 'mk_vit_tower_cls_d1_tok_img1024_r4_6f9102'

def setup_inputs(seed: int=0):
    np.random.seed(seed)
    _w = jnp.asarray

    def _rec_inputs():
        import jax
        import jax.numpy as jnp
        _rk = jax.random.key(seed)
        x = jax.random.uniform(jax.random.fold_in(_rk, 1), (16, 3, 256, 256), jnp.float32, 0.0, 1)
        cls_tok = 0.02 * jax.random.normal(jax.random.fold_in(_rk, 5), (1, 1, 256), jnp.float32)
        return (x, cls_tok)
    x, cls_tok = _rec_inputs()

    def _L0_tok_setup():
        import jax, jax.numpy as jnp
        import numpy as np
        _GRAY_W = (0.2989, 0.587, 0.114)
        key = jax.random.key(seed)
        x = jax.random.uniform(key, (32, 3, 256, 256), dtype=jnp.float32)
        sx = jnp.array([[-3.0, 0.0, 3.0], [-10.0, 0.0, 10.0], [-3.0, 0.0, 3.0]], dtype=jnp.float32)
        scharr = jnp.stack([sx, sx.T])[:, None, :, :]
        return {'x': x, 'scharr': scharr}
    _L0_tok_all = _L0_tok_setup()
    _L0_tok_in = {k: v for k, v in _L0_tok_all.items() if k in ('scharr',)}
    del _L0_tok_all

    def _L0_attn_setup():
        import jax, jax.numpy as jnp
        import numpy as np
        KEY_DIM = 256
        SCALE = KEY_DIM ** (-0.5)
        key = jax.random.key(seed)
        k1, k2, k3, k4 = jax.random.split(key, 4)
        B, S, E = (4, 512, 256)
        x = jax.random.normal(k1, (B, S, E), dtype=jnp.float32)
        WQ = jax.random.normal(k2, (KEY_DIM, E), dtype=jnp.float32) * E ** (-0.5)
        WK = jax.random.normal(k3, (KEY_DIM, E), dtype=jnp.float32) * E ** (-0.5)
        WV = jax.random.normal(k4, (KEY_DIM, E), dtype=jnp.float32) * E ** (-0.5)
        return {'x': x, 'WQ': WQ, 'WK': WK, 'WV': WV}
    _L0_attn_all = _L0_attn_setup()
    _L0_attn_in = {k: v for k, v in _L0_attn_all.items() if k in ('WQ', 'WK', 'WV')}
    del _L0_attn_all

    def _L0_ffn_setup():
        import jax, jax.numpy as jnp
        import numpy as np
        B, SEQ, DIM = (2, 1024, 256)
        E, S = (8, 128)
        HID = 4 * DIM
        SCALE = DIM ** 0.5

        def rmsnorm(x, gamma):
            n = jnp.linalg.norm(x, axis=-1, keepdims=True)
            return x / jnp.maximum(n, 1e-12) * SCALE * gamma
        key = jax.random.key(seed)
        ks = jax.random.split(key, 4)
        w_init = lambda k, shape: jax.random.normal(k, shape, dtype=jnp.float32) * 0.02
        return {'x': jax.random.normal(ks[0], (B, SEQ, DIM), dtype=jnp.float32), 'norm_gamma': jnp.ones((DIM,), jnp.float32), 'slot_norm_gamma': jnp.ones((DIM,), jnp.float32), 'slot_embeds': jax.random.normal(ks[1], (E, S, DIM), dtype=jnp.float32), 'w1': w_init(ks[2], (E, DIM, HID)), 'b1': jnp.zeros((E, HID), jnp.float32), 'w2': w_init(ks[3], (E, HID, DIM)), 'b2': jnp.zeros((E, DIM), jnp.float32)}
    _L0_ffn_all = _L0_ffn_setup()
    _L0_ffn_in = {k: v for k, v in _L0_ffn_all.items() if k in ('norm_gamma', 'slot_norm_gamma', 'slot_embeds', 'w1', 'b1', 'w2', 'b2')}
    del _L0_ffn_all
    return {'x': x, 'cls_tok': cls_tok, 'L0_tok_scharr': _L0_tok_in['scharr'], 'L0_attn_WQ': _L0_attn_in['WQ'], 'L0_attn_WK': _L0_attn_in['WK'], 'L0_attn_WV': _L0_attn_in['WV'], 'L0_ffn_norm_gamma': _L0_ffn_in['norm_gamma'], 'L0_ffn_slot_norm_gamma': _L0_ffn_in['slot_norm_gamma'], 'L0_ffn_slot_embeds': _L0_ffn_in['slot_embeds'], 'L0_ffn_w1': _L0_ffn_in['w1'], 'L0_ffn_b1': _L0_ffn_in['b1'], 'L0_ffn_w2': _L0_ffn_in['w2'], 'L0_ffn_b2': _L0_ffn_in['b2']}

def reference(x, cls_tok, L0_tok_scharr, L0_attn_WQ, L0_attn_WK, L0_attn_WV, L0_ffn_norm_gamma, L0_ffn_slot_norm_gamma, L0_ffn_slot_embeds, L0_ffn_w1, L0_ffn_b1, L0_ffn_w2, L0_ffn_b2):
    import jax
    import jax.numpy as jnp

    def _L0_tok_ref(x, scharr):
        import jax, jax.numpy as jnp
        import numpy as np
        _GRAY_W = (0.2989, 0.587, 0.114)
        w = jnp.asarray(_GRAY_W, dtype=x.dtype)
        gray = jnp.einsum('bchw,c->bhw', x, w)[:, None]
        edges = jax.lax.conv_general_dilated(gray, scharr, window_strides=(1, 1), padding='SAME', dimension_numbers=('NCHW', 'OIHW', 'NCHW'))
        abs_edges = jnp.sqrt(jnp.square(edges))
        edge = abs_edges.sum(axis=1) / 2
        return edge

    def _L0_attn_ref(x, WQ, WK, WV):
        import jax, jax.numpy as jnp
        import numpy as np
        KEY_DIM = 256
        SCALE = KEY_DIM ** (-0.5)
        q = jnp.einsum('bse,ke->bsk', x, WQ)
        k = jnp.einsum('bse,ke->bsk', x, WK)
        v = jnp.einsum('bse,ve->bsv', x, WV)
        scores = jnp.einsum('bsk,btk->bst', q, k) * SCALE
        masked = jnp.where(jnp.tril(scores) == 0, -jnp.inf, scores)
        attn = jax.nn.softmax(masked, axis=-1)
        return jnp.einsum('bst,btv->bsv', attn, v)

    def _L0_ffn_ref(x, norm_gamma, slot_norm_gamma, slot_embeds, w1, b1, w2, b2):
        import jax, jax.numpy as jnp
        import numpy as np
        B, SEQ, DIM = (2, 1024, 256)
        E, S = (8, 128)
        HID = 4 * DIM
        SCALE = DIM ** 0.5

        def rmsnorm(x, gamma):
            n = jnp.linalg.norm(x, axis=-1, keepdims=True)
            return x / jnp.maximum(n, 1e-12) * SCALE * gamma
        xn = rmsnorm(x, norm_gamma)
        sn = rmsnorm(slot_embeds, slot_norm_gamma)
        logits = jnp.einsum('bnd,esd->bnes', xn, sn)
        dispatch = jax.nn.softmax(logits, axis=1)
        b, n, e, s = logits.shape
        combine = jax.nn.softmax(logits.reshape(b, n, e * s), axis=-1)
        slots = jnp.einsum('bnd,bnes->besd', xn, dispatch)
        h = jnp.einsum('besd,edh->besh', slots, w1) + b1[None, :, None, :]
        h = jax.nn.gelu(h, approximate=False)
        eo = jnp.einsum('besh,ehd->besd', h, w2) + b2[None, :, None, :]
        eo = eo.reshape(b, e * s, DIM)
        out = jnp.einsum('bmd,bnm->bnd', eo, combine)
        return out
    h = _L0_tok_ref(x, L0_tok_scharr)
    h = jnp.concatenate([jnp.broadcast_to(cls_tok, (h.shape[0], 1, h.shape[2])), h], axis=1)
    h = h + _L0_attn_ref(_layernorm(h, axis=-1), L0_attn_WQ, L0_attn_WK, L0_attn_WV)
    h = h + _L0_ffn_ref(_layernorm(h, axis=-1), L0_ffn_norm_gamma, L0_ffn_slot_norm_gamma, L0_ffn_slot_embeds, L0_ffn_w1, L0_ffn_b1, L0_ffn_w2, L0_ffn_b2)
    return h

_drawn_inputs = setup_inputs


def setup_inputs(seed=0):
    import zlib

    import numpy as np

    out = dict(_drawn_inputs(seed))
    spreads = {'L0_ffn_norm_gamma': (1.0, 0.2),
     'L0_ffn_slot_norm_gamma': (1.0, 0.2),
     'L0_ffn_b1': (0.0, 0.658),
     'L0_ffn_b2': (0.0, 0.1)}
    factors = {}
    for name, (base, spread) in spreads.items():
        noise = np.random.default_rng([zlib.crc32(name.encode()), seed]).standard_normal(out[name].shape)
        drawn = base * np.exp(spread * noise) if base else spread * noise
        out[name] = jnp.asarray(drawn.astype(out[name].dtype))
    for name, factor in factors.items():
        out[name] = (out[name] * factor).astype(out[name].dtype)
    return out
```

```python
import concourse.bass as bass
from concourse import mybir
from contextlib import ExitStack


def vit_tower(
    nc: bass.Bass,
    x: bass.AP,
    cls_tok: bass.AP,
    scharr: bass.AP,
    wq: bass.AP,
    wk: bass.AP,
    wv: bass.AP,
    norm_gamma: bass.AP,
    slot_norm_gamma: bass.AP,
    slot_embeds: bass.AP,
    w1: bass.AP,
    b1: bass.AP,
    w2: bass.AP,
    b2: bass.AP,
    out: bass.AP,
):
    f32 = mybir.dt.float32
    f32r = mybir.dt.float32r
    ALU = mybir.AluOpType
    ACT = mybir.ActivationFunctionType
    AX = mybir.AxisListType

    P = 128
    B = x.shape[0]
    CH = x.shape[1]
    D = x.shape[3]
    R = x.shape[2] // P
    C = D // P
    NQ = R * P
    NT = NQ + 2
    E, DH = b1.shape
    M = slot_embeds.shape[0] * slot_embeds.shape[1]
    G = 4
    NG = B // G
    J = DH // P
    W = G * P
    RING = 4
    GRAY_W = (0.2989, 0.587, 0.114)
    EPS = 1e-5
    SCALE = float(D) ** -0.5
    RMS = float(D) ** 0.5
    BIG = 1e30
    XW = D + 2

    ctx = ExitStack()
    with ctx:
        def sem(name):
            return ctx.enter_context(nc.semaphore(name))

        def keep(name, shape, dt=f32):
            return ctx.enter_context(nc.sbuf_tensor(name, shape, dt))

        ident = keep("ident", [P, P])
        upper = keep("upper", [P, R, NT])
        qk_hi = keep("qk_hi", [P, C, D], f32r)
        qk_lo = keep("qk_lo", [P, C, D], f32r)
        wvT_hi = keep("wvT_hi", [P, C, D], f32r)
        wvT_lo = keep("wvT_lo", [P, C, D], f32r)
        snT_hi = keep("snT_hi", [P, C, M], f32r)
        snT_lo = keep("snT_lo", [P, C, M], f32r)
        b1T = keep("b1T", [P, E * J])
        gam = keep("gam", [P, C])
        taps = keep("taps", [P, 18])
        vcls_b = keep("vcls_b", [P, D])
        hcls_b = keep("hcls_b", [P, D])
        xcls_hi = keep("xcls_hi", [P, C, 2], f32r)
        xcls_lo = keep("xcls_lo", [P, C, 2], f32r)
        ycls3 = keep("ycls3", [3, D], f32r)
        lclsT = keep("lclsT", [P, E])
        ccls_hi = keep("ccls_hi", [P, E, 2], f32r)
        ccls_lo = keep("ccls_lo", [P, E, 2], f32r)
        rcls = keep("rcls", [P, 1])
        slot_hi = keep("slot_hi", [P, E, 2 * W], f32r)
        slot_lo = keep("slot_lo", [P, E, 2 * W], f32r)
        cexp = keep("cexp", [P, G, R, M])
        edge = keep("edge", [P, G, R, D])
        hres = keep("hres", [P, G, R, D])
        w1_in = keep("w1_in", [P, C, DH // 2])
        w2_in = keep("w2_in", [P, J // 2, D])
        b2_b = keep("b2_b", [P, D])
        mv1 = keep("mv1", [P, G * R, 2])
        mv1_b = keep("mv1_b", [P, R, 2])
        mv2 = keep("mv2", [P, G * R, 2])
        st1 = keep("st1", [P, R, 6])
        st2 = keep("st2", [P, R, 6])
        ve1 = keep("ve1", [P, G * R])
        sd1 = keep("sd1", [P, G * R])
        rstd1 = keep("rstd1", [P, G * R])
        ve2 = keep("ve2", [P, 2, G * R])
        sq2 = keep("sq2", [P, 2, G * R])
        rr2 = keep("rr2", [P, G * R])
        nn2 = keep("nn2", [P, G * R])
        rn2 = keep("rn2", [P, G * R])
        s2 = keep("s2", [P, G * R])
        mx = keep("mx", [P, R])
        negm = keep("negm", [P, R])
        asum = keep("asum", [P, 2, R])
        arinv = keep("arinv", [P, R])
        cmx = keep("cmx", [P, R])
        cneg = keep("cneg", [P, R])
        csum = keep("csum", [P, G * R])
        crinv = keep("crinv", [P, G * R])
        tmx = keep("tmx", [P, E])
        tmc = keep("tmc", [P, E])
        tneg = keep("tneg", [P, E])
        tdl = keep("tdl", [P, E])
        dsum = keep("dsum", [P, E])
        ecls = keep("ecls", [P, E])
        dtot = keep("dtot", [P, E])
        drinv = keep("drinv", [P, E])
        dcls = keep("dcls", [P, E])
        dclsh = keep("dclsh", [P, E], f32r)
        dc3 = keep("dc3", [P, E, 3])
        ocls = keep("ocls", [P, C, G])
        fcls = keep("fcls", [G, D])

        def phase(*specs):
            with ExitStack() as s:
                return [s.enter_context(nc.sbuf_tensor(n, sh, dt)) for n, sh, dt in specs]

        wq_n, wk_n, wv_n, sn_n, b1_n, sgam, gg, clsrow, junk, ssq, snorm, srin, cst, cmv, cve, csq, csc, \
            xc, xc_hi, xc_lo, gc_hi, gc_lo, cf, yc, yc_hi, yc_lo, y3, cmax, cnegm, csumc, cexpT = phase(
                ("wq_n", [P, C, D], f32), ("wk_n", [P, C, D], f32), ("wv_n", [P, C, D], f32),
                ("sn_n", [P, E, D], f32), ("b1_n", [E * J, P], f32), ("sgam", [P, C], f32),
                ("gg", [P, C], f32), ("clsrow", [P, D], f32), ("junk", [P, M], f32),
                ("ssq", [P, E], f32), ("snorm", [P, E], f32), ("srin", [P, E], f32),
                ("cst", [P, 2, 6], f32), ("cmv", [P, 2, 2], f32), ("cve", [P, 4], f32),
                ("csq", [P, 4], f32), ("csc", [P, 8], f32),
                ("xc", [P, D], f32), ("xc_hi", [P, C, P], f32r), ("xc_lo", [P, C, P], f32r),
                ("gc_hi", [P, C, P], f32r), ("gc_lo", [P, C, P], f32r), ("cf", [P, 4], f32),
                ("yc", [P, D], f32), ("yc_hi", [P, C, P], f32r), ("yc_lo", [P, C, P], f32r),
                ("y3", [P, C, 3], f32), ("cmax", [P, 1], f32), ("cnegm", [P, 1], f32),
                ("csumc", [P, 1], f32), ("cexpT", [P, E], f32))
        xhat, xT_hi, xT_lo, g_hi, g_lo, v_hi, v_lo, masked, sm, prob, pT_hi, pT_lo, osum = phase(
            ("xhat", [P, 2, R, D], f32), ("xT_hi", [P, 2, C, NT], f32r), ("xT_lo", [P, 2, C, NT], f32r),
            ("g_hi", [P, C, NQ], f32r), ("g_lo", [P, C, NQ], f32r),
            ("v_hi", [P, 2, R, D], f32r), ("v_lo", [P, 2, R, D], f32r),
            ("masked", [P, R, NT], f32), ("sm", [P, R, NT], f32), ("prob", [P, 2, R, NT], f32),
            ("pT_hi", [P, R, NQ], f32r), ("pT_lo", [P, R, NQ], f32r), ("osum", [P, R, D], f32))
        y, y_hi, y_lo, yT_hi, yT_lo, lsb, dT, d_hi, d_lo, d3 = phase(
            ("y", [P, 2, R, D], f32), ("y_hi", [P, 2, R, D], f32r), ("y_lo", [P, 2, R, D], f32r),
            ("yT_hi", [P, C, NQ], f32r), ("yT_lo", [P, C, NQ], f32r), ("lsb", [P, R, M], f32),
            ("dT", [P, E, NQ], f32), ("d_hi", [P, R, M], f32r), ("d_lo", [P, R, M], f32r),
            ("d3", [3, M], f32r))
        w1_hi, w1_lo, w2_hi, w2_lo, act_g, hT_hi, hT_lo, eo_f, xrow, gray, acc0, acc1 = phase(
            ("w1_hi", [P, RING, C, P], f32r), ("w1_lo", [P, RING, C, P], f32r),
            ("w2_hi", [P, RING, D], f32r), ("w2_lo", [P, RING, D], f32r),
            ("act_g", [P, 2, W], f32), ("hT_hi", [P, RING, W], f32r), ("hT_lo", [P, RING, W], f32r),
            ("eo_f", [P, 2 * W], f32),
            ("xrow", [P, CH, R * D], f32), ("gray", [P, R + 2, XW], f32),
            ("acc0", [P, R, D], f32), ("acc1", [P, R, D], f32))
        cT_hi, cT_lo, oT = phase(
            ("cT_hi", [P, 2, E, NT], f32r), ("cT_lo", [P, 2, E, NT], f32r), ("oT", [P, 2, C, NT], f32))

        ps = ctx.enter_context(nc.psum_tensor("ps", [P, 8 * 512], f32))

        def bank(k, n=1):
            return ps[:, 512 * k:512 * (k + n)]

        passed = sem("passed")
        const_loaded = sem("const_loaded")
        pool_setup = sem("pool_setup")
        masks_ready = sem("masks_ready")
        pe_setup = sem("pe_setup")
        act_setup = sem("act_setup")
        square_link = sem("square_link")
        dve_setup = sem("dve_setup")
        halo_zero = sem("halo_zero")
        x_loaded = sem("x_loaded")
        gray_first = sem("gray_first")
        gray_done = sem("gray_done")
        halo_loaded = sem("halo_loaded")
        token_link = sem("token_link")
        edge_done = sem("edge_done")
        ve1_ready = sem("ve1_ready")
        sd1_ready = sem("sd1_ready")
        attn_link = sem("attn_link")
        xhat_ready = sem("xhat_ready")
        xT_ready = sem("xT_ready")
        xT_rounded = sem("xT_rounded")
        xT_split = sem("xT_split")
        g_ready = sem("g_ready")
        g_rounded = sem("g_rounded")
        g_split = sem("g_split")
        v_ready = sem("v_ready")
        v_rounded = sem("v_rounded")
        v_split = sem("v_split")
        scores_ready = sem("scores_ready")
        scores_masked = sem("scores_masked")
        negm_ready = sem("negm_ready")
        prob_ready = sem("prob_ready")
        pT_ready = sem("pT_ready")
        pT_rounded = sem("pT_rounded")
        pT_split = sem("pT_split")
        attn_ready = sem("attn_ready")
        h_ready = sem("h_ready")
        ve2_ready = sem("ve2_ready")
        sq2_ready = sem("sq2_ready")
        disp_link = sem("disp_link")
        y_ready = sem("y_ready")
        y_rounded = sem("y_rounded")
        y_split = sem("y_split")
        yT_ready = sem("yT_ready")
        yT_rounded = sem("yT_rounded")
        yT_split = sem("yT_split")
        logits_ready = sem("logits_ready")
        lsb_ready = sem("lsb_ready")
        cneg_ready = sem("cneg_ready")
        cexp_ready = sem("cexp_ready")
        lT_ready = sem("lT_ready")
        tneg_ready = sem("tneg_ready")
        dT_exp = sem("dT_exp")
        dT_scaled = sem("dT_scaled")
        d_ready = sem("d_ready")
        d_rounded = sem("d_rounded")
        d_split = sem("d_split")
        d3_ready = sem("d3_ready")
        d3_copied = sem("d3_copied")
        slots_ready = sem("slots_ready")
        slots_rounded = sem("slots_rounded")
        slots_split = sem("slots_split")
        w_loaded = sem("w_loaded")
        b2_loaded = sem("b2_loaded")
        w_link = sem("w_link")
        w_split = sem("w_split")
        tile_free = sem("tile_free")
        hbank_free = sem("hbank_free")
        hidden_ready = sem("hidden_ready")
        hT_rounded = sem("hT_rounded")
        hT_split = sem("hT_split")
        eo_summed = sem("eo_summed")
        eo_rounded = sem("eo_rounded")
        eo_split = sem("eo_split")
        crinv_ready = sem("crinv_ready")
        cT_ready = sem("cT_ready")
        cT_rounded = sem("cT_rounded")
        cT_split = sem("cT_split")
        outT_ready = sem("outT_ready")
        outT_copied = sem("outT_copied")
        fin_ready = sem("fin_ready")
        fin_done = sem("fin_done")
        out_stored = sem("out_stored")
        fcls_ready = sem("fcls_ready")
        fcls_done = sem("fcls_done")
        cls_stored = sem("cls_stored")

        block = ctx.enter_context(nc.Block())

        def apart(eng):
            eng.sem_inc(passed, 1)

        def over_groups(eng, body):
            with eng.Fori(0, NG - 1) as g:
                body(g, False)
            body(NG - 1, True)

        @block.sync
        def _(sp):
            rows = lambda a: a.rearrange("(c p) n -> p c n", p=P)
            sp.dma_start(xrow[:, :, :], x[0].rearrange("c (p r) w -> p c (r w)", p=P)).then_inc(x_loaded, 16)
            sp.dma_start(taps[:, :], scharr.rearrange("k a y x -> a (k y x)").to_broadcast([P, 18]))\
              .then_inc(const_loaded, 16)
            sp.dma_start(clsrow[:, :], cls_tok[0].to_broadcast([P, D])).then_inc(const_loaded, 16)
            sp.dma_start(wq_n[:, :, :], rows(wq)).then_inc(const_loaded, 16)
            sp.dma_start(wk_n[:, :, :], rows(wk)).then_inc(const_loaded, 16)
            sp.dma_start(wv_n[:, :, :], rows(wv)).then_inc(const_loaded, 16)
            sp.dma_start(sn_n[:, :, :], slot_embeds.rearrange("e s d -> s e d")).then_inc(const_loaded, 16)
            sp.dma_start(b1_n[:, :], b1.rearrange("e (j p) -> (e j) p", p=P)).then_inc(const_loaded, 16)
            with nc.allow_non_contiguous_dma(reason="two columns of 128 scales"):
                sp.dma_start(gam[:, :], norm_gamma.rearrange("(c p) -> p c", p=P)).then_inc(const_loaded, 16)
                sp.dma_start(sgam[:, :], slot_norm_gamma.rearrange("(c p) -> p c", p=P))\
                  .then_inc(const_loaded, 16)

            def load_image(i):
                sp.wait_ge(gray_done, i)
                sp.dma_start(xrow[:, :, :], x[i].rearrange("c (p r) w -> p c (r w)", p=P))\
                  .then_inc(x_loaded, 16)

            def load_halo(i):
                sp.wait_ge(gray_done, i + 1)
                sp.dma_start(gray[1:113, 0, 1:D + 1], gray[0:112, R, 1:D + 1]).then_inc(halo_loaded, 16)
                sp.dma_start(gray[113:P, 0, 1:D + 1], gray[112:P - 1, R, 1:D + 1]).then_inc(halo_loaded, 16)
                sp.dma_start(gray[0:112, R + 1, 1:D + 1], gray[1:113, 1, 1:D + 1]).then_inc(halo_loaded, 16)
                sp.dma_start(gray[112:P - 1, R + 1, 1:D + 1], gray[113:P, 1, 1:D + 1])\
                  .then_inc(halo_loaded, 16)

            def load_half(g, e, half):
                q = (g * E + e) * 2 + half
                sp.wait_ge(w_split, q * J + 1)
                sp.dma_start(w1_in[:, :, :], w1[e].rearrange("(c p) h -> p c h", p=P)
                             [:, :, half * DH // 2:(half + 1) * DH // 2]).then_inc(w_loaded, 16)
                sp.dma_start(w2_in[:, :, :], w2[e].rearrange("(j p) d -> p j d", p=P)
                             [:, half * J // 2:(half + 1) * J // 2, :]).then_inc(w_loaded, 16)

            def load_b2(g, e):
                sp.wait_ge(eo_summed, g * E + e + 1)
                sp.dma_start(b2_b[:, :], b2[e].rearrange("(a d) -> a d", a=1).to_broadcast([P, D]))\
                  .then_inc(b2_loaded, 16)

            load_halo(0)
            for i in range(1, G):
                load_image(i)
                load_halo(i)

            def group(g, last):
                if last:
                    with sp.Fori(0, E) as e:
                        load_half(g, e, 0)
                        load_half(g, e, 1)
                        load_b2(g, e)
                else:
                    with sp.Fori(0, E // 2) as pair:
                        i = g * G + G + pair
                        load_half(g, pair * 2, 0)
                        load_image_next(g, pair, i)
                        load_half(g, pair * 2, 1)
                        load_b2(g, pair * 2)
                        load_halo(i)
                        load_half(g, pair * 2 + 1, 0)
                        load_half(g, pair * 2 + 1, 1)
                        load_b2(g, pair * 2 + 1)
                for b in range(G):
                    sp.wait_ge(fin_done, g * G + b + 1)
                    sp.dma_start(out[g * G + b, 1:1 + NQ, :].rearrange("(p r) d -> p r d", r=R),
                                 hres[:, b, :, :]).then_inc(out_stored, 16)
                sp.wait_ge(fcls_done, g + 1)
                apart(sp)
                sp.dma_start(out[bass.ds(g * G, G), 0, :], fcls[:, :]).then_inc(cls_stored, 16)

            def load_image_next(g, pair, i):
                sp.wait_ge(slots_split, (g + 1) * G * C)
                load_image(i)

            over_groups(sp, group)
            sp.wait_ge(out_stored, 16 * B + 1)
            sp.wait_ge(cls_stored, 16 * NG + 1)

        @block.gpsimd
        def _(pool):
            pool.sem_inc(tile_free, RING)
            pool.sem_inc(hbank_free, RING)
            pool.sem_inc(hT_split, 2)
            for s in (w_split, eo_summed, out_stored, cls_stored):
                pool.sem_inc(s, 1)
            nc.gpsimd.memset(ident[:, :], 0.0).then_inc(pool_setup, 1)
            nc.gpsimd.memset(upper[:, :, :], 0.0).then_inc(pool_setup, 1)
            pool.wait_ge(pool_setup, 2)
            nc.gpsimd.affine_select(out=ident[:, :], in_=ident[:, :], compare_op=ALU.not_equal, fill=1.0,
                                    base=0, pattern=[[-1, P]], channel_multiplier=1).then_inc(masks_ready, 1)
            for r in range(R):
                v = upper[:, r, 0:NQ].rearrange("p (a b) -> p a b", a=R)
                nc.gpsimd.affine_select(out=v, in_=v, compare_op=ALU.is_ge, fill=1.0, base=r,
                                        pattern=[[-1, R], [-R, P]], channel_multiplier=R)\
                  .then_inc(masks_ready, 1)
                nc.gpsimd.memset(upper[:, r, NT - 1:NT], 1.0).then_inc(masks_ready, 1)

            def split_tile(g, e, j):
                t = (g * E + e) * J + j
                q = (g * E + e) * 2 + j // (J // 2)
                k, jj = j % RING, j % (J // 2)
                if jj == 0:
                    pool.wait_ge(w_loaded, 32 * q + 32)
                pool.wait_ge(tile_free, t + 1)
                apart(pool)
                w1v = w1_in[:, :, jj * P:(jj + 1) * P]
                nc.gpsimd.tensor_copy(w1_hi[:, k, :, :], w1v).then_inc(w_link, 1)
                nc.gpsimd.tensor_copy(w2_hi[:, k, :], w2_in[:, jj, :]).then_inc(w_link, 1)
                pool.wait_ge(w_link, 2 * t + 2)
                nc.gpsimd.tensor_tensor(w1_lo[:, k, :, :], w1v, w1_hi[:, k, :, :].bitcast(f32), ALU.subtract)\
                  .then_inc(w_split, 1)
                nc.gpsimd.tensor_tensor(w2_lo[:, k, :], w2_in[:, jj, :], w2_hi[:, k, :].bitcast(f32),
                                        ALU.subtract).then_inc(w_split, 1)

            def group(g, last):
                pool.wait_ge(slots_split, (g + 1) * G * C)
                apart(pool)
                with pool.Fori(0, E) as e:
                    for j in range(J):
                        split_tile(g, e, j)

            over_groups(pool, group)

        @block.tensor
        def _(pe):
            def mm3(o, w_hi, w_lo, x_hi, x_lo, first, last, shared=False):
                nc.tensor.matmul(o, w_lo, x_hi, start=first, stop=False, skip_group_check=shared)
                nc.tensor.matmul(o, w_hi, x_lo, start=False, stop=False, skip_group_check=shared)
                return nc.tensor.matmul(o, w_hi, x_hi, start=False, stop=last, skip_group_check=shared)

            def transpose(o, i):
                return nc.tensor.transpose(o, i, ident[0:i.shape[0], 0:i.shape[0]])

            pe.wait_ge(const_loaded, 16 * 9)
            pe.wait_ge(masks_ready, 1)
            for ec in range(C):
                for kc in range(C):
                    m = nc.tensor.matmul(bank(0)[:, ec * D:(ec + 1) * D], wq_n[:, kc, ec * P:(ec + 1) * P],
                                         wk_n[:, kc, :], start=kc == 0, stop=kc == C - 1)
            for vc in range(C):
                for ec in range(C):
                    transpose(bank(1)[:, ec * D + vc * P:ec * D + (vc + 1) * P],
                              wv_n[:, vc, ec * P:(ec + 1) * P])
            transpose(bank(2)[:, 0:E * J], b1_n[:, :]).then_inc(pe_setup, 1)
            pe.wait_ge(dve_setup, 1)
            for c in range(C):
                for e in range(E):
                    m = transpose(bank(4 + 2 * c + e // 4)[:, e % 4 * P:(e % 4 + 1) * P],
                                  sn_n[:, e, c * P:(c + 1) * P])
            m.then_inc(pe_setup, 1)
            pe.wait_ge(dve_setup, 2)
            pe.wait_ge(dve_setup, 3)
            for c in range(C):
                m = transpose(bank(0)[:, c * P:(c + 1) * P], xc[:, c * P:(c + 1) * P])
            m.then_inc(pe_setup, 1)
            pe.wait_ge(dve_setup, 4)
            for c in range(C):
                mm3(bank(1)[:, 0:D], xc_hi[:, c, :], xc_lo[:, c, :], wvT_hi[:, c, :], wvT_lo[:, c, :],
                    c == 0, c == C - 1)
            for c2 in range(C):
                for c in range(C):
                    m = mm3(bank(2)[:, c2 * P:(c2 + 1) * P], qk_hi[:, c, c2 * P:(c2 + 1) * P],
                            qk_lo[:, c, c2 * P:(c2 + 1) * P], xc_hi[:, c, :], xc_lo[:, c, :],
                            c == 0, c == C - 1)
            m.then_inc(pe_setup, 1)
            pe.wait_ge(dve_setup, 5)
            for c in range(C):
                m = mm3(bank(3)[:, 0:P], gc_hi[:, c, :], gc_lo[:, c, :], xc_hi[:, c, :], xc_lo[:, c, :],
                        c == 0, c == C - 1)
            m.then_inc(pe_setup, 1)
            pe.wait_ge(dve_setup, 6)
            for c in range(C):
                m = transpose(bank(0)[:, c * P:(c + 1) * P], yc[:, c * P:(c + 1) * P])
            m.then_inc(pe_setup, 1)
            pe.wait_ge(dve_setup, 7)
            for half in range(2):
                for c in range(C):
                    mm3(bank(4 + half), yc_hi[:, c, :], yc_lo[:, c, :],
                        snT_hi[:, c, half * 512:(half + 1) * 512], snT_lo[:, c, half * 512:(half + 1) * 512],
                        c == 0, c == C - 1)
            for e in range(E):
                for c in range(C):
                    mm3(bank(6)[:, 2 * e:2 * e + 2], snT_hi[:, c, e * P:(e + 1) * P],
                        snT_lo[:, c, e * P:(e + 1) * P], yc_hi[:, c, 0:2], yc_lo[:, c, 0:2],
                        c == 0, c == C - 1)
            for c in range(C):
                m = transpose(bank(7)[0:3, c * P:(c + 1) * P], y3[:, c, :])
            m.then_inc(pe_setup, 1)
            pe.wait_ge(dve_setup, 9)

            def attn_xT(g, b):
                n = g * G + b
                pe.wait_ge(xhat_ready, n + 1)
                if b >= 2:
                    pe.wait_ge(xT_split, n - 1)
                for r in range(R):
                    for c in range(C):
                        m = transpose(bank(b % 2)[:, c * NQ + r * P:c * NQ + (r + 1) * P],
                                      xhat[:, b % 2, r, c * P:(c + 1) * P])
                m.then_inc(xT_ready, 1)

            def attn_scores(g, b):
                n, k = g * G + b, b % 2
                pe.wait_ge(xT_split, n + 1)
                for c2 in range(C):
                    for c in range(C):
                        m = mm3(bank(2)[:, c2 * NQ:(c2 + 1) * NQ], qk_hi[:, c, c2 * P:(c2 + 1) * P],
                                qk_lo[:, c, c2 * P:(c2 + 1) * P], xT_hi[:, k, c, 0:NQ], xT_lo[:, k, c, 0:NQ],
                                c == 0, c == C - 1)
                m.then_inc(g_ready, 1)
                if b >= 1:
                    pe.wait_ge(v_split, n)
                for r in range(R):
                    for c in range(C):
                        m = mm3(bank(3)[:, r * D:(r + 1) * D], xT_hi[:, k, c, r * P:(r + 1) * P],
                                xT_lo[:, k, c, r * P:(r + 1) * P], wvT_hi[:, c, :], wvT_lo[:, c, :],
                                c == 0, c == C - 1)
                m.then_inc(v_ready, 1)
                pe.wait_ge(g_split, n + 1)
                if b >= 1:
                    pe.wait_ge(scores_masked, n)
                for r in range(R):
                    for c in range(C):
                        m = mm3(bank(4 + r)[:, 0:NT], g_hi[:, c, r * P:(r + 1) * P],
                                g_lo[:, c, r * P:(r + 1) * P], xT_hi[:, k, c, :], xT_lo[:, k, c, :],
                                c == 0, c == C - 1)
                m.then_inc(scores_ready, 1)

            def attn_out(g, b):
                n, k = g * G + b, b % 2
                pe.wait_ge(prob_ready, n + 1)
                for r in range(R):
                    for r2 in range(R):
                        m = transpose(bank(6)[:, r2 * NQ + r * P:r2 * NQ + (r + 1) * P],
                                      prob[:, k, r, r2 * P:(r2 + 1) * P])
                m.then_inc(pT_ready, 1)
                pe.wait_ge(pT_split, n + 1)
                pe.wait_ge(v_split, n + 1)
                if b >= 1:
                    pe.wait_ge(h_ready, n)
                for r in range(R):
                    for r2 in range(R):
                        m = mm3(bank(7)[:, r * D:(r + 1) * D], pT_hi[:, r2, r * P:(r + 1) * P],
                                pT_lo[:, r2, r * P:(r + 1) * P], v_hi[:, k, r2, :], v_lo[:, k, r2, :],
                                r2 == 0, r2 == R - 1)
                m.then_inc(attn_ready, 1)

            def disp_yT(g, b):
                n = g * G + b
                pe.wait_ge(y_ready, n + 1)
                if b >= 1:
                    pe.wait_ge(lsb_ready, n * R)
                for r in range(R):
                    for c in range(C):
                        m = transpose(bank(3)[:, c * NQ + r * P:c * NQ + (r + 1) * P],
                                      y[:, b % 2, r, c * P:(c + 1) * P])
                m.then_inc(yT_ready, 1)

            def disp_logits(g, b):
                n = g * G + b
                pe.wait_ge(yT_split, n + 1)
                for r in range(R):
                    for half in range(2):
                        for c in range(C):
                            m = mm3(bank(2 * r + half), yT_hi[:, c, r * P:(r + 1) * P],
                                    yT_lo[:, c, r * P:(r + 1) * P],
                                    snT_hi[:, c, half * 512:(half + 1) * 512],
                                    snT_lo[:, c, half * 512:(half + 1) * 512], c == 0, c == C - 1)
                    m.then_inc(logits_ready, 1)

            def disp_lT(g, b):
                n = g * G + b
                pe.wait_ge(lsb_ready, n * R + R)
                if b >= 1:
                    pe.wait_ge(slots_split, n * C)
                for e in range(E):
                    for r in range(R):
                        m = transpose(bank(4 + e // 2)[:, e % 2 * NQ + r * P:e % 2 * NQ + (r + 1) * P],
                                      lsb[:, r, e * P:(e + 1) * P])
                m.then_inc(lT_ready, 1)

            def disp_slots(g, b):
                n, k = g * G + b, b % 2
                pe.wait_ge(dT_scaled, n + 1)
                if b < G - 1:
                    pe.wait_ge(lsb_ready, n * R + 2 * R)
                for r in range(R):
                    for e in range(E):
                        m = transpose(bank(2 * r + e // 4)[:, e % 4 * P:(e % 4 + 1) * P],
                                      dT[:, e, r * P:(r + 1) * P])
                    m.then_inc(d_ready, 1)
                for e in range(E):
                    m = transpose(bank(4 + e // 4)[0:3, e % 4 * P:(e % 4 + 1) * P], dc3[:, e, :])
                m.then_inc(d3_ready, 1)
                pe.wait_ge(d_split, n * R + R)
                pe.wait_ge(y_split, n + 1)
                pe.wait_ge(d3_copied, n + 1)
                for c in (1, 0):
                    for half in range(2):
                        h = slice(half * 512, (half + 1) * 512)
                        for r in range(R):
                            mm3(bank(4 + 2 * c + half), y_hi[:, k, r, c * P:(c + 1) * P],
                                y_lo[:, k, r, c * P:(c + 1) * P], d_hi[:, r, h], d_lo[:, r, h], r == 0, False)
                        m = nc.tensor.matmul(bank(4 + 2 * c + half), ycls3[:, c * P:(c + 1) * P], d3[:, h],
                                             start=False, stop=True)
                    m.then_inc(slots_ready, 1)

            def hidden(g, e, j):
                t = (g * E + e) * J + j
                k = j % RING
                pe.wait_ge(w_split, 2 * t + 3)
                pe.wait_ge(hbank_free, t + 1)
                for c in range(C):
                    m = mm3(bank(k), w1_hi[:, k, c, :], w1_lo[:, k, c, :],
                            slot_hi[:, e, c * W:(c + 1) * W], slot_lo[:, e, c * W:(c + 1) * W],
                            c == 0, c == C - 1)
                m.then_inc(hidden_ready, 1)

            def expert_out(g, e, j):
                t = (g * E + e) * J + j
                k = j % RING
                pe.wait_ge(hT_split, t + 3)
                if j == 0:
                    pe.wait_ge(eo_summed, g * E + e + 1)
                for b in range(G):
                    o = bank(4 + b // 2)[:, b % 2 * D:(b % 2 + 1) * D]
                    m = mm3(o, hT_hi[:, k, b * P:(b + 1) * P], hT_lo[:, k, b * P:(b + 1) * P],
                            w2_hi[:, k, :], w2_lo[:, k, :], j == 0 and b % 2 == 0, j == J - 1, shared=True)
                m.then_inc(tile_free, 1)

            def comb_cT(g, b):
                n = g * G + b
                if b >= 1:
                    pe.wait_ge(cT_split, n * E // 2)
                for e in range(E):
                    for r in range(R):
                        m = transpose(bank(e // 2)[:, e % 2 * NQ + r * P:e % 2 * NQ + (r + 1) * P],
                                      cexp[:, b, r, e * P:(e + 1) * P])
                    if e % 2:
                        m.then_inc(cT_ready, 1)

            def comb_out(g, b):
                n = g * G + b
                if b == 0:
                    pe.wait_ge(crinv_ready, g + 1)
                    pe.wait_ge(eo_split, (g + 1) * E)
                pe.wait_ge(cT_split, (n + 1) * E // 2)
                if b >= 1:
                    pe.wait_ge(outT_copied, n * C)
                for c in range(C):
                    for e in range(E):
                        o = b * D + c * P
                        m = mm3(bank(4 + c)[:, 0:NT], slot_hi[:, e, o:o + P], slot_lo[:, e, o:o + P],
                                cT_hi[:, b % 2, e, :], cT_lo[:, b % 2, e, :], e == 0, e == E - 1)
                    m.then_inc(outT_ready, 1)

            def comb_fin(g, b):
                n = g * G + b
                pe.wait_ge(outT_copied, n * C + C)
                if b >= 1:
                    pe.wait_ge(fin_done, n)
                for r in range(R):
                    for c in range(C):
                        m = transpose(bank(6)[:, r * D + c * P:r * D + (c + 1) * P],
                                      oT[:, b % 2, c, r * P:(r + 1) * P])
                m.then_inc(fin_ready, 1)

            def group(g, last):
                attn_xT(g, 0)
                for b in range(G):
                    if b < G - 1:
                        attn_xT(g, b + 1)
                    attn_scores(g, b)
                    if b >= 1:
                        attn_out(g, b - 1)
                attn_out(g, G - 1)

                disp_yT(g, 0)
                disp_logits(g, 0)
                disp_yT(g, 1)
                disp_lT(g, 0)
                for b in range(G):
                    if b < G - 1:
                        disp_logits(g, b + 1)
                    disp_slots(g, b)
                    if b < G - 2:
                        disp_yT(g, b + 2)
                    if b < G - 1:
                        disp_lT(g, b + 1)

                pe.wait_ge(slots_split, (g + 1) * G * C)
                hidden(g, 0, 0)
                hidden(g, 0, 1)
                with pe.Fori(0, E - 1) as e:
                    for j in range(J):
                        if j < J - 2:
                            hidden(g, e, j + 2)
                        else:
                            hidden(g, e + 1, j + 2 - J)
                        expert_out(g, e, j)
                for j in range(J):
                    if j < J - 2:
                        hidden(g, E - 1, j + 2)
                    expert_out(g, E - 1, j)

                comb_cT(g, 0)
                for b in range(G):
                    if b < G - 1:
                        comb_cT(g, b + 1)
                    comb_out(g, b)
                    if b >= 1:
                        comb_fin(g, b - 1)
                comb_fin(g, G - 1)
                for c in range(C):
                    m = transpose(bank(7)[0:G, c * P:(c + 1) * P], ocls[:, c, :])
                m.then_inc(fcls_ready, 1)

            over_groups(pe, group)

        @block.scalar
        def _(act):
            copy = lambda o, i, **k: nc.scalar.activation(o, i, ACT.Copy, **k)

            act.wait_ge(const_loaded, 16 * 9)
            for e in range(E):
                nc.scalar.activation(junk[:, 0:D], sn_n[:, e, :], ACT.Square, accum_out=ssq[:, e:e + 1])\
                  .then_inc(square_link, 1)
                act.wait_ge(square_link, e + 1)
            act.sem_inc(act_setup, 1)
            nc.scalar.activation(snorm[:, :], ssq[:, :], ACT.Sqrt).then_inc(act_setup, 1)
            act.wait_ge(halo_zero, 2)
            nc.scalar.activation(csq[:, 0:1], cve[:, 0:1], ACT.Sqrt).then_inc(act_setup, 1)
            act.wait_ge(pe_setup, 1)
            copy(qk_hi[:, :, :], bank(0).rearrange("p (c n) -> p c n", c=C)).then_inc(act_setup, 1)
            copy(wvT_hi[:, :, :], bank(1).rearrange("p (c n) -> p c n", c=C)).then_inc(act_setup, 1)
            copy(b1T[:, :], bank(2)[:, 0:E * J]).then_inc(act_setup, 1)
            act.wait_ge(pe_setup, 2)
            act.wait_ge(dve_setup, 1)
            for c in range(C):
                copy(snT_hi[:, c, :], bank(4 + 2 * c, 2), scale=gg[:, c:c + 1]).then_inc(act_setup, 1)
            act.wait_ge(pe_setup, 3)
            copy(xc_hi[:, :, :], bank(0)[:, 0:D].rearrange("p (c n) -> p c n", c=C)).then_inc(act_setup, 1)
            act.wait_ge(pe_setup, 4)
            copy(vcls_b[:, :], bank(1)[:, 0:D]).then_inc(act_setup, 1)
            copy(gc_hi[:, :, :], bank(2)[:, 0:D].rearrange("p (c n) -> p c n", c=C)).then_inc(act_setup, 1)
            act.wait_ge(halo_zero, 3)
            nc.scalar.activation(csq[:, 2:4], cve[:, 2:4], ACT.Sqrt).then_inc(act_setup, 1)
            act.wait_ge(pe_setup, 6)
            copy(yc_hi[:, :, :], bank(0)[:, 0:D].rearrange("p (c n) -> p c n", c=C)).then_inc(act_setup, 1)
            act.wait_ge(dve_setup, 8)
            nc.scalar.activation(junk[:, :], bank(4, 2), ACT.Exp, bias=cnegm[:, 0:1],
                                 accum_out=csumc[:, 0:1]).then_inc(act_setup, 1)
            nc.scalar.activation(cexpT[:, :], lclsT[:, :], ACT.Exp, bias=cnegm[:, 0:1])\
              .then_inc(act_setup, 1)
            act.wait_ge(act_setup, 15)
            copy(ccls_hi[:, :, 0], cexpT[:, :]).then_inc(act_setup, 1)
            copy(ycls3[:, :], bank(7)[0:3, 0:D]).then_inc(act_setup, 1)

            def gray_start(i):
                act.wait_ge(x_loaded, 16 * i + 16)
                act.wait_ge(edge_done, i)
                copy(acc0[:, :, :], xrow[:, 0, :].rearrange("p (r w) -> p r w", r=R), scale=GRAY_W[0])\
                    .then_inc(gray_first, 1)

            for i in range(G):
                gray_start(i)

            def attn_front(g, b):
                n, k = g * G + b, b % 2
                act.wait_ge(xT_ready, n + 1)
                if b >= 2:
                    act.wait_ge(scores_ready, n - 1)
                copy(xT_hi[:, k, :, 0:NQ], bank(k).rearrange("p (c n) -> p c n", c=C)).then_inc(xT_rounded, 1)

            def attn_mid(g, b):
                n, k = g * G + b, b % 2
                act.wait_ge(g_ready, n + 1)
                if b >= 1:
                    act.wait_ge(scores_ready, n)
                copy(g_hi[:, :, :], bank(2).rearrange("p (c n) -> p c n", c=C), scale=SCALE)\
                    .then_inc(g_rounded, 1)
                act.wait_ge(v_ready, n + 1)
                if b >= 2:
                    act.wait_ge(attn_ready, n - 1)
                copy(v_hi[:, k, :, :], bank(3).rearrange("p (r n) -> p r n", r=R)).then_inc(v_rounded, 1)

            def attn_exp(g, b):
                n, k = g * G + b, b % 2
                act.wait_ge(negm_ready, n + 1)
                if b >= 2:
                    act.wait_ge(pT_ready, n - 1)
                    act.wait_ge(h_ready, n - 1)
                for r in range(R):
                    m = nc.scalar.activation(prob[:, k, r, :], sm[:, r, :], ACT.Exp, bias=negm[:, r:r + 1],
                                             accum_out=asum[:, k, r:r + 1])
                m.then_inc(prob_ready, 1)

            def attn_pT(g, b):
                n = g * G + b
                act.wait_ge(pT_ready, n + 1)
                if b >= 1:
                    act.wait_ge(attn_ready, n)
                copy(pT_hi[:, :, :], bank(6).rearrange("p (r n) -> p r n", r=R)).then_inc(pT_rounded, 1)

            def disp_y(g, b):
                n, k = g * G + b, b % 2
                act.wait_ge(y_ready, n + 1)
                if b >= 2:
                    act.wait_ge(slots_ready, (n - 1) * C)
                copy(y_hi[:, k, :, :], y[:, k, :, :]).then_inc(y_rounded, 1)
                act.wait_ge(yT_ready, n + 1)
                if b >= 1:
                    act.wait_ge(logits_ready, n * R)
                copy(yT_hi[:, :, :], bank(3).rearrange("p (c n) -> p c n", c=C)).then_inc(yT_rounded, 1)

            def disp_lsb(g, b):
                n = g * G + b
                if b >= 1:
                    act.wait_ge(lT_ready, n)
                    act.wait_ge(cexp_ready, n * R)
                for r in range(R):
                    act.wait_ge(logits_ready, n * R + r + 1)
                    copy(lsb[:, r, :], bank(2 * r, 2)).then_inc(lsb_ready, 1)

            def disp_cexp(g, b):
                n = g * G + b
                for r in range(R):
                    act.wait_ge(cneg_ready, n * R + r + 1)
                    nc.scalar.activation(cexp[:, b, r, :], lsb[:, r, :], ACT.Exp, bias=cneg[:, r:r + 1],
                                         accum_out=csum[:, b * R + r:b * R + r + 1]).then_inc(cexp_ready, 1)

            def disp_dT(g, b):
                n = g * G + b
                act.wait_ge(tneg_ready, n + 1)
                if b >= 1:
                    act.wait_ge(d_ready, n * R)
                for e in range(E):
                    nc.scalar.activation(dT[:, e, :], bank(4 + e // 2)[:, e % 2 * NQ:(e % 2 + 1) * NQ], ACT.Exp,
                                         bias=tneg[:, e:e + 1], accum_out=dsum[:, e:e + 1])
                nc.scalar.activation(ecls[:, :], tdl[:, :], ACT.Exp).then_inc(dT_exp, 1)

            def disp_d(g, b):
                n = g * G + b
                for r in range(R):
                    act.wait_ge(d_ready, n * R + r + 1)
                    if b >= 1:
                        act.wait_ge(slots_ready, n * C)
                    copy(d_hi[:, r, :], bank(2 * r, 2)).then_inc(d_rounded, 1)
                act.wait_ge(d3_ready, n + 1)
                copy(d3[:, :], ps[0:3, 512 * 4:512 * 6]).then_inc(d3_copied, 1)

            def slot_view(t, b, c):
                return t[:, :, c * W + b * P:c * W + (b + 1) * P]

            def disp_slots(g, b):
                n = g * G + b
                for k, c in enumerate((1, 0)):
                    act.wait_ge(slots_ready, n * C + k + 1)
                    copy(slot_view(slot_hi, b, c), bank(4 + 2 * c, 2).rearrange("p (e m) -> p e m", e=E),
                         scale=gam[:, c:c + 1]).then_inc(slots_rounded, 1)

            def gelu(g, e, j):
                t = (g * E + e) * J + j
                k = j % RING
                act.wait_ge(hidden_ready, t + 1)
                act.wait_ge(hT_split, t + 1)
                nc.scalar.activation(act_g[:, j % 2, :], bank(k), ACT.Gelu, bias=b1T[:, bass.ds(e * J + j, 1)])\
                  .then_inc(hbank_free, 1)
                act.wait_ge(hbank_free, t + 1 + RING)
                act.wait_ge(tile_free, t + 1)
                copy(hT_hi[:, k, :], act_g[:, j % 2, :]).then_inc(hT_rounded, 1)

            def expert_hi(g, e):
                act.wait_ge(eo_summed, g * E + e + 2)
                copy(slot_hi[:, e, :], eo_f[:, :]).then_inc(eo_rounded, 1)

            def comb_cT(g, b):
                n = g * G + b
                for k in range(E // 2):
                    act.wait_ge(cT_ready, n * E // 2 + k + 1)
                    if b >= 2:
                        act.wait_ge(outT_ready, (n - 1) * C)
                    copy(cT_hi[:, b % 2, 2 * k:2 * k + 2, 0:NQ],
                         bank(k).rearrange("p (e n) -> p e n", e=2)).then_inc(cT_rounded, 1)

            def comb_oT(g, b):
                n = g * G + b
                for c in range(C):
                    act.wait_ge(outT_ready, n * C + c + 1)
                    if b >= 2:
                        act.wait_ge(fin_ready, n - 1)
                    copy(ocls[:, c, b:b + 1], bank(4 + c)[:, NQ:NQ + 1])
                    copy(oT[:, b % 2, c, :], bank(4 + c)[:, 0:NT]).then_inc(outT_copied, 1)

            def group(g, last):
                act.wait_ge(ve1_ready, g + 1)
                nc.scalar.activation(sd1[:, :], ve1[:, :], ACT.Sqrt).then_inc(sd1_ready, 1)
                attn_front(g, 0)
                for b in range(G):
                    if b < G - 1:
                        attn_front(g, b + 1)
                    attn_mid(g, b)
                    if b >= 1:
                        attn_pT(g, b - 1)
                    attn_exp(g, b)
                attn_pT(g, G - 1)
                act.wait_ge(ve2_ready, g + 1)
                nc.scalar.activation(sq2[:, :, :], ve2[:, :, :], ACT.Sqrt).then_inc(sq2_ready, 1)

                disp_y(g, 0)
                disp_lsb(g, 0)
                disp_y(g, 1)
                disp_cexp(g, 0)
                for b in range(G):
                    disp_dT(g, b)
                    if b < G - 1:
                        disp_lsb(g, b + 1)
                    disp_d(g, b)
                    if b < G - 1:
                        disp_cexp(g, b + 1)
                    disp_slots(g, b)
                    if b < G - 2:
                        disp_y(g, b + 2)

                def expert(e, pair, odd):
                    for j in range(J):
                        gelu(g, e, j)
                        if pair is not None and not odd and j == 0:
                            act.wait_ge(halo_zero, 4 + g)
                            gray_start(g * G + G + pair)
                    expert_hi(g, e)

                if last:
                    with act.Fori(0, E) as e:
                        expert(e, None, False)
                else:
                    with act.Fori(0, E // 2) as pair:
                        expert(pair * 2, pair, False)
                        expert(pair * 2 + 1, pair, True)

                comb_cT(g, 0)
                for b in range(G):
                    if b < G - 1:
                        comb_cT(g, b + 1)
                    comb_oT(g, b)

            over_groups(act, group)

        @block.vector
        def _(dve):
            STT = nc.vector.scalar_tensor_tensor
            f = lambda t: t.bitcast(f32)

            def lo(o, value, hi):
                return nc.vector.tensor_tensor(o, value, f(hi), ALU.subtract)

            class Link:
                def __init__(self, s, base):
                    self.s, self.base, self.n = s, base, 0

                def __call__(self, ins):
                    self.n += 1
                    ins.then_inc(self.s, 1)
                    dve.wait_ge(self.s, self.base + self.n)

            link = Link(disp_link, 0)
            nc.vector.memset(gray[:, :, :], 0.0).then_inc(halo_zero, 1)
            nc.vector.memset(xcls_hi[:, :, :].bitcast(f32), 0.0)
            nc.vector.memset(xcls_lo[:, :, :].bitcast(f32), 0.0)
            nc.vector.memset(ccls_hi[:, :, :].bitcast(f32), 0.0)
            nc.vector.memset(ccls_lo[:, :, :].bitcast(f32), 0.0)
            dve.wait_ge(const_loaded, 16 * 9)
            dve.wait_ge(masks_ready, 1 + 2 * R)
            link(nc.vector.tensor_scalar(taps[:, :], taps[:, :], 0.5, None, ALU.mult))
            link(nc.vector.tensor_tensor(gg[:, :], gam[:, :], sgam[:, :], ALU.mult))
            link(nc.vector.bn_stats(cst[:, 0, :], clsrow[:, :]))
            link(nc.vector.bn_aggr(cmv[:, 0, :], cst[:, 0, :]))
            nc.vector.tensor_scalar(cve[:, 0:1], cmv[:, 0, 1:2], EPS, None, ALU.add).then_inc(halo_zero, 1)
            dve.wait_ge(act_setup, 2)
            link(nc.vector.tensor_scalar(snorm[:, :], snorm[:, :], 1e-12, None, ALU.max))
            link(nc.vector.reciprocal(srin[:, :], snorm[:, :]))
            for e in range(E):
                m = nc.vector.tensor_scalar(sn_n[:, e, :], sn_n[:, e, :], srin[:, e:e + 1], RMS, ALU.mult, ALU.mult)
            m.then_inc(dve_setup, 1)
            dve.wait_ge(act_setup, 3)
            link(nc.vector.reciprocal(csc[:, 0:1], csq[:, 0:1]))
            nc.vector.tensor_scalar(xc[:, :], clsrow[:, :], cmv[:, 0, 0:1], csc[:, 0:1], ALU.subtract, ALU.mult)\
              .then_inc(dve_setup, 1)
            dve.wait_ge(act_setup, 4)
            lo(qk_lo[:, :, :], bank(0).rearrange("p (c n) -> p c n", c=C), qk_hi[:, :, :])
            dve.wait_ge(act_setup, 5)
            lo(wvT_lo[:, :, :], bank(1).rearrange("p (c n) -> p c n", c=C), wvT_hi[:, :, :])
            for c in range(C):
                dve.wait_ge(act_setup, 7 + c)
                m = STT(snT_lo[:, c, :], bank(4 + 2 * c, 2), gg[:, c:c + 1], f(snT_hi[:, c, :]),
                        ALU.mult, ALU.subtract)
            m.then_inc(dve_setup, 1)
            dve.wait_ge(act_setup, 9)
            link(lo(xc_lo[:, :, :], bank(0)[:, 0:D].rearrange("p (c n) -> p c n", c=C), xc_hi[:, :, :]))
            nc.vector.tensor_copy(xcls_hi[:, :, 0:1], xc_hi[:, :, 0:1])
            nc.vector.tensor_copy(xcls_lo[:, :, 0:1], xc_lo[:, :, 0:1]).then_inc(dve_setup, 1)
            dve.wait_ge(act_setup, 11)
            lo(gc_lo[:, :, :], bank(2)[:, 0:D].rearrange("p (c n) -> p c n", c=C), gc_hi[:, :, :])\
                .then_inc(dve_setup, 1)
            dve.wait_ge(pe_setup, 5)
            link(nc.vector.tensor_scalar(cf[:, 0:1], bank(3)[:, 0:1], 0.0, None, ALU.not_equal))
            link(nc.vector.reciprocal(cf[:, 1:2], cf[:, 0:1]))
            link(nc.vector.tensor_tensor(cf[:, 2:3], cf[:, 0:1], cf[:, 1:2], ALU.mult))
            link(STT(hcls_b[:, :], vcls_b[:, :], cf[:, 2:3], clsrow[:, :], ALU.mult, ALU.add))
            link(nc.vector.bn_stats(cst[:, 1, :], hcls_b[:, :]))
            link(nc.vector.bn_aggr(cmv[:, 1, :], cst[:, 1, :]))
            nc.vector.tensor_scalar(cve[:, 2:3], cmv[:, 1, 1:2], EPS, None, ALU.add)
            nc.vector.tensor_scalar(cve[:, 3:4], cmv[:, 1, 1:2], float(D), None, ALU.mult).then_inc(halo_zero, 1)
            dve.wait_ge(act_setup, 12)
            link(nc.vector.reciprocal(csc[:, 2:3], csq[:, 2:3]))
            link(nc.vector.tensor_tensor(csc[:, 3:4], csc[:, 2:3], csq[:, 3:4], ALU.mult))
            link(nc.vector.tensor_scalar(csc[:, 4:5], csc[:, 3:4], 1e-12, None, ALU.max))
            link(nc.vector.reciprocal(csc[:, 5:6], csc[:, 4:5]))
            link(STT(csc[:, 6:7], csc[:, 5:6], RMS, csc[:, 2:3], ALU.mult, ALU.mult))
            nc.vector.tensor_scalar(yc[:, :], hcls_b[:, :], cmv[:, 1, 0:1], csc[:, 6:7], ALU.subtract, ALU.mult)\
              .then_inc(dve_setup, 1)
            dve.wait_ge(act_setup, 13)
            link(lo(yc_lo[:, :, :], bank(0)[:, 0:D].rearrange("p (c n) -> p c n", c=C), yc_hi[:, :, :]))
            for k, t in enumerate((yc_hi, yc_lo, yc_hi)):
                m = nc.vector.tensor_copy(y3[:, :, k:k + 1], f(t[:, :, 0:1]))
            m.then_inc(dve_setup, 1)
            dve.wait_ge(pe_setup, 7)
            nc.vector.tensor_copy(lclsT[:, :], bank(6)[:, 0:2 * E].rearrange("p (e k) -> p e k", k=2)[:, :, 0])
            link(nc.vector.reduce_max(cmax[:, :], bank(4, 2), axis=AX.X))
            nc.vector.tensor_scalar(cnegm[:, :], cmax[:, :], -1.0, None, ALU.mult).then_inc(dve_setup, 1)
            dve.wait_ge(act_setup, 14)
            nc.vector.reciprocal(rcls[:, :], csumc[:, :])
            dve.wait_ge(act_setup, 17)
            lo(ccls_lo[:, :, 0], cexpT[:, :], ccls_hi[:, :, 0]).then_inc(dve_setup, 1)
            dve.wait_ge(dve_setup, 9)
            SETUP_LINKS = link.n

            T_LINKS = 24

            def gray_rest(i, link):
                dve.wait_ge(gray_first, i + 1)
                link(STT(acc0[:, :, :], xrow[:, 1, :].rearrange("p (r w) -> p r w", r=R), GRAY_W[1],
                         acc0[:, :, :], ALU.mult, ALU.add))
                STT(gray[:, 1:R + 1, 1:D + 1], xrow[:, 2, :].rearrange("p (r w) -> p r w", r=R), GRAY_W[2],
                    acc0[:, :, :], ALU.mult, ALU.add).then_inc(gray_done, 1)

            def conv_tap(i, tap, link):
                dy, dx = divmod(tap, 3)
                if tap == 0:
                    dve.wait_ge(halo_loaded, 64 * i + 64)
                    dve.wait_ge(gray_done, i + 1)
                src = gray[:, dy:dy + R, dx:dx + D]
                for k, acc in enumerate((acc0, acc1)):
                    w = taps[:, 9 * k + tap:9 * k + tap + 1]
                    if tap == 0:
                        m = nc.vector.tensor_scalar(acc[:, :, :], src, w, None, ALU.mult)
                    else:
                        m = STT(acc[:, :, :], src, w, acc[:, :, :], ALU.mult, ALU.add)
                link(m)

            def edge_sum(b, link):
                for acc in (acc0, acc1):
                    m = STT(acc[:, :, :], acc[:, :, :], -1.0, acc[:, :, :], ALU.mult, ALU.max)
                link(m)
                link(nc.vector.tensor_tensor(edge[:, b, :, :], acc1[:, :, :], acc0[:, :, :], ALU.add))

            def edge_stats(b, link):
                for r in range(R):
                    link(nc.vector.bn_stats(st1[:, r, :], edge[:, b, r, :]))
                apart(dve)
                for r in range(R):
                    m = nc.vector.bn_aggr(mv1_b[:, r, :], st1[:, r, :])
                link(m)
                nc.vector.tensor_copy(mv1[:, bass.ds(b * R, R), :], mv1_b[:, :, :]).then_inc(edge_done, 1)

            for i in range(G):
                link = Link(token_link, i * T_LINKS)
                gray_rest(i, link)
                for tap in range(9):
                    conv_tap(i, tap, link)
                edge_sum(i, link)
                edge_stats(i, link)
                for _ in range(T_LINKS - link.n):
                    dve.sem_inc(token_link, 1)

            A_LINKS = 80

            def attn_xhat(g, b, link):
                n = g * G + b
                if b >= 2:
                    dve.wait_ge(xT_ready, n - 1)
                for r in range(R):
                    q = b * R + r
                    m = nc.vector.tensor_scalar(xhat[:, b % 2, r, :], edge[:, b, r, :], mv1[:, q, 0:1],
                                                rstd1[:, q:q + 1], ALU.subtract, ALU.mult)
                m.then_inc(xhat_ready, 1)

            def attn_front(g, b):
                n, k = g * G + b, b % 2
                dve.wait_ge(xT_rounded, n + 1)
                lo(xT_lo[:, k, :, 0:NQ], bank(k).rearrange("p (c n) -> p c n", c=C), xT_hi[:, k, :, 0:NQ])\
                    .then_inc(xT_split, 1)

            def attn_mid(g, b, link):
                n, k = g * G + b, b % 2
                dve.wait_ge(g_rounded, n + 1)
                STT(g_lo[:, :, :], bank(2).rearrange("p (c n) -> p c n", c=C), SCALE, f(g_hi[:, :, :]),
                    ALU.mult, ALU.subtract).then_inc(g_split, 1)
                dve.wait_ge(v_rounded, n + 1)
                lo(v_lo[:, k, :, :], bank(3).rearrange("p (r n) -> p r n", r=R), v_hi[:, k, :, :])\
                    .then_inc(v_split, 1)

            def attn_mask(g, b, link):
                n = g * G + b
                dve.wait_ge(scores_ready, n + 1)
                s = bank(4, 2).rearrange("p (r n) -> p r n", r=R)[:, :, 0:NT]
                link(STT(masked[:, :, :], s, 0.0, upper[:, :, :], ALU.is_equal, ALU.max))
                if b >= 1:
                    dve.wait_ge(prob_ready, n)
                STT(sm[:, :, :], masked[:, :, :], -BIG, s, ALU.mult, ALU.add).then_inc(scores_masked, 1)
                dve.wait_ge(scores_masked, n + 1)
                link(nc.vector.reduce_max(mx[:, :], sm[:, :, :], axis=AX.X))
                nc.vector.tensor_scalar(negm[:, :], mx[:, :], -1.0, BIG / 10, ALU.mult, ALU.min)\
                  .then_inc(negm_ready, 1)

            def attn_pT(g, b):
                dve.wait_ge(pT_rounded, g * G + b + 1)
                lo(pT_lo[:, :, :], bank(6).rearrange("p (r n) -> p r n", r=R), pT_hi[:, :, :]).then_inc(pT_split, 1)

            def attn_res(g, b, link):
                n, k = g * G + b, b % 2
                if b == 0:
                    dve.wait_ge(out_stored, 16 * G * g + 1)
                dve.wait_ge(prob_ready, n + 1)
                link(nc.vector.reciprocal(arinv[:, :], asum[:, k, :]))
                dve.wait_ge(attn_ready, n + 1)
                for r in range(R):
                    m = STT(osum[:, r, :], vcls_b[:, :], prob[:, k, r, NQ:NQ + 1], bank(7)[:, r * D:(r + 1) * D],
                            ALU.mult, ALU.add)
                link(m)
                for r in range(R):
                    m = STT(hres[:, b, r, :], osum[:, r, :], arinv[:, r:r + 1], edge[:, b, r, :],
                            ALU.mult, ALU.add)
                m.then_inc(h_ready, 1)
                dve.wait_ge(h_ready, n + 1)
                for r in range(R):
                    m = nc.vector.bn_stats(st2[:, r, :], hres[:, b, r, :])
                link(m)
                apart(dve)
                for r in range(R):
                    m = nc.vector.bn_aggr(mv2[:, b * R + r, :], st2[:, r, :])
                link(m)

            L_LINKS = 80

            def disp_y(g, b, link):
                n, k = g * G + b, b % 2
                if b >= 2:
                    dve.wait_ge(yT_ready, n - 1)
                for r in range(R):
                    q = b * R + r
                    m = nc.vector.tensor_scalar(y[:, k, r, :], hres[:, b, r, :], mv2[:, q, 0:1], s2[:, q:q + 1],
                                                ALU.subtract, ALU.mult)
                m.then_inc(y_ready, 1)

            def disp_split_y(g, b):
                n, k = g * G + b, b % 2
                dve.wait_ge(y_rounded, n + 1)
                lo(y_lo[:, k, :, :], y[:, k, :, :], y_hi[:, k, :, :]).then_inc(y_split, 1)
                dve.wait_ge(yT_rounded, n + 1)
                lo(yT_lo[:, :, :], bank(3).rearrange("p (c n) -> p c n", c=C), yT_hi[:, :, :])\
                    .then_inc(yT_split, 1)

            def disp_max(g, b, link):
                n = g * G + b
                for r in range(R):
                    dve.wait_ge(lsb_ready, n * R + r + 1)
                    if b >= 1:
                        dve.wait_ge(cexp_ready, n * R)
                    link(nc.vector.reduce_max(cmx[:, r:r + 1], lsb[:, r, :], axis=AX.X))
                    nc.vector.tensor_scalar(cneg[:, r:r + 1], cmx[:, r:r + 1], -1.0, None, ALU.mult)\
                      .then_inc(cneg_ready, 1)

            def disp_maxT(g, b, link):
                n = g * G + b
                dve.wait_ge(lT_ready, n + 1)
                link(nc.vector.reduce_max(tmx[:, :], bank(4, 4).rearrange("p (e n) -> p e n", e=E), axis=AX.X))
                link(nc.vector.tensor_tensor(tmc[:, :], tmx[:, :], lclsT[:, :], ALU.max))
                nc.vector.tensor_tensor(tdl[:, :], lclsT[:, :], tmc[:, :], ALU.subtract)
                nc.vector.tensor_scalar(tneg[:, :], tmc[:, :], -1.0, None, ALU.mult).then_inc(tneg_ready, 1)

            def disp_scale(g, b, link):
                n = g * G + b
                dve.wait_ge(dT_exp, n + 1)
                link(nc.vector.tensor_tensor(dtot[:, :], dsum[:, :], ecls[:, :], ALU.add))
                link(nc.vector.reciprocal(drinv[:, :], dtot[:, :]))
                link(nc.vector.tensor_tensor(dcls[:, :], ecls[:, :], drinv[:, :], ALU.mult))
                link(nc.vector.tensor_copy(dclsh[:, :], dcls[:, :]))
                nc.vector.tensor_copy(dc3[:, :, 0], f(dclsh[:, :]))
                nc.vector.tensor_copy(dc3[:, :, 1], f(dclsh[:, :]))
                lo(dc3[:, :, 2], dcls[:, :], dclsh[:, :])
                for e in range(E):
                    m = nc.vector.tensor_scalar(dT[:, e, :], dT[:, e, :], drinv[:, e:e + 1], None, ALU.mult)
                m.then_inc(dT_scaled, 1)

            def disp_d(g, b):
                n = g * G + b
                for r in range(R):
                    dve.wait_ge(d_rounded, n * R + r + 1)
                    lo(d_lo[:, r, :], bank(2 * r, 2), d_hi[:, r, :]).then_inc(d_split, 1)

            def slot_view(t, b, c):
                return t[:, :, c * W + b * P:c * W + (b + 1) * P]

            def disp_slots(g, b):
                n = g * G + b
                for k, c in enumerate((1, 0)):
                    dve.wait_ge(slots_rounded, n * C + k + 1)
                    STT(slot_view(slot_lo, b, c), bank(4 + 2 * c, 2).rearrange("p (e m) -> p e m", e=E),
                        gam[:, c:c + 1], f(slot_view(slot_hi, b, c)), ALU.mult, ALU.subtract)\
                        .then_inc(slots_split, 1)

            def split_hidden(g, e, j):
                t = (g * E + e) * J + j
                dve.wait_ge(hT_rounded, t + 1)
                lo(hT_lo[:, j % RING, :], act_g[:, j % 2, :], hT_hi[:, j % RING, :]).then_inc(hT_split, 1)

            def expert_sum(g, e):
                dve.wait_ge(tile_free, (g * E + e + 1) * J + RING)
                dve.wait_ge(b2_loaded, 16 * (g * E + e) + 16)
                o = bank(4, 2).rearrange("p (b d) -> p b d", b=G)
                nc.vector.tensor_tensor(eo_f[:, :].rearrange("p (b d) -> p b d", b=G), o,
                                        b2_b[:, :].rearrange("p (a d) -> p a d", a=1).to_broadcast([P, G, D]),
                                        ALU.add).then_inc(eo_summed, 1)

            def expert_lo(g, e):
                dve.wait_ge(eo_rounded, g * E + e + 1)
                lo(slot_lo[:, e, :], eo_f[:, :], slot_hi[:, e, :]).then_inc(eo_split, 1)

            def comb_cT(g, b):
                n = g * G + b
                for k in range(E // 2):
                    dve.wait_ge(cT_rounded, n * E // 2 + k + 1)
                    lo(cT_lo[:, b % 2, 2 * k:2 * k + 2, 0:NQ], bank(k).rearrange("p (e n) -> p e n", e=2),
                       cT_hi[:, b % 2, 2 * k:2 * k + 2, 0:NQ]).then_inc(cT_split, 1)

            def comb_fin(g, b):
                n = g * G + b
                dve.wait_ge(fin_ready, n + 1)
                for r in range(R):
                    q = b * R + r
                    m = STT(hres[:, b, r, :], bank(6)[:, r * D:(r + 1) * D], crinv[:, q:q + 1], hres[:, b, r, :],
                            ALU.mult, ALU.add)
                m.then_inc(fin_done, 1)

            def group(g, last):
                link = Link(attn_link, g * A_LINKS)
                dve.wait_ge(edge_done, (g + 1) * G)
                nc.vector.tensor_scalar(ve1[:, :], mv1[:, :, 1], EPS, None, ALU.add).then_inc(ve1_ready, 1)
                for k in range(2):
                    nc.vector.tensor_copy(xT_hi[:, k, :, NQ:NT], xcls_hi[:, :, :])
                    nc.vector.tensor_copy(xT_lo[:, k, :, NQ:NT], xcls_lo[:, :, :])
                dve.wait_ge(sd1_ready, g + 1)
                link(nc.vector.reciprocal(rstd1[:, :], sd1[:, :]))
                attn_xhat(g, 0, link)
                attn_xhat(g, 1, link)
                attn_front(g, 0)
                for b in range(G):
                    if b < G - 1:
                        attn_front(g, b + 1)
                    if b < G - 2:
                        attn_xhat(g, b + 2, link)
                    attn_mid(g, b, link)
                    if b >= 1:
                        attn_pT(g, b - 1)
                    attn_mask(g, b, link)
                    if b >= 1:
                        attn_res(g, b - 1, link)
                attn_pT(g, G - 1)
                attn_res(g, G - 1, link)
                nc.vector.tensor_scalar(ve2[:, 0, :], mv2[:, :, 1], EPS, None, ALU.add)
                nc.vector.tensor_scalar(ve2[:, 1, :], mv2[:, :, 1], float(D), None, ALU.mult).then_inc(ve2_ready, 1)
                dve.wait_ge(sq2_ready, g + 1)
                link(nc.vector.reciprocal(rr2[:, :], sq2[:, 0, :]))
                link(nc.vector.tensor_tensor(nn2[:, :], rr2[:, :], sq2[:, 1, :], ALU.mult))
                link(nc.vector.tensor_scalar(nn2[:, :], nn2[:, :], 1e-12, None, ALU.max))
                link(nc.vector.reciprocal(rn2[:, :], nn2[:, :]))
                link(STT(s2[:, :], rn2[:, :], RMS, rr2[:, :], ALU.mult, ALU.mult))
                for _ in range(A_LINKS - link.n):
                    dve.sem_inc(attn_link, 1)

                link = Link(disp_link, SETUP_LINKS + g * L_LINKS)
                disp_y(g, 0, link)
                disp_y(g, 1, link)
                disp_split_y(g, 0)
                disp_max(g, 0, link)
                disp_split_y(g, 1)
                for b in range(G):
                    disp_maxT(g, b, link)
                    disp_scale(g, b, link)
                    if b < G - 1:
                        disp_max(g, b + 1, link)
                    disp_d(g, b)
                    if b < G - 2:
                        disp_y(g, b + 2, link)
                    disp_slots(g, b)
                    if b < G - 2:
                        disp_split_y(g, b + 2)
                for _ in range(L_LINKS - link.n):
                    dve.sem_inc(disp_link, 1)

                if last:
                    with dve.Fori(0, E) as e:
                        for j in range(J):
                            split_hidden(g, e, j)
                        expert_sum(g, e)
                        expert_lo(g, e)
                else:
                    nc.vector.memset(gray[:, :, :], 0.0).then_inc(halo_zero, 1)
                    dve.wait_ge(halo_zero, 4 + g)
                    apart(dve)
                    with dve.Fori(0, E // 2) as pair:
                        i = g * G + G + pair
                        link = Link(token_link, i * T_LINKS)
                        for odd in range(2):
                            e = pair * 2 + odd
                            for j in range(J):
                                split_hidden(g, e, j)
                                step = odd * J + j
                                if step == 1:
                                    gray_rest(i, link)
                                if 4 <= step < 13:
                                    conv_tap(i, step - 4, link)
                                if step == 13:
                                    edge_sum(pair, link)
                                if step == 14:
                                    edge_stats(pair, link)
                            expert_sum(g, e)
                            expert_lo(g, e)
                        for _ in range(T_LINKS - link.n):
                            dve.sem_inc(token_link, 1)

                for k in range(2):
                    nc.vector.tensor_copy(cT_hi[:, k, :, NQ:NT], ccls_hi[:, :, :])
                    nc.vector.tensor_copy(cT_lo[:, k, :, NQ:NT], ccls_lo[:, :, :])
                nc.vector.reciprocal(crinv[:, :], csum[:, :]).then_inc(crinv_ready, 1)
                dve.wait_ge(crinv_ready, g + 1)
                comb_cT(g, 0)
                for b in range(G):
                    if b < G - 1:
                        comb_cT(g, b + 1)
                    if b >= 1:
                        comb_fin(g, b - 1)
                comb_fin(g, G - 1)
                dve.wait_ge(fcls_ready, g + 1)
                dve.wait_ge(cls_stored, 16 * g + 1)
                STT(fcls[:, :], ps[0:G, 512 * 7:512 * 7 + D], rcls[0:G, :], hcls_b[0:G, :], ALU.mult, ALU.add)\
                    .then_inc(fcls_done, 1)

            over_groups(dve, group)


_INS = ['x', 'cls_tok', 'L0_tok_scharr', 'L0_attn_WQ', 'L0_attn_WK', 'L0_attn_WV', 'L0_ffn_norm_gamma',
        'L0_ffn_slot_norm_gamma', 'L0_ffn_slot_embeds', 'L0_ffn_w1', 'L0_ffn_b1', 'L0_ffn_w2', 'L0_ffn_b2']
_OUTS = [((16, 257, 256), 'float32')]


def kernel(**inputs):
    import numpy as _np
    import concourse.bacc as _bacc
    from concourse import mybir as _mybir
    from concourse.bass_utils import run_bass_kernel_spmd as _run

    nc = _bacc.Bacc("TRN2", target_bir_lowering=False, num_devices=1)
    arrays, args = {}, []
    for name in _INS:
        a = _np.ascontiguousarray(inputs[name])
        arrays[f"in_{name}_dram"] = a
        args.append(nc.dram_tensor(f"in_{name}_dram", a.shape, _mybir.dt.from_np(a.dtype), kind="ExternalInput").ap())
    for i, (shape, dtype) in enumerate(_OUTS):
        dt = _mybir.dt.from_np(_np.dtype(dtype))
        args.append(nc.dram_tensor(f"out_{i}_dram", shape, dt, kind="ExternalOutput").ap())
    vit_tower(nc, *args)
    r = _run(nc, [arrays], core_ids=[0])
    got = tuple(r.results[0][f"out_{i}_dram"] for i in range(len(_OUTS)))
    return got[0]
```

```python
import concourse.bass as bass
from concourse import mybir
from contextlib import ExitStack


def vit_tower(
    nc: bass.Bass,
    x: bass.AP,
    cls_tok: bass.AP,
    scharr: bass.AP,
    wq: bass.AP,
    wk: bass.AP,
    wv: bass.AP,
    norm_gamma: bass.AP,
    slot_norm_gamma: bass.AP,
    slot_embeds: bass.AP,
    w1: bass.AP,
    b1: bass.AP,
    w2: bass.AP,
    b2: bass.AP,
    out: bass.AP,
):
    f32 = mybir.dt.float32
    f32r = mybir.dt.float32r
    ALU = mybir.AluOpType
    ACT = mybir.ActivationFunctionType
    AX = mybir.AxisListType

    P = 128
    B = x.shape[0]
    CH = x.shape[1]
    D = x.shape[3]
    R = x.shape[2] // P
    C = D // P
    NQ = R * P
    NT = NQ + 2
    E, DH = b1.shape
    M = slot_embeds.shape[0] * slot_embeds.shape[1]
    G = 4
    NG = B // G
    J = DH // P
    W = G * P
    RING = 4
    AHEAD = 3
    GRAY_W = (0.2989, 0.587, 0.114)
    EPS = 1e-5
    SCALE = float(D) ** -0.5
    RMS = float(D) ** 0.5
    BIG = 1e30
    XW = D + 2

    ctx = ExitStack()
    with ctx:
        def sem(name):
            return ctx.enter_context(nc.semaphore(name))

        def keep(name, shape, dt=f32):
            return ctx.enter_context(nc.sbuf_tensor(name, shape, dt))

        ident = keep("ident", [P, P])
        upper = keep("upper", [P, R, NT])
        qk_hi = keep("qk_hi", [P, C, D], f32r)
        qk_lo = keep("qk_lo", [P, C, D], f32r)
        wvT_hi = keep("wvT_hi", [P, C, D], f32r)
        wvT_lo = keep("wvT_lo", [P, C, D], f32r)
        snT_hi = keep("snT_hi", [P, C, M], f32r)
        snT_lo = keep("snT_lo", [P, C, M], f32r)
        b1T = keep("b1T", [P, E * J])
        gam = keep("gam", [P, C])
        taps = keep("taps", [P, 18])
        vcls_b = keep("vcls_b", [P, D])
        hcls_b = keep("hcls_b", [P, D])
        xcls_hi = keep("xcls_hi", [P, C, 2], f32r)
        xcls_lo = keep("xcls_lo", [P, C, 2], f32r)
        ycls3 = keep("ycls3", [3, D], f32r)
        lclsT = keep("lclsT", [P, E])
        nlclsT = keep("nlclsT", [P, E])
        ccls_hi = keep("ccls_hi", [P, E, 2], f32r)
        ccls_lo = keep("ccls_lo", [P, E, 2], f32r)
        rcls = keep("rcls", [P, 1])
        slot_hi = keep("slot_hi", [P, E, 2 * W], f32r)
        slot_lo = keep("slot_lo", [P, E, 2 * W], f32r)
        cexp = keep("cexp", [P, G, R, M])
        edge = keep("edge", [P, G, R, D])
        hres = keep("hres", [P, G, R, D])
        w1_in = keep("w1_in", [P, 2, C, 2 * P])
        w2_in = keep("w2_in", [P, 2, 2, D])
        b2_b = keep("b2_b", [P, D])
        mv1 = keep("mv1", [P, G * R, 2])
        mv1_b = keep("mv1_b", [P, R, 2])
        mv2 = keep("mv2", [P, G * R, 2])
        st1 = keep("st1", [P, R, 6])
        st2 = keep("st2", [P, R, 6])
        ve1 = keep("ve1", [P, G * R])
        sd1 = keep("sd1", [P, G * R])
        rstd1 = keep("rstd1", [P, G * R])
        ve2 = keep("ve2", [P, 2, G * R])
        sq2 = keep("sq2", [P, 2, G * R])
        rr2 = keep("rr2", [P, G * R])
        nn2 = keep("nn2", [P, G * R])
        rn2 = keep("rn2", [P, G * R])
        s2 = keep("s2", [P, G * R])
        mx = keep("mx", [P, R])
        negm = keep("negm", [P, R])
        asum = keep("asum", [P, 2, R])
        arinv = keep("arinv", [P, R])
        cmx = keep("cmx", [P, R])
        cneg = keep("cneg", [P, R])
        csum = keep("csum", [P, G * R])
        crinv = keep("crinv", [P, G * R])
        tmx = keep("tmx", [P, E])
        tneg = keep("tneg", [P, E])
        tdl = keep("tdl", [P, E])
        dsum = keep("dsum", [P, E])
        ecls = keep("ecls", [P, E])
        dtot = keep("dtot", [P, E])
        drinv = keep("drinv", [P, E])
        dcls = keep("dcls", [P, E])
        dclsh = keep("dclsh", [P, E], f32r)
        dc3 = keep("dc3", [P, E, 3])
        ocls = keep("ocls", [P, C, G])
        fcls = keep("fcls", [G, D])

        def phase(*specs):
            with ExitStack() as s:
                return [s.enter_context(nc.sbuf_tensor(n, sh, dt)) for n, sh, dt in specs]

        wq_n, wk_n, wv_n, sn_n, b1_n, sgam, gg, clsrow, junk, ssq, snorm, srin, cst, cmv, cve, csq, csc, \
            xc, xc_hi, xc_lo, gc_hi, gc_lo, cf, yc, yc_hi, yc_lo, y3, cmax, cnegm, csumc, cexpT = phase(
                ("wq_n", [P, C, D], f32), ("wk_n", [P, C, D], f32), ("wv_n", [P, C, D], f32),
                ("sn_n", [P, E, D], f32), ("b1_n", [E * J, P], f32), ("sgam", [P, C], f32),
                ("gg", [P, C], f32), ("clsrow", [P, D], f32), ("junk", [P, M], f32),
                ("ssq", [P, E], f32), ("snorm", [P, E], f32), ("srin", [P, E], f32),
                ("cst", [P, 2, 6], f32), ("cmv", [P, 2, 2], f32), ("cve", [P, 4], f32),
                ("csq", [P, 4], f32), ("csc", [P, 8], f32),
                ("xc", [P, D], f32), ("xc_hi", [P, C, P], f32r), ("xc_lo", [P, C, P], f32r),
                ("gc_hi", [P, C, P], f32r), ("gc_lo", [P, C, P], f32r), ("cf", [P, 4], f32),
                ("yc", [P, D], f32), ("yc_hi", [P, C, P], f32r), ("yc_lo", [P, C, P], f32r),
                ("y3", [P, C, 3], f32), ("cmax", [P, 1], f32), ("cnegm", [P, 1], f32),
                ("csumc", [P, 1], f32), ("cexpT", [P, E], f32))
        xhat, xT_hi, xT_lo, g_hi, g_lo, v_hi, v_lo, masked, sm, prob, pT_hi, pT_lo, osum = phase(
            ("xhat", [P, 2, R, D], f32), ("xT_hi", [P, 2, C, NT], f32r), ("xT_lo", [P, 2, C, NT], f32r),
            ("g_hi", [P, C, NQ], f32r), ("g_lo", [P, C, NQ], f32r),
            ("v_hi", [P, 2, R, D], f32r), ("v_lo", [P, 2, R, D], f32r),
            ("masked", [P, R, NT], f32), ("sm", [P, R, NT], f32), ("prob", [P, 2, R, NT], f32),
            ("pT_hi", [P, R, NQ], f32r), ("pT_lo", [P, R, NQ], f32r), ("osum", [P, R, D], f32))
        y, y_hi, y_lo, yT_hi, yT_lo, lsb, dT, d_hi, d_lo, d3 = phase(
            ("y", [P, 2, R, D], f32), ("y_hi", [P, 2, R, D], f32r), ("y_lo", [P, 2, R, D], f32r),
            ("yT_hi", [P, C, NQ], f32r), ("yT_lo", [P, C, NQ], f32r), ("lsb", [P, R, M], f32),
            ("dT", [P, E, NQ], f32), ("d_hi", [P, R, M], f32r), ("d_lo", [P, R, M], f32r),
            ("d3", [3, M], f32r))
        w1_hi, w1_lo, w2_hi, w2_lo, hT_hi, hT_lo, eo_f, xrow, gray = phase(
            ("w1_hi", [P, J // 2, C, 2 * P], f32r), ("w1_lo", [P, J // 2, C, 2 * P], f32r),
            ("w2_hi", [P, 2, 2, D], f32r), ("w2_lo", [P, 2, 2, D], f32r),
            ("hT_hi", [P, RING, W], f32r), ("hT_lo", [P, RING, W], f32r), ("eo_f", [P, 2 * W], f32),
            ("xrow", [P, CH, R * D], f32), ("gray", [P, R + 2, XW], f32))
        cT_hi, cT_lo, oT = phase(
            ("cT_hi", [P, 2, E, NT], f32r), ("cT_lo", [P, 2, E, NT], f32r), ("oT", [P, 2, C, NT], f32))

        ps = ctx.enter_context(nc.psum_tensor("ps", [P, 8 * 512], f32))

        def bank(k, n=1):
            return ps[:, 512 * k:512 * (k + n)]

        acc0, acc1 = (bank(k).rearrange("p (r w) -> p r w", r=R) for k in (6, 7))

        passed = sem("passed")
        const_loaded = sem("const_loaded")
        pool_setup = sem("pool_setup")
        masks_ready = sem("masks_ready")
        pe_setup = sem("pe_setup")
        act_setup = sem("act_setup")
        square_link = sem("square_link")
        dve_setup = sem("dve_setup")
        halo_zero = sem("halo_zero")
        x_loaded = sem("x_loaded")
        gray_first = sem("gray_first")
        conv_done = sem("conv_done")
        abs_done = sem("abs_done")
        gray_done = sem("gray_done")
        halo_loaded = sem("halo_loaded")
        token_link = sem("token_link")
        edge_done = sem("edge_done")
        ve1_ready = sem("ve1_ready")
        sd1_ready = sem("sd1_ready")
        attn_link = sem("attn_link")
        xhat_ready = sem("xhat_ready")
        xT_ready = sem("xT_ready")
        xT_rounded = sem("xT_rounded")
        xT_split = sem("xT_split")
        g_ready = sem("g_ready")
        g_rounded = sem("g_rounded")
        g_split = sem("g_split")
        v_ready = sem("v_ready")
        v_rounded = sem("v_rounded")
        v_split = sem("v_split")
        scores_ready = sem("scores_ready")
        scores_masked = sem("scores_masked")
        negm_ready = sem("negm_ready")
        prob_ready = sem("prob_ready")
        pT_ready = sem("pT_ready")
        pT_rounded = sem("pT_rounded")
        pT_split = sem("pT_split")
        attn_ready = sem("attn_ready")
        h_ready = sem("h_ready")
        ve2_ready = sem("ve2_ready")
        sq2_ready = sem("sq2_ready")
        disp_link = sem("disp_link")
        y_ready = sem("y_ready")
        y_rounded = sem("y_rounded")
        y_split = sem("y_split")
        yT_ready = sem("yT_ready")
        yT_rounded = sem("yT_rounded")
        yT_split = sem("yT_split")
        logits_ready = sem("logits_ready")
        lsb_ready = sem("lsb_ready")
        cneg_ready = sem("cneg_ready")
        cexp_ready = sem("cexp_ready")
        lT_ready = sem("lT_ready")
        tneg_ready = sem("tneg_ready")
        dT_exp = sem("dT_exp")
        dT_scaled = sem("dT_scaled")
        d_ready = sem("d_ready")
        d_rounded = sem("d_rounded")
        d_split = sem("d_split")
        dc3_ready = sem("dc3_ready")
        d3_ready = sem("d3_ready")
        d3_copied = sem("d3_copied")
        slots_ready = sem("slots_ready")
        slots_rounded = sem("slots_rounded")
        slots_split = sem("slots_split")
        w1_loaded = [sem(f"w1_loaded{k}") for k in range(2)]
        w2_loaded = [sem(f"w2_loaded{k}") for k in range(2)]
        b2_loaded = sem("b2_loaded")
        w1_rounded = sem("w1_rounded")
        w2_rounded = sem("w2_rounded")
        w1_split = sem("w1_split")
        w2_split = sem("w2_split")
        tile_free = sem("tile_free")
        gelu_done = sem("gelu_done")
        hidden_ready = sem("hidden_ready")
        hT_rounded = sem("hT_rounded")
        hT_split = sem("hT_split")
        eo_summed = sem("eo_summed")
        eo_rounded = sem("eo_rounded")
        eo_split = sem("eo_split")
        crinv_ready = sem("crinv_ready")
        cT_ready = sem("cT_ready")
        cT_rounded = sem("cT_rounded")
        cT_split = sem("cT_split")
        outT_ready = sem("outT_ready")
        outT_copied = sem("outT_copied")
        fin_ready = sem("fin_ready")
        fin_done = sem("fin_done")
        out_stored = sem("out_stored")
        fcls_ready = sem("fcls_ready")
        fcls_done = sem("fcls_done")
        cls_stored = sem("cls_stored")

        block = ctx.enter_context(nc.Block())

        def apart(eng):
            eng.sem_inc(passed, 1)

        def over_groups(eng, body):
            with eng.Fori(0, NG - 1) as g:
                body(g, False)
            body(NG - 1, True)

        @block.sync
        def _(sp):
            rows = lambda a: a.rearrange("(c p) n -> p c n", p=P)
            sp.dma_start(xrow[:, :, :], x[0].rearrange("c (p r) w -> p c (r w)", p=P)).then_inc(x_loaded, 16)
            sp.dma_start(taps[:, :], scharr.rearrange("k a y x -> a (k y x)").to_broadcast([P, 18]))\
              .then_inc(const_loaded, 16)
            sp.dma_start(clsrow[:, :], cls_tok[0].to_broadcast([P, D])).then_inc(const_loaded, 16)
            sp.dma_start(wq_n[:, :, :], rows(wq)).then_inc(const_loaded, 16)
            sp.dma_start(wk_n[:, :, :], rows(wk)).then_inc(const_loaded, 16)
            sp.dma_start(wv_n[:, :, :], rows(wv)).then_inc(const_loaded, 16)
            sp.dma_start(sn_n[:, :, :], slot_embeds.rearrange("e s d -> s e d")).then_inc(const_loaded, 16)
            sp.dma_start(b1_n[:, :], b1.rearrange("e (j p) -> (e j) p", p=P)).then_inc(const_loaded, 16)
            with nc.allow_non_contiguous_dma(reason="two columns of 128 scales"):
                sp.dma_start(gam[:, :], norm_gamma.rearrange("(c p) -> p c", p=P)).then_inc(const_loaded, 16)
                sp.dma_start(sgam[:, :], slot_norm_gamma.rearrange("(c p) -> p c", p=P))\
                  .then_inc(const_loaded, 16)

            def load_image(i):
                sp.wait_ge(gray_done, i)
                apart(sp)
                sp.dma_start(xrow[:, :, :], x[i].rearrange("c (p r) w -> p c (r w)", p=P))\
                  .then_inc(x_loaded, 16)

            def load_halo(i):
                sp.wait_ge(gray_done, i + 1)
                sp.dma_start(gray[1:113, 0, 1:D + 1], gray[0:112, R, 1:D + 1]).then_inc(halo_loaded, 16)
                sp.dma_start(gray[113:P, 0, 1:D + 1], gray[112:P - 1, R, 1:D + 1]).then_inc(halo_loaded, 16)
                sp.dma_start(gray[0:112, R + 1, 1:D + 1], gray[1:113, 1, 1:D + 1]).then_inc(halo_loaded, 16)
                sp.dma_start(gray[112:P - 1, R + 1, 1:D + 1], gray[113:P, 1, 1:D + 1])\
                  .then_inc(halo_loaded, 16)

            def load_w1(g, e, q, w=None):
                n, k = (g * E + e) * (J // 2) + q, q % 2
                sp.wait_ge(w1_split, n + 1)
                apart(sp)
                sp.dma_start(w1_in[:, k, :, :], w1[e if w is None else w].rearrange("(c p) h -> p c h", p=P)
                             [:, :, 2 * q * P:(2 * q + 2) * P]).then_inc(w1_loaded[k], 16)

            def load_w2(g, e, q):
                n, k = (g * E + e) * (J // 2) + q, q % 2
                sp.wait_ge(w2_split, n + 1)
                apart(sp)
                sp.dma_start(w2_in[:, k, :, :], w2[e].rearrange("(j p) d -> p j d", p=P)
                             [:, 2 * q:2 * q + 2, :]).then_inc(w2_loaded[k], 16)

            def load_b2(g, e):
                sp.wait_ge(eo_summed, g * E + e + 1)
                apart(sp)
                sp.dma_start(b2_b[:, :], b2[e].rearrange("(a d) -> a d", a=1).to_broadcast([P, D]))\
                  .then_inc(b2_loaded, 16)

            load_halo(0)
            for i in range(1, G):
                load_image(i)
                load_halo(i)

            def group(g, last):
                def experts(pair, final):
                    i = g * G + G + pair
                    for odd in range(2):
                        e = pair * 2 + odd
                        for q in range(J // 2):
                            if q < J // 2 - 2:
                                load_w1(g, e, q + 2)
                            elif not (final and odd):
                                load_w1(g, e + 1, q + 2 - J // 2)
                            elif not last:
                                load_w1(g, E, q + 2 - J // 2, 0)
                            load_w2(g, e, q)
                            if not last and not odd and q == 1:
                                sp.wait_ge(slots_split, (g + 1) * G * 2 * C)
                                apart(sp)
                                load_image(i)
                            if not last and odd and q == 0:
                                load_halo(i)
                        load_b2(g, e)

                with sp.Fori(0, E // 2 - 1) as pair:
                    experts(pair, False)
                experts(E // 2 - 1, True)
                for b in range(G):
                    sp.wait_ge(fin_done, g * G + b + 1)
                    sp.dma_start(out[g * G + b, 1:1 + NQ, :].rearrange("(p r) d -> p r d", r=R),
                                 hres[:, b, :, :]).then_inc(out_stored, 16)
                sp.wait_ge(fcls_done, g + 1)
                apart(sp)
                sp.dma_start(out[bass.ds(g * G, G), 0, :], fcls[:, :]).then_inc(cls_stored, 16)

            load_w1(0, 0, 0)
            load_w1(0, 0, 1)
            over_groups(sp, group)
            sp.wait_ge(out_stored, 16 * B + 1)
            sp.wait_ge(cls_stored, 16 * NG + 1)

        @block.gpsimd
        def _(pool):
            pool.sem_inc(tile_free, RING)
            pool.sem_inc(w1_split, 2)
            pool.sem_inc(w2_split, 2)
            for s in (eo_summed, out_stored, cls_stored):
                pool.sem_inc(s, 1)
            nc.gpsimd.memset(ident[:, :], 0.0).then_inc(pool_setup, 1)
            nc.gpsimd.memset(upper[:, :, :], 0.0).then_inc(pool_setup, 1)
            pool.wait_ge(pool_setup, 2)
            nc.gpsimd.affine_select(out=ident[:, :], in_=ident[:, :], compare_op=ALU.not_equal, fill=1.0,
                                    base=0, pattern=[[-1, P]], channel_multiplier=1).then_inc(masks_ready, 1)
            for r in range(R):
                v = upper[:, r, 0:NQ].rearrange("p (a b) -> p a b", a=R)
                nc.gpsimd.affine_select(out=v, in_=v, compare_op=ALU.is_ge, fill=1.0, base=r,
                                        pattern=[[-1, R], [-R, P]], channel_multiplier=R)\
                  .then_inc(masks_ready, 1)
                nc.gpsimd.memset(upper[:, r, NT - 1:NT], 1.0).then_inc(masks_ready, 1)

            def group(g, last):
                def split_w1(e, q):
                    pool.wait_ge(w1_rounded, (g * E + e) * (J // 2) + q + 1)
                    nc.gpsimd.tensor_tensor(w1_lo[:, q, :, :], w1_in[:, q % 2, :, :],
                                            w1_hi[:, q, :, :].bitcast(f32), ALU.subtract).then_inc(w1_split, 1)

                def split_w2(e, q):
                    pool.wait_ge(w2_rounded, (g * E + e) * (J // 2) + q + 1)
                    nc.gpsimd.tensor_tensor(w2_lo[:, q % 2, :, :], w2_in[:, q % 2, :, :],
                                            w2_hi[:, q % 2, :, :].bitcast(f32), ALU.subtract)\
                      .then_inc(w2_split, 1)

                for q in range(3):
                    split_w1(0, q)
                split_w2(0, 0)
                with pool.Fori(0, E - 1) as e:
                    split_w1(e, 3)
                    for q in range(3):
                        split_w2(e, q + 1)
                        split_w1(e + 1, q)
                    split_w2(e + 1, 0)
                split_w1(E - 1, 3)
                for q in range(1, J // 2):
                    split_w2(E - 1, q)

            over_groups(pool, group)

        @block.tensor
        def _(pe):
            def mm3(o, w_hi, w_lo, x_hi, x_lo, first, last, shared=False):
                nc.tensor.matmul(o, w_lo, x_hi, start=first, stop=False, skip_group_check=shared)
                nc.tensor.matmul(o, w_hi, x_lo, start=False, stop=False, skip_group_check=shared)
                return nc.tensor.matmul(o, w_hi, x_hi, start=False, stop=last, skip_group_check=shared)

            def transpose(o, i):
                return nc.tensor.transpose(o, i, ident[0:i.shape[0], 0:i.shape[0]])

            pe.wait_ge(const_loaded, 16 * 9)
            pe.wait_ge(masks_ready, 1)
            for ec in range(C):
                for kc in range(C):
                    m = nc.tensor.matmul(bank(0)[:, ec * D:(ec + 1) * D], wq_n[:, kc, ec * P:(ec + 1) * P],
                                         wk_n[:, kc, :], start=kc == 0, stop=kc == C - 1)
            for vc in range(C):
                for ec in range(C):
                    m = transpose(bank(1)[:, ec * D + vc * P:ec * D + (vc + 1) * P],
                              wv_n[:, vc, ec * P:(ec + 1) * P])
            m.then_inc(pe_setup, 1)
            pe.wait_ge(dve_setup, 1)
            for c in range(C):
                for e in range(E):
                    m = transpose(bank(2 + 2 * c + e // 4)[:, e % 4 * P:(e % 4 + 1) * P],
                                  sn_n[:, e, c * P:(c + 1) * P])
            m.then_inc(pe_setup, 1)
            pe.wait_ge(dve_setup, 2)
            pe.wait_ge(dve_setup, 3)
            transpose(bank(0)[:, D:D + E * J], b1_n[:, :])
            for c in range(C):
                m = transpose(bank(0)[:, c * P:(c + 1) * P], xc[:, c * P:(c + 1) * P])
            m.then_inc(pe_setup, 1)
            pe.wait_ge(dve_setup, 4)
            for c in range(C):
                mm3(bank(1)[:, 0:D], xc_hi[:, c, :], xc_lo[:, c, :], wvT_hi[:, c, :], wvT_lo[:, c, :],
                    c == 0, c == C - 1)
            for c2 in range(C):
                for c in range(C):
                    m = mm3(bank(2)[:, c2 * P:(c2 + 1) * P], qk_hi[:, c, c2 * P:(c2 + 1) * P],
                            qk_lo[:, c, c2 * P:(c2 + 1) * P], xc_hi[:, c, :], xc_lo[:, c, :],
                            c == 0, c == C - 1)
            m.then_inc(pe_setup, 1)
            pe.wait_ge(dve_setup, 5)
            for c in range(C):
                m = mm3(bank(3)[:, 0:P], gc_hi[:, c, :], gc_lo[:, c, :], xc_hi[:, c, :], xc_lo[:, c, :],
                        c == 0, c == C - 1)
            m.then_inc(pe_setup, 1)
            pe.wait_ge(dve_setup, 6)
            for c in range(C):
                m = transpose(bank(0)[:, c * P:(c + 1) * P], yc[:, c * P:(c + 1) * P])
            m.then_inc(pe_setup, 1)
            pe.wait_ge(dve_setup, 7)
            for half in range(2):
                for c in range(C):
                    mm3(bank(4 + half), yc_hi[:, c, :], yc_lo[:, c, :],
                        snT_hi[:, c, half * 512:(half + 1) * 512], snT_lo[:, c, half * 512:(half + 1) * 512],
                        c == 0, c == C - 1)
            for e in range(E):
                for c in range(C):
                    mm3(bank(2)[:, 2 * e:2 * e + 2], snT_hi[:, c, e * P:(e + 1) * P],
                        snT_lo[:, c, e * P:(e + 1) * P], yc_hi[:, c, 0:2], yc_lo[:, c, 0:2],
                        c == 0, c == C - 1)
            for c in range(C):
                m = transpose(bank(3)[0:3, c * P:(c + 1) * P], y3[:, c, :])
            m.then_inc(pe_setup, 1)
            pe.wait_ge(dve_setup, 9)

            def attn_xT(g, b):
                n = g * G + b
                pe.wait_ge(xhat_ready, n + 1)
                if b >= 2:
                    pe.wait_ge(xT_split, n - 1)
                for r in range(R):
                    for c in range(C):
                        m = transpose(bank(b % 2)[:, c * NQ + r * P:c * NQ + (r + 1) * P],
                                      xhat[:, b % 2, r, c * P:(c + 1) * P])
                m.then_inc(xT_ready, 1)

            def attn_scores(g, b):
                n, k = g * G + b, b % 2
                pe.wait_ge(xT_split, n + 1)
                for c2 in range(C):
                    for c in range(C):
                        m = mm3(bank(2)[:, c2 * NQ:(c2 + 1) * NQ], qk_hi[:, c, c2 * P:(c2 + 1) * P],
                                qk_lo[:, c, c2 * P:(c2 + 1) * P], xT_hi[:, k, c, 0:NQ], xT_lo[:, k, c, 0:NQ],
                                c == 0, c == C - 1)
                m.then_inc(g_ready, 1)
                if b >= 1:
                    pe.wait_ge(v_split, n)
                for r in range(R):
                    for c in range(C):
                        m = mm3(bank(3)[:, r * D:(r + 1) * D], xT_hi[:, k, c, r * P:(r + 1) * P],
                                xT_lo[:, k, c, r * P:(r + 1) * P], wvT_hi[:, c, :], wvT_lo[:, c, :],
                                c == 0, c == C - 1)
                m.then_inc(v_ready, 1)
                pe.wait_ge(g_split, n + 1)
                if b >= 1:
                    pe.wait_ge(scores_masked, n)
                for r in range(R):
                    for c in range(C):
                        m = mm3(bank(4 + r)[:, 0:NT], g_hi[:, c, r * P:(r + 1) * P],
                                g_lo[:, c, r * P:(r + 1) * P], xT_hi[:, k, c, :], xT_lo[:, k, c, :],
                                c == 0, c == C - 1)
                m.then_inc(scores_ready, 1)

            def attn_out(g, b):
                n, k = g * G + b, b % 2
                pe.wait_ge(prob_ready, n + 1)
                for r in range(R):
                    for r2 in range(R):
                        m = transpose(bank(6)[:, r2 * NQ + r * P:r2 * NQ + (r + 1) * P],
                                      prob[:, k, r, r2 * P:(r2 + 1) * P])
                m.then_inc(pT_ready, 1)
                pe.wait_ge(pT_split, n + 1)
                pe.wait_ge(v_split, n + 1)
                if b >= 1:
                    pe.wait_ge(h_ready, n)
                for r in range(R):
                    for r2 in range(R):
                        m = mm3(bank(7)[:, r * D:(r + 1) * D], pT_hi[:, r2, r * P:(r + 1) * P],
                                pT_lo[:, r2, r * P:(r + 1) * P], v_hi[:, k, r2, :], v_lo[:, k, r2, :],
                                r2 == 0, r2 == R - 1)
                m.then_inc(attn_ready, 1)

            def disp_yT(g, b):
                n = g * G + b
                pe.wait_ge(y_ready, n + 1)
                if b >= 1:
                    pe.wait_ge(lsb_ready, n * R)
                for r in range(R):
                    for c in range(C):
                        m = transpose(bank(3)[:, c * NQ + r * P:c * NQ + (r + 1) * P],
                                      y[:, b % 2, r, c * P:(c + 1) * P])
                m.then_inc(yT_ready, 1)

            def disp_logits(g, b):
                n = g * G + b
                pe.wait_ge(yT_split, n + 1)
                for r in range(R):
                    for half in range(2):
                        for c in range(C):
                            m = mm3(bank(2 * r + half), yT_hi[:, c, r * P:(r + 1) * P],
                                    yT_lo[:, c, r * P:(r + 1) * P],
                                    snT_hi[:, c, half * 512:(half + 1) * 512],
                                    snT_lo[:, c, half * 512:(half + 1) * 512], c == 0, c == C - 1)
                    m.then_inc(logits_ready, 1)

            def disp_lT(g, b):
                n = g * G + b
                pe.wait_ge(lsb_ready, n * R + R)
                for e in range(E):
                    if b >= 1 and e % 2 == 0:
                        pe.wait_ge(slots_split, (n - 1) * 2 * C + e // 2 + 1)
                    for r in range(R):
                        m = transpose(bank(4 + e // 2)[:, e % 2 * NQ + r * P:e % 2 * NQ + (r + 1) * P],
                                      lsb[:, r, e * P:(e + 1) * P])
                    if e % 2:
                        m.then_inc(lT_ready, 1)

            def disp_slots(g, b):
                n, k = g * G + b, b % 2
                if b < G - 1:
                    pe.wait_ge(lsb_ready, n * R + 2 * R)
                for e in range(E):
                    if e % 2 == 0:
                        pe.wait_ge(dT_scaled, n * E // 2 + e // 2 + 1)
                    for r in range(R):
                        m = transpose(bank(2 * (e // 4) + r)[:, e % 4 * P:(e % 4 + 1) * P],
                                      dT[:, e, r * P:(r + 1) * P])
                    if e % 4 == 3:
                        m.then_inc(d_ready, 1)
                pe.wait_ge(dc3_ready, n + 1)
                for e in range(E):
                    m = transpose(bank(6 + e // 4)[0:3, e % 4 * P:(e % 4 + 1) * P], dc3[:, e, :])
                m.then_inc(d3_ready, 1)
                pe.wait_ge(y_split, n + 1)
                for c in range(C):
                    for half in range(2):
                        h = slice(half * 512, (half + 1) * 512)
                        if c == 0:
                            pe.wait_ge(d_split, n * 2 + half + 1)
                        for r in range(R):
                            mm3(bank(4 + 2 * c + half), y_hi[:, k, r, c * P:(c + 1) * P],
                                y_lo[:, k, r, c * P:(c + 1) * P], d_hi[:, r, h], d_lo[:, r, h], r == 0, False)
                        if c == 0 and half == 0:
                            pe.wait_ge(d3_copied, n + 1)
                        nc.tensor.matmul(bank(4 + 2 * c + half), ycls3[:, c * P:(c + 1) * P], d3[:, h],
                                         start=False, stop=True).then_inc(slots_ready, 1)

            def hidden(g, e, j):
                k, jj = j // 2, slice(j % 2 * P, (j % 2 + 1) * P)
                if j % 2 == 0:
                    pe.wait_ge(w1_split, (g * E + e) * (J // 2) + j // 2 + 3)
                for c in range(C):
                    m = mm3(bank(j % RING), w1_hi[:, k, c, jj], w1_lo[:, k, c, jj],
                            slot_hi[:, e, c * W:(c + 1) * W], slot_lo[:, e, c * W:(c + 1) * W],
                            c == 0, c == C - 1)
                m.then_inc(hidden_ready, 1)

            def expert_out(g, e, j):
                t = (g * E + e) * J + j
                k = j % RING
                if j % 2 == 0:
                    pe.wait_ge(w2_split, (g * E + e) * (J // 2) + j // 2 + 3)
                pe.wait_ge(hT_split, t + 1)
                if j == 0:
                    pe.wait_ge(eo_summed, g * E + e + 1)
                for b in range(G):
                    o = bank(4 + b // 2)[:, b % 2 * D:(b % 2 + 1) * D]
                    m = mm3(o, hT_hi[:, k, b * P:(b + 1) * P], hT_lo[:, k, b * P:(b + 1) * P],
                            w2_hi[:, j // 2 % 2, j % 2, :], w2_lo[:, j // 2 % 2, j % 2, :], j == 0 and b % 2 == 0, j == J - 1, shared=True)
                m.then_inc(tile_free, 1)

            def comb_cT(g, b):
                n = g * G + b
                if b >= 1:
                    pe.wait_ge(cT_split, n * E // 2)
                for e in range(E):
                    for r in range(R):
                        m = transpose(bank(e // 2)[:, e % 2 * NQ + r * P:e % 2 * NQ + (r + 1) * P],
                                      cexp[:, b, r, e * P:(e + 1) * P])
                    if e % 2:
                        m.then_inc(cT_ready, 1)

            def comb_out(g, b):
                n = g * G + b
                if b == 0:
                    pe.wait_ge(crinv_ready, g + 1)
                    pe.wait_ge(eo_split, (g + 1) * E)
                pe.wait_ge(cT_split, (n + 1) * E // 2)
                if b >= 1:
                    pe.wait_ge(outT_copied, n * C)
                for c in range(C):
                    for e in range(E):
                        o = b * D + c * P
                        m = mm3(bank(4 + c)[:, 0:NT], slot_hi[:, e, o:o + P], slot_lo[:, e, o:o + P],
                                cT_hi[:, b % 2, e, :], cT_lo[:, b % 2, e, :], e == 0, e == E - 1)
                    m.then_inc(outT_ready, 1)

            def comb_fin(g, b):
                n = g * G + b
                pe.wait_ge(outT_copied, n * C + C)
                if b >= 1:
                    pe.wait_ge(fin_done, n)
                for r in range(R):
                    for c in range(C):
                        m = transpose(bank(6)[:, r * D + c * P:r * D + (c + 1) * P],
                                      oT[:, b % 2, c, r * P:(r + 1) * P])
                m.then_inc(fin_ready, 1)

            def group(g, last):
                attn_xT(g, 0)
                for b in range(G):
                    if b < G - 1:
                        attn_xT(g, b + 1)
                    attn_scores(g, b)
                    if b >= 1:
                        attn_out(g, b - 1)
                attn_out(g, G - 1)

                disp_yT(g, 0)
                disp_logits(g, 0)
                disp_yT(g, 1)
                disp_lT(g, 0)
                for b in range(G):
                    if b < G - 1:
                        disp_logits(g, b + 1)
                    disp_slots(g, b)
                    if b < G - 2:
                        disp_yT(g, b + 2)
                    if b < G - 1:
                        disp_lT(g, b + 1)

                pe.wait_ge(slots_split, (g + 1) * G * 2 * C)
                for j in range(AHEAD):
                    hidden(g, 0, j)
                with pe.Fori(0, E - 1) as e:
                    for j in range(J):
                        if j < J - AHEAD:
                            hidden(g, e, j + AHEAD)
                        else:
                            hidden(g, e + 1, j + AHEAD - J)
                        expert_out(g, e, j)
                for j in range(J):
                    if j < J - AHEAD:
                        hidden(g, E - 1, j + AHEAD)
                    expert_out(g, E - 1, j)

                comb_cT(g, 0)
                for b in range(G):
                    if b < G - 1:
                        comb_cT(g, b + 1)
                    comb_out(g, b)
                    if b >= 1:
                        comb_fin(g, b - 1)
                comb_fin(g, G - 1)
                for c in range(C):
                    m = transpose(bank(7)[0:G, c * P:(c + 1) * P], ocls[:, c, :])
                m.then_inc(fcls_ready, 1)

            over_groups(pe, group)

        @block.scalar
        def _(act):
            copy = lambda o, i, **k: nc.scalar.activation(o, i, ACT.Copy, **k)

            act.wait_ge(const_loaded, 16 * 9)
            for e in range(E):
                nc.scalar.activation(junk[:, 0:D], sn_n[:, e, :], ACT.Square, accum_out=ssq[:, e:e + 1])\
                  .then_inc(square_link, 1)
                act.wait_ge(square_link, e + 1)
            act.sem_inc(act_setup, 1)
            nc.scalar.activation(snorm[:, :], ssq[:, :], ACT.Sqrt).then_inc(act_setup, 1)
            act.wait_ge(halo_zero, 2)
            nc.scalar.activation(csq[:, 0:1], cve[:, 0:1], ACT.Sqrt).then_inc(act_setup, 1)
            act.wait_ge(pe_setup, 1)
            copy(qk_hi[:, :, :], bank(0).rearrange("p (c n) -> p c n", c=C)).then_inc(act_setup, 1)
            copy(wvT_hi[:, :, :], bank(1).rearrange("p (c n) -> p c n", c=C)).then_inc(act_setup, 1)
            act.wait_ge(pe_setup, 2)
            act.wait_ge(dve_setup, 1)
            for c in range(C):
                copy(snT_hi[:, c, :], bank(2 + 2 * c, 2), scale=gg[:, c:c + 1]).then_inc(act_setup, 1)
            act.wait_ge(pe_setup, 3)
            copy(b1T[:, :], bank(0)[:, D:D + E * J])
            copy(xc_hi[:, :, :], bank(0)[:, 0:D].rearrange("p (c n) -> p c n", c=C)).then_inc(act_setup, 1)
            act.wait_ge(pe_setup, 4)
            copy(vcls_b[:, :], bank(1)[:, 0:D]).then_inc(act_setup, 1)
            copy(gc_hi[:, :, :], bank(2)[:, 0:D].rearrange("p (c n) -> p c n", c=C)).then_inc(act_setup, 1)
            act.wait_ge(halo_zero, 3)
            nc.scalar.activation(csq[:, 2:4], cve[:, 2:4], ACT.Sqrt).then_inc(act_setup, 1)
            act.wait_ge(pe_setup, 6)
            copy(yc_hi[:, :, :], bank(0)[:, 0:D].rearrange("p (c n) -> p c n", c=C)).then_inc(act_setup, 1)
            act.wait_ge(dve_setup, 8)
            nc.scalar.activation(junk[:, :], bank(4, 2), ACT.Exp, bias=cnegm[:, 0:1],
                                 accum_out=csumc[:, 0:1]).then_inc(act_setup, 1)
            nc.scalar.activation(cexpT[:, :], lclsT[:, :], ACT.Exp, bias=cnegm[:, 0:1])\
              .then_inc(act_setup, 1)
            act.wait_ge(act_setup, 14)
            copy(ccls_hi[:, :, 0], cexpT[:, :]).then_inc(act_setup, 1)
            copy(ycls3[:, :], bank(3)[0:3, 0:D]).then_inc(act_setup, 1)

            def gray_start(i):
                act.wait_ge(x_loaded, 16 * i + 16)
                act.wait_ge(edge_done, i)
                copy(acc0[:, :, :], xrow[:, 0, :].rearrange("p (r w) -> p r w", r=R), scale=GRAY_W[0])\
                    .then_inc(gray_first, 1)

            def edge_abs(i, b):
                act.wait_ge(conv_done, i + 1)
                nc.scalar.activation(edge[:, b, :, :], acc0[:, :, :], ACT.Abs)
                nc.scalar.activation(acc1[:, :, :], acc1[:, :, :], ACT.Abs).then_inc(abs_done, 1)

            for i in range(G):
                gray_start(i)
                edge_abs(i, i)

            def attn_front(g, b):
                n, k = g * G + b, b % 2
                act.wait_ge(xT_ready, n + 1)
                if b >= 2:
                    act.wait_ge(scores_ready, n - 1)
                copy(xT_hi[:, k, :, 0:NQ], bank(k).rearrange("p (c n) -> p c n", c=C)).then_inc(xT_rounded, 1)

            def attn_mid(g, b):
                n, k = g * G + b, b % 2
                act.wait_ge(g_ready, n + 1)
                if b >= 1:
                    act.wait_ge(scores_ready, n)
                copy(g_hi[:, :, :], bank(2).rearrange("p (c n) -> p c n", c=C), scale=SCALE)\
                    .then_inc(g_rounded, 1)
                act.wait_ge(v_ready, n + 1)
                if b >= 2:
                    act.wait_ge(attn_ready, n - 1)
                copy(v_hi[:, k, :, :], bank(3).rearrange("p (r n) -> p r n", r=R)).then_inc(v_rounded, 1)

            def attn_exp(g, b):
                n, k = g * G + b, b % 2
                act.wait_ge(negm_ready, n + 1)
                if b >= 2:
                    act.wait_ge(pT_ready, n - 1)
                    act.wait_ge(h_ready, n - 1)
                for r in range(R):
                    m = nc.scalar.activation(prob[:, k, r, :], sm[:, r, :], ACT.Exp, bias=negm[:, r:r + 1],
                                             accum_out=asum[:, k, r:r + 1])
                m.then_inc(prob_ready, 1)

            def attn_pT(g, b):
                n = g * G + b
                act.wait_ge(pT_ready, n + 1)
                if b >= 1:
                    act.wait_ge(attn_ready, n)
                copy(pT_hi[:, :, :], bank(6).rearrange("p (r n) -> p r n", r=R)).then_inc(pT_rounded, 1)

            def disp_y(g, b):
                n, k = g * G + b, b % 2
                act.wait_ge(y_ready, n + 1)
                if b >= 2:
                    act.wait_ge(slots_ready, (n - 1) * 2 * C)
                copy(y_hi[:, k, :, :], y[:, k, :, :]).then_inc(y_rounded, 1)
                act.wait_ge(yT_ready, n + 1)
                if b >= 1:
                    act.wait_ge(logits_ready, n * R)
                copy(yT_hi[:, :, :], bank(3).rearrange("p (c n) -> p c n", c=C)).then_inc(yT_rounded, 1)

            def disp_lsb(g, b):
                n = g * G + b
                if b >= 1:
                    act.wait_ge(lT_ready, n)
                    act.wait_ge(cexp_ready, n * R)
                for r in range(R):
                    act.wait_ge(logits_ready, n * R + r + 1)
                    copy(lsb[:, r, :], bank(2 * r, 2)).then_inc(lsb_ready, 1)

            def disp_cexp(g, b):
                n = g * G + b
                for r in range(R):
                    act.wait_ge(cneg_ready, n * R + r + 1)
                    nc.scalar.activation(cexp[:, b, r, :], lsb[:, r, :], ACT.Exp, bias=cneg[:, r:r + 1],
                                         accum_out=csum[:, b * R + r:b * R + r + 1]).then_inc(cexp_ready, 1)

            def disp_dT(g, b):
                n = g * G + b
                if b >= 1:
                    act.wait_ge(d_ready, n * 2)
                for q in range(E // 2):
                    act.wait_ge(tneg_ready, n * E // 2 + q + 1)
                    for e in (2 * q, 2 * q + 1):
                        nc.scalar.activation(dT[:, e, :], bank(4 + q)[:, e % 2 * NQ:(e % 2 + 1) * NQ], ACT.Exp,
                                             bias=tneg[:, e:e + 1], accum_out=dsum[:, e:e + 1])
                    nc.scalar.activation(ecls[:, 2 * q:2 * q + 2], tdl[:, 2 * q:2 * q + 2], ACT.Exp)\
                      .then_inc(dT_exp, 1)

            def disp_d(g, b):
                n = g * G + b
                if b >= 1:
                    act.wait_ge(slots_ready, n * 2 * C)
                for half in range(2):
                    act.wait_ge(d_ready, n * 2 + half + 1)
                    copy(d_hi[:, :, half * 512:(half + 1) * 512], bank(2 * half, 2).rearrange("p (r n) -> p r n", r=R)).then_inc(d_rounded, 1)
                act.wait_ge(d3_ready, n + 1)
                copy(d3[:, :], ps[0:3, 512 * 6:512 * 8]).then_inc(d3_copied, 1)

            def slot_view(t, b, c, half):
                e = slice(half * E // 2, (half + 1) * E // 2)
                return t[:, e, c * W + b * P:c * W + (b + 1) * P]

            def disp_slots(g, b):
                n = g * G + b
                for c in range(C):
                    for half in range(2):
                        k = 2 * c + half
                        act.wait_ge(slots_ready, n * 2 * C + k + 1)
                        copy(slot_view(slot_hi, b, c, half), bank(4 + k).rearrange("p (e m) -> p e m", m=P),
                             scale=gam[:, c:c + 1]).then_inc(slots_rounded, 1)

            def gelu(g, e, j):
                t = (g * E + e) * J + j
                k = j % RING
                act.wait_ge(hidden_ready, t + 1)
                nc.scalar.activation(bank(k), bank(k), ACT.Gelu, bias=b1T[:, bass.ds(e * J + j, 1)])\
                  .then_inc(gelu_done, 1)
                act.wait_ge(gelu_done, t + 1)
                act.wait_ge(tile_free, t + 1)
                copy(hT_hi[:, k, :], bank(k)).then_inc(hT_rounded, 1)

            def round_w1(g, e, q):
                n, k = (g * E + e) * 2 + q // 2, q % 2
                act.wait_ge(w1_loaded[k], 16 * n + 16)
                copy(w1_hi[:, q, :, :], w1_in[:, k, :, :]).then_inc(w1_rounded, 1)

            def expert_hi(g, e):
                act.wait_ge(eo_summed, g * E + e + 2)
                copy(slot_hi[:, e, :], eo_f[:, :]).then_inc(eo_rounded, 1)

            def comb_cT(g, b):
                n = g * G + b
                for k in range(E // 2):
                    act.wait_ge(cT_ready, n * E // 2 + k + 1)
                    if b >= 2:
                        act.wait_ge(outT_ready, (n - 1) * C)
                    copy(cT_hi[:, b % 2, 2 * k:2 * k + 2, 0:NQ],
                         bank(k).rearrange("p (e n) -> p e n", e=2)).then_inc(cT_rounded, 1)

            def comb_oT(g, b):
                n = g * G + b
                for c in range(C):
                    act.wait_ge(outT_ready, n * C + c + 1)
                    if b >= 2:
                        act.wait_ge(fin_ready, n - 1)
                    copy(ocls[:, c, b:b + 1], bank(4 + c)[:, NQ:NQ + 1])
                    copy(oT[:, b % 2, c, :], bank(4 + c)[:, 0:NT]).then_inc(outT_copied, 1)

            def group(g, last):
                act.wait_ge(ve1_ready, g + 1)
                nc.scalar.activation(sd1[:, :], ve1[:, :], ACT.Sqrt).then_inc(sd1_ready, 1)
                attn_front(g, 0)
                for b in range(G):
                    if b < G - 1:
                        attn_front(g, b + 1)
                    attn_mid(g, b)
                    if b >= 1:
                        attn_pT(g, b - 1)
                    attn_exp(g, b)
                attn_pT(g, G - 1)
                act.wait_ge(ve2_ready, g + 1)
                nc.scalar.activation(sq2[:, :, :], ve2[:, :, :], ACT.Sqrt).then_inc(sq2_ready, 1)

                disp_y(g, 0)
                disp_lsb(g, 0)
                disp_y(g, 1)
                disp_cexp(g, 0)
                for b in range(G):
                    disp_dT(g, b)
                    if b < G - 1:
                        disp_lsb(g, b + 1)
                    disp_d(g, b)
                    if b < G - 1:
                        disp_cexp(g, b + 1)
                    disp_slots(g, b)
                    if b < G - 2:
                        disp_y(g, b + 2)

                act.wait_ge(slots_split, (g + 1) * G * 2 * C)
                for q in range(3):
                    round_w1(g, 0, q)

                def tile(e, j, final):
                    gelu(g, e, j)
                    if j == 1:
                        round_w1(g, e, 3)
                    if j in (3, 5, 7) and not final:
                        round_w1(g, e + 1, j // 2 - 1)

                def experts(pair, final):
                    for odd in range(2):
                        e = pair * 2 + odd
                        for j in range(2, J + 2):
                            if j < J:
                                tile(e, j, final and odd)
                            elif not (final and odd):
                                tile(e + 1, j - J, False)
                            if j == 2 and not odd and not last:
                                act.wait_ge(halo_zero, 4 + g)
                                gray_start(g * G + G + pair)
                            if j == 7 and odd and not last:
                                edge_abs(g * G + G + pair, pair)
                        expert_hi(g, e)

                tile(0, 0, False)
                tile(0, 1, False)
                with act.Fori(0, E // 2 - 1) as pair:
                    experts(pair, False)
                experts(E // 2 - 1, True)

                comb_cT(g, 0)
                for b in range(G):
                    if b < G - 1:
                        comb_cT(g, b + 1)
                    comb_oT(g, b)

            over_groups(act, group)

        @block.vector
        def _(dve):
            STT = nc.vector.scalar_tensor_tensor
            f = lambda t: t.bitcast(f32)

            def lo(o, value, hi):
                return nc.vector.tensor_tensor(o, value, f(hi), ALU.subtract)

            class Link:
                def __init__(self, s, base):
                    self.s, self.base, self.n = s, base, 0

                def __call__(self, ins):
                    self.n += 1
                    ins.then_inc(self.s, 1)
                    dve.wait_ge(self.s, self.base + self.n)

            link = Link(disp_link, 0)
            nc.vector.memset(gray[:, :, :], 0.0).then_inc(halo_zero, 1)
            nc.vector.memset(xcls_hi[:, :, :].bitcast(f32), 0.0)
            nc.vector.memset(xcls_lo[:, :, :].bitcast(f32), 0.0)
            nc.vector.memset(ccls_hi[:, :, :].bitcast(f32), 0.0)
            nc.vector.memset(ccls_lo[:, :, :].bitcast(f32), 0.0)
            dve.wait_ge(const_loaded, 16 * 9)
            dve.wait_ge(masks_ready, 1 + 2 * R)
            link(nc.vector.tensor_scalar(taps[:, :], taps[:, :], 0.5, None, ALU.mult))
            link(nc.vector.tensor_tensor(gg[:, :], gam[:, :], sgam[:, :], ALU.mult))
            link(nc.vector.bn_stats(cst[:, 0, :], clsrow[:, :]))
            link(nc.vector.bn_aggr(cmv[:, 0, :], cst[:, 0, :]))
            nc.vector.tensor_scalar(cve[:, 0:1], cmv[:, 0, 1:2], EPS, None, ALU.add).then_inc(halo_zero, 1)
            dve.wait_ge(act_setup, 2)
            link(nc.vector.tensor_scalar(snorm[:, :], snorm[:, :], 1e-12, None, ALU.max))
            link(nc.vector.reciprocal(srin[:, :], snorm[:, :]))
            for e in range(E):
                m = nc.vector.tensor_scalar(sn_n[:, e, :], sn_n[:, e, :], srin[:, e:e + 1], RMS, ALU.mult, ALU.mult)
            m.then_inc(dve_setup, 1)
            dve.wait_ge(act_setup, 3)
            link(nc.vector.reciprocal(csc[:, 0:1], csq[:, 0:1]))
            nc.vector.tensor_scalar(xc[:, :], clsrow[:, :], cmv[:, 0, 0:1], csc[:, 0:1], ALU.subtract, ALU.mult)\
              .then_inc(dve_setup, 1)
            dve.wait_ge(act_setup, 4)
            lo(qk_lo[:, :, :], bank(0).rearrange("p (c n) -> p c n", c=C), qk_hi[:, :, :])
            dve.wait_ge(act_setup, 5)
            lo(wvT_lo[:, :, :], bank(1).rearrange("p (c n) -> p c n", c=C), wvT_hi[:, :, :])
            for c in range(C):
                dve.wait_ge(act_setup, 6 + c)
                m = STT(snT_lo[:, c, :], bank(2 + 2 * c, 2), gg[:, c:c + 1], f(snT_hi[:, c, :]),
                        ALU.mult, ALU.subtract)
            m.then_inc(dve_setup, 1)
            dve.wait_ge(act_setup, 8)
            link(lo(xc_lo[:, :, :], bank(0)[:, 0:D].rearrange("p (c n) -> p c n", c=C), xc_hi[:, :, :]))
            nc.vector.tensor_copy(xcls_hi[:, :, 0:1], xc_hi[:, :, 0:1])
            nc.vector.tensor_copy(xcls_lo[:, :, 0:1], xc_lo[:, :, 0:1]).then_inc(dve_setup, 1)
            dve.wait_ge(act_setup, 10)
            lo(gc_lo[:, :, :], bank(2)[:, 0:D].rearrange("p (c n) -> p c n", c=C), gc_hi[:, :, :])\
                .then_inc(dve_setup, 1)
            dve.wait_ge(pe_setup, 5)
            link(nc.vector.tensor_scalar(cf[:, 0:1], bank(3)[:, 0:1], 0.0, None, ALU.not_equal))
            link(nc.vector.reciprocal(cf[:, 1:2], cf[:, 0:1]))
            link(nc.vector.tensor_tensor(cf[:, 2:3], cf[:, 0:1], cf[:, 1:2], ALU.mult))
            link(STT(hcls_b[:, :], vcls_b[:, :], cf[:, 2:3], clsrow[:, :], ALU.mult, ALU.add))
            link(nc.vector.bn_stats(cst[:, 1, :], hcls_b[:, :]))
            link(nc.vector.bn_aggr(cmv[:, 1, :], cst[:, 1, :]))
            nc.vector.tensor_scalar(cve[:, 2:3], cmv[:, 1, 1:2], EPS, None, ALU.add)
            nc.vector.tensor_scalar(cve[:, 3:4], cmv[:, 1, 1:2], float(D), None, ALU.mult).then_inc(halo_zero, 1)
            dve.wait_ge(act_setup, 11)
            link(nc.vector.reciprocal(csc[:, 2:3], csq[:, 2:3]))
            link(nc.vector.tensor_tensor(csc[:, 3:4], csc[:, 2:3], csq[:, 3:4], ALU.mult))
            link(nc.vector.tensor_scalar(csc[:, 4:5], csc[:, 3:4], 1e-12, None, ALU.max))
            link(nc.vector.reciprocal(csc[:, 5:6], csc[:, 4:5]))
            link(STT(csc[:, 6:7], csc[:, 5:6], RMS, csc[:, 2:3], ALU.mult, ALU.mult))
            nc.vector.tensor_scalar(yc[:, :], hcls_b[:, :], cmv[:, 1, 0:1], csc[:, 6:7], ALU.subtract, ALU.mult)\
              .then_inc(dve_setup, 1)
            dve.wait_ge(act_setup, 12)
            link(lo(yc_lo[:, :, :], bank(0)[:, 0:D].rearrange("p (c n) -> p c n", c=C), yc_hi[:, :, :]))
            for k, t in enumerate((yc_hi, yc_lo, yc_hi)):
                m = nc.vector.tensor_copy(y3[:, :, k:k + 1], f(t[:, :, 0:1]))
            m.then_inc(dve_setup, 1)
            dve.wait_ge(pe_setup, 7)
            lcls = bank(2)[:, 0:2 * E].rearrange("p (e k) -> p e k", k=2)[:, :, 0]
            nc.vector.tensor_copy(lclsT[:, :], lcls)
            nc.vector.tensor_scalar(nlclsT[:, :], lcls, -1.0, None, ALU.mult)
            link(nc.vector.reduce_max(cmax[:, :], bank(4, 2), axis=AX.X))
            nc.vector.tensor_scalar(cnegm[:, :], cmax[:, :], -1.0, None, ALU.mult).then_inc(dve_setup, 1)
            dve.wait_ge(act_setup, 13)
            nc.vector.reciprocal(rcls[:, :], csumc[:, :])
            dve.wait_ge(act_setup, 16)
            lo(ccls_lo[:, :, 0], cexpT[:, :], ccls_hi[:, :, 0]).then_inc(dve_setup, 1)
            dve.wait_ge(dve_setup, 9)
            SETUP_LINKS = link.n

            T_LINKS = 24

            def gray_rest(i, link):
                dve.wait_ge(gray_first, i + 1)
                link(STT(acc0[:, :, :], xrow[:, 1, :].rearrange("p (r w) -> p r w", r=R), GRAY_W[1],
                         acc0[:, :, :], ALU.mult, ALU.add))
                STT(gray[:, 1:R + 1, 1:D + 1], xrow[:, 2, :].rearrange("p (r w) -> p r w", r=R), GRAY_W[2],
                    acc0[:, :, :], ALU.mult, ALU.add).then_inc(gray_done, 1)

            def conv_tap(i, tap, link):
                dy, dx = divmod(tap, 3)
                if tap == 0:
                    dve.wait_ge(halo_loaded, 64 * i + 64)
                    dve.wait_ge(gray_done, i + 1)
                src = gray[:, dy:dy + R, dx:dx + D]
                for k, acc in enumerate((acc0, acc1)):
                    w = taps[:, 9 * k + tap:9 * k + tap + 1]
                    if tap == 0:
                        m = nc.vector.tensor_scalar(acc[:, :, :], src, w, None, ALU.mult)
                    else:
                        m = STT(acc[:, :, :], src, w, acc[:, :, :], ALU.mult, ALU.add)
                if tap == 8:
                    m.then_inc(conv_done, 1)
                else:
                    link(m)

            def edge_sum(i, b, link):
                dve.wait_ge(abs_done, i + 1)
                e = edge[:, b, :, :]
                link(nc.vector.tensor_tensor(e, acc1[:, :, :], e, ALU.add))

            def edge_stats(b, link):
                for r in range(R):
                    link(nc.vector.bn_stats(st1[:, r, :], edge[:, b, r, :]))
                apart(dve)
                for r in range(R):
                    m = nc.vector.bn_aggr(mv1_b[:, r, :], st1[:, r, :])
                link(m)
                nc.vector.tensor_copy(mv1[:, bass.ds(b * R, R), :], mv1_b[:, :, :]).then_inc(edge_done, 1)

            for i in range(G):
                link = Link(token_link, i * T_LINKS)
                gray_rest(i, link)
                for tap in range(9):
                    conv_tap(i, tap, link)
                edge_sum(i, i, link)
                edge_stats(i, link)
                for _ in range(T_LINKS - link.n):
                    dve.sem_inc(token_link, 1)

            A_LINKS = 80

            def attn_xhat(g, b, link):
                n = g * G + b
                if b >= 2:
                    dve.wait_ge(xT_ready, n - 1)
                for r in range(R):
                    q = b * R + r
                    m = nc.vector.tensor_scalar(xhat[:, b % 2, r, :], edge[:, b, r, :], mv1[:, q, 0:1],
                                                rstd1[:, q:q + 1], ALU.subtract, ALU.mult)
                m.then_inc(xhat_ready, 1)

            def attn_front(g, b):
                n, k = g * G + b, b % 2
                dve.wait_ge(xT_rounded, n + 1)
                lo(xT_lo[:, k, :, 0:NQ], bank(k).rearrange("p (c n) -> p c n", c=C), xT_hi[:, k, :, 0:NQ])\
                    .then_inc(xT_split, 1)

            def attn_mid(g, b, link):
                n, k = g * G + b, b % 2
                dve.wait_ge(g_rounded, n + 1)
                STT(g_lo[:, :, :], bank(2).rearrange("p (c n) -> p c n", c=C), SCALE, f(g_hi[:, :, :]),
                    ALU.mult, ALU.subtract).then_inc(g_split, 1)
                dve.wait_ge(v_rounded, n + 1)
                lo(v_lo[:, k, :, :], bank(3).rearrange("p (r n) -> p r n", r=R), v_hi[:, k, :, :])\
                    .then_inc(v_split, 1)

            def attn_mask(g, b, link):
                n = g * G + b
                dve.wait_ge(scores_ready, n + 1)
                s = bank(4, 2).rearrange("p (r n) -> p r n", r=R)[:, :, 0:NT]
                link(STT(masked[:, :, :], s, 0.0, upper[:, :, :], ALU.is_equal, ALU.max))
                if b >= 1:
                    dve.wait_ge(prob_ready, n)
                STT(sm[:, :, :], masked[:, :, :], -BIG, s, ALU.mult, ALU.add).then_inc(scores_masked, 1)
                dve.wait_ge(scores_masked, n + 1)
                link(nc.vector.reduce_max(mx[:, :], sm[:, :, :], axis=AX.X))
                nc.vector.tensor_scalar(negm[:, :], mx[:, :], -1.0, BIG / 10, ALU.mult, ALU.min)\
                  .then_inc(negm_ready, 1)

            def attn_pT(g, b):
                dve.wait_ge(pT_rounded, g * G + b + 1)
                lo(pT_lo[:, :, :], bank(6).rearrange("p (r n) -> p r n", r=R), pT_hi[:, :, :]).then_inc(pT_split, 1)

            def attn_res(g, b, link):
                n, k = g * G + b, b % 2
                if b == 0:
                    dve.wait_ge(out_stored, 16 * G * g + 1)
                dve.wait_ge(prob_ready, n + 1)
                link(nc.vector.reciprocal(arinv[:, :], asum[:, k, :]))
                dve.wait_ge(attn_ready, n + 1)
                for r in range(R):
                    m = STT(osum[:, r, :], vcls_b[:, :], prob[:, k, r, NQ:NQ + 1], bank(7)[:, r * D:(r + 1) * D],
                            ALU.mult, ALU.add)
                link(m)
                for r in range(R):
                    m = STT(hres[:, b, r, :], osum[:, r, :], arinv[:, r:r + 1], edge[:, b, r, :],
                            ALU.mult, ALU.add)
                m.then_inc(h_ready, 1)
                dve.wait_ge(h_ready, n + 1)
                for r in range(R):
                    m = nc.vector.bn_stats(st2[:, r, :], hres[:, b, r, :])
                link(m)
                apart(dve)
                for r in range(R):
                    m = nc.vector.bn_aggr(mv2[:, b * R + r, :], st2[:, r, :])
                link(m)

            L_LINKS = 80

            def disp_y(g, b, link):
                n, k = g * G + b, b % 2
                if b >= 2:
                    dve.wait_ge(yT_ready, n - 1)
                for r in range(R):
                    q = b * R + r
                    m = nc.vector.tensor_scalar(y[:, k, r, :], hres[:, b, r, :], mv2[:, q, 0:1], s2[:, q:q + 1],
                                                ALU.subtract, ALU.mult)
                m.then_inc(y_ready, 1)

            def disp_split_y(g, b):
                n, k = g * G + b, b % 2
                dve.wait_ge(y_rounded, n + 1)
                lo(y_lo[:, k, :, :], y[:, k, :, :], y_hi[:, k, :, :]).then_inc(y_split, 1)
                dve.wait_ge(yT_rounded, n + 1)
                lo(yT_lo[:, :, :], bank(3).rearrange("p (c n) -> p c n", c=C), yT_hi[:, :, :])\
                    .then_inc(yT_split, 1)

            def disp_max(g, b, link):
                n = g * G + b
                for r in range(R):
                    dve.wait_ge(lsb_ready, n * R + r + 1)
                    if b >= 1:
                        dve.wait_ge(cexp_ready, n * R)
                    link(nc.vector.reduce_max(cmx[:, r:r + 1], lsb[:, r, :], axis=AX.X))
                    nc.vector.tensor_scalar(cneg[:, r:r + 1], cmx[:, r:r + 1], -1.0, None, ALU.mult)\
                      .then_inc(cneg_ready, 1)

            def disp_maxT(g, b, link):
                n = g * G + b
                for q in range(E // 2):
                    e = slice(2 * q, 2 * q + 2)
                    dve.wait_ge(lT_ready, n * E // 2 + q + 1)
                    link(nc.vector.reduce_max(tmx[:, e], bank(4 + q).rearrange("p (e n) -> p e n", e=2),
                                              axis=AX.X))
                    link(STT(tneg[:, e], tmx[:, e], -1.0, nlclsT[:, e], ALU.mult, ALU.min))
                    nc.vector.tensor_tensor(tdl[:, e], lclsT[:, e], tneg[:, e], ALU.add).then_inc(tneg_ready, 1)

            def disp_scale(g, b, link):
                n = g * G + b
                for q in range(E // 2):
                    s = slice(2 * q, 2 * q + 2)
                    dve.wait_ge(dT_exp, n * E // 2 + q + 1)
                    link(nc.vector.tensor_tensor(dtot[:, s], dsum[:, s], ecls[:, s], ALU.add))
                    link(nc.vector.reciprocal(drinv[:, s], dtot[:, s]))
                    for e in (2 * q, 2 * q + 1):
                        m = nc.vector.tensor_scalar(dT[:, e, :], dT[:, e, :], drinv[:, e:e + 1], None, ALU.mult)
                    m.then_inc(dT_scaled, 1)
                link(nc.vector.tensor_tensor(dcls[:, :], ecls[:, :], drinv[:, :], ALU.mult))
                link(nc.vector.tensor_copy(dclsh[:, :], dcls[:, :]))
                nc.vector.tensor_copy(dc3[:, :, 0], f(dclsh[:, :]))
                nc.vector.tensor_copy(dc3[:, :, 1], f(dclsh[:, :]))
                lo(dc3[:, :, 2], dcls[:, :], dclsh[:, :]).then_inc(dc3_ready, 1)

            def disp_d(g, b):
                n = g * G + b
                for half in range(2):
                    dve.wait_ge(d_rounded, n * 2 + half + 1)
                    h = slice(half * 512, (half + 1) * 512)
                    lo(d_lo[:, :, h], bank(2 * half, 2).rearrange("p (r n) -> p r n", r=R),
                       d_hi[:, :, h]).then_inc(d_split, 1)

            def slot_view(t, b, c, half):
                e = slice(half * E // 2, (half + 1) * E // 2)
                return t[:, e, c * W + b * P:c * W + (b + 1) * P]

            def disp_slots(g, b):
                n = g * G + b
                for c in range(C):
                    for half in range(2):
                        k = 2 * c + half
                        dve.wait_ge(slots_rounded, n * 2 * C + k + 1)
                        STT(slot_view(slot_lo, b, c, half), bank(4 + k).rearrange("p (e m) -> p e m", m=P),
                            gam[:, c:c + 1], f(slot_view(slot_hi, b, c, half)), ALU.mult, ALU.subtract)\
                            .then_inc(slots_split, 1)

            def split_hidden(g, e, j):
                dve.wait_ge(hT_rounded, (g * E + e) * J + j + 1)
                lo(hT_lo[:, j % RING, :], bank(j % RING), hT_hi[:, j % RING, :]).then_inc(hT_split, 1)

            def round_w2(g, e, q):
                n, k = (g * E + e) * 2 + q // 2, q % 2
                dve.wait_ge(w2_loaded[k], 16 * n + 16)
                dve.wait_ge(tile_free, (g * E + e) * J + 2 * q - 2 + RING)
                nc.vector.tensor_copy(w2_hi[:, k, :, :], w2_in[:, k, :, :]).then_inc(w2_rounded, 1)

            def expert_sum(g, e):
                dve.wait_ge(tile_free, (g * E + e + 1) * J + RING)
                dve.wait_ge(b2_loaded, 16 * (g * E + e) + 16)
                o = bank(4, 2).rearrange("p (b d) -> p b d", b=G)
                nc.vector.tensor_tensor(eo_f[:, :].rearrange("p (b d) -> p b d", b=G), o,
                                        b2_b[:, :].rearrange("p (a d) -> p a d", a=1).to_broadcast([P, G, D]),
                                        ALU.add).then_inc(eo_summed, 1)

            def expert_lo(g, e):
                dve.wait_ge(eo_rounded, g * E + e + 1)
                lo(slot_lo[:, e, :], eo_f[:, :], slot_hi[:, e, :]).then_inc(eo_split, 1)

            def comb_cT(g, b):
                n = g * G + b
                for k in range(E // 2):
                    dve.wait_ge(cT_rounded, n * E // 2 + k + 1)
                    lo(cT_lo[:, b % 2, 2 * k:2 * k + 2, 0:NQ], bank(k).rearrange("p (e n) -> p e n", e=2),
                       cT_hi[:, b % 2, 2 * k:2 * k + 2, 0:NQ]).then_inc(cT_split, 1)

            def comb_fin(g, b):
                n = g * G + b
                dve.wait_ge(fin_ready, n + 1)
                for r in range(R):
                    q = b * R + r
                    m = STT(hres[:, b, r, :], bank(6)[:, r * D:(r + 1) * D], crinv[:, q:q + 1], hres[:, b, r, :],
                            ALU.mult, ALU.add)
                m.then_inc(fin_done, 1)

            def group(g, last):
                link = Link(attn_link, g * A_LINKS)
                dve.wait_ge(edge_done, (g + 1) * G)
                nc.vector.tensor_scalar(ve1[:, :], mv1[:, :, 1], EPS, None, ALU.add).then_inc(ve1_ready, 1)
                for k in range(2):
                    nc.vector.tensor_copy(xT_hi[:, k, :, NQ:NT], xcls_hi[:, :, :])
                    nc.vector.tensor_copy(xT_lo[:, k, :, NQ:NT], xcls_lo[:, :, :])
                dve.wait_ge(sd1_ready, g + 1)
                link(nc.vector.reciprocal(rstd1[:, :], sd1[:, :]))
                attn_xhat(g, 0, link)
                attn_xhat(g, 1, link)
                attn_front(g, 0)
                for b in range(G):
                    if b < G - 1:
                        attn_front(g, b + 1)
                    if b < G - 2:
                        attn_xhat(g, b + 2, link)
                    attn_mid(g, b, link)
                    if b >= 1:
                        attn_pT(g, b - 1)
                    attn_mask(g, b, link)
                    if b >= 1:
                        attn_res(g, b - 1, link)
                attn_pT(g, G - 1)
                attn_res(g, G - 1, link)
                nc.vector.tensor_scalar(ve2[:, 0, :], mv2[:, :, 1], EPS, None, ALU.add)
                nc.vector.tensor_scalar(ve2[:, 1, :], mv2[:, :, 1], float(D), None, ALU.mult).then_inc(ve2_ready, 1)
                dve.wait_ge(sq2_ready, g + 1)
                link(nc.vector.reciprocal(rr2[:, :], sq2[:, 0, :]))
                link(nc.vector.tensor_tensor(nn2[:, :], rr2[:, :], sq2[:, 1, :], ALU.mult))
                link(nc.vector.tensor_scalar(nn2[:, :], nn2[:, :], 1e-12, None, ALU.max))
                link(nc.vector.reciprocal(rn2[:, :], nn2[:, :]))
                link(STT(s2[:, :], rn2[:, :], RMS, rr2[:, :], ALU.mult, ALU.mult))
                for _ in range(A_LINKS - link.n):
                    dve.sem_inc(attn_link, 1)

                link = Link(disp_link, SETUP_LINKS + g * L_LINKS)
                disp_y(g, 0, link)
                disp_y(g, 1, link)
                disp_split_y(g, 0)
                disp_max(g, 0, link)
                disp_split_y(g, 1)
                for b in range(G):
                    disp_maxT(g, b, link)
                    disp_scale(g, b, link)
                    if b < G - 1:
                        disp_max(g, b + 1, link)
                    disp_d(g, b)
                    if b < G - 2:
                        disp_y(g, b + 2, link)
                    disp_slots(g, b)
                    if b < G - 2:
                        disp_split_y(g, b + 2)
                for _ in range(L_LINKS - link.n):
                    dve.sem_inc(disp_link, 1)

                if not last:
                    nc.vector.memset(gray[:, :, :], 0.0).then_inc(halo_zero, 1)

                def experts(pair, final):
                    i = g * G + G + pair
                    link = Link(token_link, i * T_LINKS)
                    for odd in range(2):
                        e = pair * 2 + odd
                        for j in range(2, J + 2):
                            if j < J:
                                split_hidden(g, e, j)
                            elif not (final and odd):
                                split_hidden(g, e + 1, j - J)
                            if j in (3, 5):
                                round_w2(g, e, j // 2 + 1)
                            if j == 7 and not (final and odd):
                                round_w2(g, e + 1, 0)
                            step = odd * J + j - 2
                            if last:
                                continue
                            if step == 1:
                                gray_rest(i, link)
                            if 4 <= step < 13:
                                conv_tap(i, step - 4, link)
                            if step == 14:
                                edge_sum(i, pair, link)
                            if step == 15:
                                edge_stats(pair, link)
                        expert_sum(g, e)
                        if not (final and odd):
                            round_w2(g, e + 1, 1)
                        expert_lo(g, e)
                    if not last:
                        for _ in range(T_LINKS - link.n):
                            dve.sem_inc(token_link, 1)

                round_w2(g, 0, 0)
                split_hidden(g, 0, 0)
                split_hidden(g, 0, 1)
                round_w2(g, 0, 1)
                with dve.Fori(0, E // 2 - 1) as pair:
                    experts(pair, False)
                experts(E // 2 - 1, True)

                dve.wait_ge(eo_split, (g + 1) * E)
                for k in range(2):
                    nc.vector.tensor_copy(cT_hi[:, k, :, NQ:NT], ccls_hi[:, :, :])
                    nc.vector.tensor_copy(cT_lo[:, k, :, NQ:NT], ccls_lo[:, :, :])
                nc.vector.reciprocal(crinv[:, :], csum[:, :]).then_inc(crinv_ready, 1)
                dve.wait_ge(crinv_ready, g + 1)
                comb_cT(g, 0)
                for b in range(G):
                    if b < G - 1:
                        comb_cT(g, b + 1)
                    if b >= 1:
                        comb_fin(g, b - 1)
                comb_fin(g, G - 1)
                dve.wait_ge(fcls_ready, g + 1)
                dve.wait_ge(cls_stored, 16 * g + 1)
                STT(fcls[:, :], ps[0:G, 512 * 7:512 * 7 + D], rcls[0:G, :], hcls_b[0:G, :], ALU.mult, ALU.add)\
                    .then_inc(fcls_done, 1)

            over_groups(dve, group)


_INS = ['x', 'cls_tok', 'L0_tok_scharr', 'L0_attn_WQ', 'L0_attn_WK', 'L0_attn_WV', 'L0_ffn_norm_gamma',
        'L0_ffn_slot_norm_gamma', 'L0_ffn_slot_embeds', 'L0_ffn_w1', 'L0_ffn_b1', 'L0_ffn_w2', 'L0_ffn_b2']
_OUTS = [((16, 257, 256), 'float32')]


def kernel(**inputs):
    import numpy as _np
    import concourse.bacc as _bacc
    from concourse import mybir as _mybir
    from concourse.bass_utils import run_bass_kernel_spmd as _run

    nc = _bacc.Bacc("TRN2", target_bir_lowering=False, num_devices=1)
    arrays, args = {}, []
    for name in _INS:
        a = _np.ascontiguousarray(inputs[name])
        arrays[f"in_{name}_dram"] = a
        args.append(nc.dram_tensor(f"in_{name}_dram", a.shape, _mybir.dt.from_np(a.dtype), kind="ExternalInput").ap())
    for i, (shape, dtype) in enumerate(_OUTS):
        dt = _mybir.dt.from_np(_np.dtype(dtype))
        args.append(nc.dram_tensor(f"out_{i}_dram", shape, dt, kind="ExternalOutput").ap())
    vit_tower(nc, *args)
    r = _run(nc, [arrays], core_ids=[0])
    got = tuple(r.results[0][f"out_{i}_dram"] for i in range(len(_OUTS)))
    return got[0]
```

```python
import concourse.bass as bass
from concourse import mybir
from contextlib import ExitStack


def vit_tower(
    nc: bass.Bass,
    x: bass.AP,
    cls_tok: bass.AP,
    scharr: bass.AP,
    wq: bass.AP,
    wk: bass.AP,
    wv: bass.AP,
    norm_gamma: bass.AP,
    slot_norm_gamma: bass.AP,
    slot_embeds: bass.AP,
    w1: bass.AP,
    b1: bass.AP,
    w2: bass.AP,
    b2: bass.AP,
    out: bass.AP,
):
    f32 = mybir.dt.float32
    f32r = mybir.dt.float32r
    ALU = mybir.AluOpType
    ACT = mybir.ActivationFunctionType
    AX = mybir.AxisListType

    P = 128
    B = x.shape[0]
    CH = x.shape[1]
    D = x.shape[3]
    R = x.shape[2] // P
    C = D // P
    NQ = R * P
    NT = NQ + 2
    E, DH = b1.shape
    M = slot_embeds.shape[0] * slot_embeds.shape[1]
    G = 4
    NG = B // G
    J = DH // P
    IT = 2 * G
    HE = E // 2
    HM = M // 2
    W = G * P
    RING = 4
    AHEAD = 3
    GRAY_W = (0.2989, 0.587, 0.114)
    EPS = 1e-5
    SCALE = float(D) ** -0.5
    RMS = float(D) ** 0.5
    BIG = 1e30
    XW = D + 2

    ctx = ExitStack()
    with ctx:
        def sem(name):
            return ctx.enter_context(nc.semaphore(name))

        def keep(name, shape, dt=f32):
            return ctx.enter_context(nc.sbuf_tensor(name, shape, dt))

        def phase(*specs):
            with ExitStack() as s:
                return [s.enter_context(nc.sbuf_tensor(n, sh, dt)) for n, sh, dt in specs]

        ident = keep("ident", [P, P])
        upper = keep("upper", [P, R, NT])
        qk_hi = keep("qk_hi", [P, C, D], f32r)
        qk_lo = keep("qk_lo", [P, C, D], f32r)
        wvT_hi = keep("wvT_hi", [P, C, D], f32r)
        wvT_lo = keep("wvT_lo", [P, C, D], f32r)
        snT_hi = keep("snT_hi", [P, C, M], f32r)
        snT_lo = keep("snT_lo", [P, C, M], f32r)
        b1T = keep("b1T", [P, E * J])
        gam = keep("gam", [P, C])
        taps = keep("taps", [P, 18])
        vcls_b = keep("vcls_b", [P, D])
        hcls_b = keep("hcls_b", [P, D])
        xcls_hi = keep("xcls_hi", [P, C, 2], f32r)
        xcls_lo = keep("xcls_lo", [P, C, 2], f32r)
        ycls3 = keep("ycls3", [3, D], f32r)
        lclsT = keep("lclsT", [P, E])
        nlclsT = keep("nlclsT", [P, E])
        ccls_hi = keep("ccls_hi", [P, E, 2], f32r)
        ccls_lo = keep("ccls_lo", [P, E, 2], f32r)
        rcls = keep("rcls", [P, 1])
        slot_hi = keep("slot_hi", [P, E, 2 * W], f32r)
        slot_lo = keep("slot_lo", [P, E, 2 * W], f32r)
        wide_id, wmat, gray_p, first_p, x_p, acc_s = phase(
            ("wide_id", [P, P + 2], f32), ("wmat", [P, 18, P + 2], f32), ("gray_p", [P, 2, R, XW], f32),
            ("first_p", [P, 2, R * D], f32), ("x_p", [P, CH, R * D], f32), ("acc_s", [P, 2, 2, R * D], f32))
        cexp = keep("cexp", [P, G, R, M])
        d_lo, = phase(("d_lo", [P, 2, R, M // 2], f32r))
        edge = keep("edge", [P, G, R, D])
        hres = keep("hres", [P, G, R, D])
        w1_in = keep("w1_in", [P, 2, C, 2 * P])
        w2_in = keep("w2_in", [P, 2, 2, D])
        b2_b = keep("b2_b", [P, D])
        mv1 = keep("mv1", [P, G * R, 2])
        mv1_b = keep("mv1_b", [P, R, 2])
        mv2 = keep("mv2", [P, G * R, 2])
        st1 = keep("st1", [P, R, 6])
        st2 = keep("st2", [P, R, 6])
        ve1 = keep("ve1", [P, G * R])
        sd1 = keep("sd1", [P, G * R])
        rstd1 = keep("rstd1", [P, G * R])
        ve2 = keep("ve2", [P, 2, G * R])
        sq2 = keep("sq2", [P, 2, G * R])
        rr2 = keep("rr2", [P, G * R])
        nn2 = keep("nn2", [P, G * R])
        rn2 = keep("rn2", [P, G * R])
        s2 = keep("s2", [P, G * R])
        mx = keep("mx", [P, R])
        negm = keep("negm", [P, R])
        asum = keep("asum", [P, 2, R])
        arinv = keep("arinv", [P, 2, R])
        pcls = keep("pcls", [P, 2, R])
        cmx = keep("cmx", [P, R])
        cneg = keep("cneg", [P, R])
        csum = keep("csum", [P, G * R])
        crinv = keep("crinv", [P, G * R])
        tmx = keep("tmx", [P, E])
        tneg = keep("tneg", [P, E])
        tdl = keep("tdl", [P, E])
        dsum = keep("dsum", [P, E])
        ecls = keep("ecls", [P, E])
        dtot = keep("dtot", [P, E])
        drinv = keep("drinv", [P, E])
        dcls = keep("dcls", [P, E])
        dclsh = keep("dclsh", [P, E], f32r)
        dc3 = keep("dc3", [P, E, 3])
        ocls = keep("ocls", [P, C, G])
        fcls = keep("fcls", [G, D])

        wq_n, wk_n, wv_n, sn_n, b1_n, sgam, gg, clsrow, junk, ssq, snorm, srin, cst, cmv, cve, csq, csc, \
            xc, xc_hi, xc_lo, gc_hi, gc_lo, cf, yc, yc_hi, yc_lo, y3, cmax, cnegm, csumc, cexpT = phase(
                ("wq_n", [P, C, D], f32), ("wk_n", [P, C, D], f32), ("wv_n", [P, C, D], f32),
                ("sn_n", [P, E, D], f32), ("b1_n", [E * J, P], f32), ("sgam", [P, C], f32),
                ("gg", [P, C], f32), ("clsrow", [P, D], f32), ("junk", [P, M], f32),
                ("ssq", [P, E], f32), ("snorm", [P, E], f32), ("srin", [P, E], f32),
                ("cst", [P, 2, 6], f32), ("cmv", [P, 2, 2], f32), ("cve", [P, 4], f32),
                ("csq", [P, 4], f32), ("csc", [P, 8], f32),
                ("xc", [P, D], f32), ("xc_hi", [P, C, P], f32r), ("xc_lo", [P, C, P], f32r),
                ("gc_hi", [P, C, P], f32r), ("gc_lo", [P, C, P], f32r), ("cf", [P, 4], f32),
                ("yc", [P, D], f32), ("yc_hi", [P, C, P], f32r), ("yc_lo", [P, C, P], f32r),
                ("y3", [P, C, 3], f32), ("cmax", [P, 1], f32), ("cnegm", [P, 1], f32),
                ("csumc", [P, 1], f32), ("cexpT", [P, E], f32))
        xhat, xT_hi, xT_lo, g_hi, g_lo, v_hi, v_lo, masked, sm, prob, pT_hi, pT_lo, base = phase(
            ("xhat", [P, 2, R, D], f32), ("xT_hi", [P, 2, C, NT], f32r), ("xT_lo", [P, 2, C, NT], f32r),
            ("g_hi", [P, C, NQ], f32r), ("g_lo", [P, C, NQ], f32r),
            ("v_hi", [P, 2, R, D], f32r), ("v_lo", [P, 2, R, D], f32r),
            ("masked", [P, R, NT], f32), ("sm", [P, R, NT], f32), ("prob", [P, 2, R, NT], f32),
            ("pT_hi", [P, R, NQ], f32r), ("pT_lo", [P, R, NQ], f32r), ("base", [P, R, D], f32))
        y, yT_hi, yT_lo, lsb, dT, y_hi, y_lo, d_hi, d3 = phase(
            ("y", [P, 2, R, D], f32), ("yT_hi", [P, C, NQ], f32r), ("yT_lo", [P, C, NQ], f32r),
            ("lsb", [P, 2, R, M], f32), ("dT", [P, E, NQ], f32),
            ("y_hi", [P, 2, R, D], f32r), ("y_lo", [P, 2, R, D], f32r),
            ("d_hi", [P, 2, R, M // 2], f32r), ("d3", [3, M // 2], f32r))
        w1_lo, w1_hi, hT_hi, hT_lo, w2_hi, w2_lo, eo_f, xrow, gray = phase(
            ("w1_lo", [P, J // 2, C, 2 * P], f32r), ("w1_hi", [P, J // 2, C, 2 * P], f32r),
            ("hT_hi", [P, RING, W], f32r), ("hT_lo", [P, RING, W], f32r),
            ("w2_hi", [P, 2, 2, D], f32r), ("w2_lo", [P, 2, 2, D], f32r), ("eo_f", [P, 2 * W], f32),
            ("xrow", [P, CH, R * D], f32), ("gray", [P, R + 2, XW], f32))
        _, cT_hi0, cT_hi1, cT_lo1, oT, _, cT_lo0 = phase(
            ("next_x", [P, 2, R * D + 2 * C * NT], f32),
            ("cT_hi0", [P, E, NT], f32r), ("cT_hi1", [P, E, NT], f32r), ("cT_lo1", [P, E, NT], f32r),
            ("oT", [P, 2, C, NT], f32), ("gap", [P, 952], f32), ("cT_lo0", [P, E, NT], f32r))
        cT_hi, cT_lo = (cT_hi0, cT_hi1), (cT_lo0, cT_lo1)

        ps = ctx.enter_context(nc.psum_tensor("ps", [P, 8 * 512], f32))

        def bank(k, n=1):
            return ps[:, 512 * k:512 * (k + n)]

        acc_bank = [bank(k).rearrange("p (r w) -> p r w", r=R) for k in (6, 7)]
        acc_sbuf = [[acc_s[:, j, k, :].rearrange("p (r w) -> p r w", r=R) for k in range(2)] for j in range(2)]

        passed = sem("passed")
        const_loaded = sem("const_loaded")
        pool_setup = sem("pool_setup")
        masks_ready = sem("masks_ready")
        pe_setup = sem("pe_setup")
        act_setup = sem("act_setup")
        square_link = sem("square_link")
        dve_setup = sem("dve_setup")
        halo_zero = sem("halo_zero")
        pe_gray_zero = sem("pe_gray_zero")
        pe_x_loaded = sem("pe_x_loaded")
        pe_gray_first = sem("pe_gray_first")
        pe_gray_done = sem("pe_gray_done")
        wmat_ready = sem("wmat_ready")
        pe_conv_done = sem("pe_conv_done")
        pe_abs_done = sem("pe_abs_done")
        pe_edge_summed = sem("pe_edge_summed")
        x_loaded = sem("x_loaded")
        gray_first = sem("gray_first")
        conv_done = sem("conv_done")
        abs_done = sem("abs_done")
        gray_done = sem("gray_done")
        halo_loaded = sem("halo_loaded")
        token_link = sem("token_link")
        edge_done = sem("edge_done")
        ve1_ready = sem("ve1_ready")
        sd1_ready = sem("sd1_ready")
        attn_link = sem("attn_link")
        rstd1_ready = sem("rstd1_ready")
        xhat_ready = sem("xhat_ready")
        xT_ready = sem("xT_ready")
        xT_rounded = sem("xT_rounded")
        xT_split = sem("xT_split")
        g_ready = sem("g_ready")
        g_rounded = sem("g_rounded")
        g_split = sem("g_split")
        v_ready = sem("v_ready")
        v_rounded = sem("v_rounded")
        v_split = sem("v_split")
        scores_ready = sem("scores_ready")
        scores_masked = sem("scores_masked")
        negm_ready = sem("negm_ready")
        prob_ready = sem("prob_ready")
        arinv_ready = sem("arinv_ready")
        clsv_ready = sem("clsv_ready")
        base_ready = sem("base_ready")
        pT_ready = sem("pT_ready")
        pT_rounded = sem("pT_rounded")
        pT_split = sem("pT_split")
        attn_ready = sem("attn_ready")
        h_ready = sem("h_ready")
        ve2_ready = sem("ve2_ready")
        sq2_ready = sem("sq2_ready")
        disp_link = sem("disp_link")
        y_ready = sem("y_ready")
        y_rounded = sem("y_rounded")
        y_split = sem("y_split")
        yT_ready = sem("yT_ready")
        yT_rounded = sem("yT_rounded")
        yT_split = sem("yT_split")
        logits_ready = sem("logits_ready")
        lsb_ready = sem("lsb_ready")
        cneg_ready = sem("cneg_ready")
        cexp_ready = sem("cexp_ready")
        lT_ready = sem("lT_ready")
        tneg_ready = sem("tneg_ready")
        dT_exp = sem("dT_exp")
        dT_scaled = sem("dT_scaled")
        d_ready = sem("d_ready")
        d_rounded = sem("d_rounded")
        d_split = sem("d_split")
        dc3_ready = sem("dc3_ready")
        d3_ready = sem("d3_ready")
        d3_copied = sem("d3_copied")
        slots_ready = sem("slots_ready")
        slots_rounded = sem("slots_rounded")
        slots_split = sem("slots_split")
        w1_loaded = [sem(f"w1_loaded{k}") for k in range(2)]
        w2_loaded = [sem(f"w2_loaded{k}") for k in range(2)]
        b2_loaded = sem("b2_loaded")
        w1_rounded = sem("w1_rounded")
        w2_rounded = sem("w2_rounded")
        w1_split = sem("w1_split")
        w2_split = sem("w2_split")
        tile_free = sem("tile_free")
        gelu_done = sem("gelu_done")
        hidden_ready = sem("hidden_ready")
        hT_rounded = sem("hT_rounded")
        hT_split = sem("hT_split")
        eo_summed = sem("eo_summed")
        eo_rounded = sem("eo_rounded")
        eo_split = sem("eo_split")
        crinv_ready = sem("crinv_ready")
        ccls_copied = sem("ccls_copied")
        cT_ready = sem("cT_ready")
        cT_rounded = sem("cT_rounded")
        cT_split = sem("cT_split")
        outT_ready = sem("outT_ready")
        outT_copied = sem("outT_copied")
        fin_ready = sem("fin_ready")
        fin_done = sem("fin_done")
        out_stored = sem("out_stored")
        fcls_ready = sem("fcls_ready")
        fcls_done = sem("fcls_done")
        cls_stored = sem("cls_stored")

        block = ctx.enter_context(nc.Block())

        def apart(eng):
            eng.sem_inc(passed, 1)

        def over_groups(eng, body):
            with eng.Fori(0, NG - 1) as g:
                body(g, False)
            body(NG - 1, True)

        @block.sync
        def _(sp):
            rows = lambda a: a.rearrange("(c p) n -> p c n", p=P)
            pixels = lambda i: x[i].rearrange("c (p r) w -> p c (r w)", p=P)
            sp.dma_start(x_p[:, :, :], pixels(0)).then_inc(pe_x_loaded, 16)
            sp.dma_start(taps[:, :], scharr.rearrange("k a y x -> a (k y x)").to_broadcast([P, 18]))\
              .then_inc(const_loaded, 16)
            sp.dma_start(xrow[:, :, :], pixels(1)).then_inc(x_loaded, 16)
            sp.dma_start(clsrow[:, :], cls_tok[0].to_broadcast([P, D])).then_inc(const_loaded, 16)
            sp.dma_start(wq_n[:, :, :], rows(wq)).then_inc(const_loaded, 16)
            sp.dma_start(wk_n[:, :, :], rows(wk)).then_inc(const_loaded, 16)
            sp.dma_start(wv_n[:, :, :], rows(wv)).then_inc(const_loaded, 16)
            sp.dma_start(sn_n[:, :, :], slot_embeds.rearrange("e s d -> s e d")).then_inc(const_loaded, 16)
            sp.dma_start(b1_n[:, :], b1.rearrange("e (j p) -> (e j) p", p=P)).then_inc(const_loaded, 16)
            with nc.allow_non_contiguous_dma(reason="two columns of 128 scales"):
                sp.dma_start(gam[:, :], norm_gamma.rearrange("(c p) -> p c", p=P)).then_inc(const_loaded, 16)
                sp.dma_start(sgam[:, :], slot_norm_gamma.rearrange("(c p) -> p c", p=P))\
                  .then_inc(const_loaded, 16)

            def load_image(t, i):
                sp.wait_ge(gray_done, t)
                apart(sp)
                sp.dma_start(xrow[:, :, :], pixels(i)).then_inc(x_loaded, 16)

            def load_halo(t):
                sp.wait_ge(gray_done, t + 1)
                sp.dma_start(gray[1:113, 0, 1:D + 1], gray[0:112, R, 1:D + 1]).then_inc(halo_loaded, 16)
                sp.dma_start(gray[113:P, 0, 1:D + 1], gray[112:P - 1, R, 1:D + 1]).then_inc(halo_loaded, 16)
                sp.dma_start(gray[0:112, R + 1, 1:D + 1], gray[1:113, 1, 1:D + 1]).then_inc(halo_loaded, 16)
                sp.dma_start(gray[112:P - 1, R + 1, 1:D + 1], gray[113:P, 1, 1:D + 1])\
                  .then_inc(halo_loaded, 16)

            def load_w1(g, e, q, w=None):
                n, k = (g * E + e) * (J // 2) + q, q % 2
                sp.wait_ge(w1_split, n + 1)
                apart(sp)
                sp.dma_start(w1_in[:, k, :, :], w1[e if w is None else w].rearrange("(c p) h -> p c h", p=P)
                             [:, :, 2 * q * P:(2 * q + 2) * P]).then_inc(w1_loaded[k], 16)

            def load_w2(g, e, q):
                n, k = (g * E + e) * (J // 2) + q, q % 2
                sp.wait_ge(w2_split, n + 1)
                apart(sp)
                sp.dma_start(w2_in[:, k, :, :], w2[e].rearrange("(j p) d -> p j d", p=P)
                             [:, 2 * q:2 * q + 2, :]).then_inc(w2_loaded[k], 16)

            def load_b2(g, e):
                sp.wait_ge(eo_summed, g * E + e + 1)
                apart(sp)
                sp.dma_start(b2_b[:, :], b2[e].rearrange("(a d) -> a d", a=1).to_broadcast([P, D]))\
                  .then_inc(b2_loaded, 16)

            sp.wait_ge(pe_gray_done, 1)
            sp.dma_start(x_p[:, :, :], pixels(2)).then_inc(pe_x_loaded, 16)
            load_halo(0)
            load_image(1, 3)
            load_halo(1)

            def group(g, last):
                def experts(pair, final):
                    t = g * G + 2 + pair
                    for odd in range(2):
                        e = pair * 2 + odd
                        for q in range(J // 2):
                            if q < J // 2 - 2:
                                load_w1(g, e, q + 2)
                            elif not (final and odd):
                                load_w1(g, e + 1, q + 2 - J // 2)
                            elif not last:
                                load_w1(g, E, q + 2 - J // 2, 0)
                            load_w2(g, e, q)
                            if not last and not odd and q == 1:
                                sp.wait_ge(slots_split, (g + 1) * IT * C)
                                apart(sp)
                                load_image(t, t + G - 2)
                            if not last and odd and q == 0:
                                load_halo(t)
                        load_b2(g, e)

                with sp.Fori(0, E // 2 - 1) as pair:
                    experts(pair, False)
                experts(E // 2 - 1, True)
                for b in range(G):
                    sp.wait_ge(fin_done, g * G + b + 1)
                    sp.dma_start(out[g * G + b, 1:1 + NQ, :].rearrange("(p r) d -> p r d", r=R),
                                 hres[:, b, :, :]).then_inc(out_stored, 16)
                sp.wait_ge(fcls_done, g + 1)
                apart(sp)
                sp.dma_start(out[bass.ds(g * G, G), 0, :], fcls[:, :]).then_inc(cls_stored, 16)

            load_w1(0, 0, 0)
            load_w1(0, 0, 1)
            over_groups(sp, group)
            sp.wait_ge(out_stored, 16 * B + 1)
            sp.wait_ge(cls_stored, 16 * NG + 1)

        @block.gpsimd
        def _(pool):
            pool.sem_inc(tile_free, RING)
            pool.sem_inc(w1_split, 2)
            pool.sem_inc(w2_split, 2)
            for s in (eo_summed, out_stored, cls_stored):
                pool.sem_inc(s, 1)
            nc.gpsimd.memset(ident[:, :], 0.0).then_inc(pool_setup, 1)
            nc.gpsimd.memset(upper[:, :, :], 0.0).then_inc(pool_setup, 1)
            pool.wait_ge(pool_setup, 2)
            nc.gpsimd.affine_select(out=ident[:, :], in_=ident[:, :], compare_op=ALU.not_equal, fill=1.0,
                                    base=0, pattern=[[-1, P]], channel_multiplier=1).then_inc(masks_ready, 1)
            for r in range(R):
                v = upper[:, r, 0:NQ].rearrange("p (a b) -> p a b", a=R)
                nc.gpsimd.affine_select(out=v, in_=v, compare_op=ALU.is_ge, fill=1.0, base=r,
                                        pattern=[[-1, R], [-R, P]], channel_multiplier=R)\
                  .then_inc(masks_ready, 1)
                nc.gpsimd.memset(upper[:, r, NT - 1:NT], 1.0).then_inc(masks_ready, 1)

            def group(g, last):
                def split_w1(e, q):
                    pool.wait_ge(w1_rounded, (g * E + e) * (J // 2) + q + 1)
                    nc.gpsimd.tensor_tensor(w1_lo[:, q, :, :], w1_in[:, q % 2, :, :],
                                            w1_hi[:, q, :, :].bitcast(f32), ALU.subtract).then_inc(w1_split, 1)

                def split_w2(e, q):
                    pool.wait_ge(w2_rounded, (g * E + e) * (J // 2) + q + 1)
                    nc.gpsimd.tensor_tensor(w2_lo[:, q % 2, :, :], w2_in[:, q % 2, :, :],
                                            w2_hi[:, q % 2, :, :].bitcast(f32), ALU.subtract)\
                      .then_inc(w2_split, 1)

                for b in range(G):
                    n = g * G + b
                    pool.wait_ge(clsv_ready, n + 1)
                    apart(pool)
                    nc.gpsimd.tensor_tensor(base[:, :, :], base[:, :, :], edge[:, b, :, :], ALU.add)\
                      .then_inc(base_ready, 1)

                for q in range(3):
                    split_w1(0, q)
                split_w2(0, 0)
                with pool.Fori(0, E - 1) as e:
                    split_w1(e, 3)
                    for q in range(3):
                        split_w2(e, q + 1)
                        split_w1(e + 1, q)
                    split_w2(e + 1, 0)
                split_w1(E - 1, 3)
                for q in range(1, J // 2):
                    split_w2(E - 1, q)

            over_groups(pool, group)

        @block.tensor
        def _(pe):
            def mm3(o, w_hi, w_lo, x_hi, x_lo, first, last, shared=False):
                nc.tensor.matmul(o, w_lo, x_hi, start=first, stop=False, skip_group_check=shared)
                nc.tensor.matmul(o, w_hi, x_lo, start=False, stop=False, skip_group_check=shared)
                return nc.tensor.matmul(o, w_hi, x_hi, start=False, stop=last, skip_group_check=shared)

            def transpose(o, i):
                return nc.tensor.transpose(o, i, ident[0:i.shape[0], 0:i.shape[0]])

            def conv(s, k, r):
                if k == 0 and r == 0:
                    pe.wait_ge(pe_gray_done, s + 1)
                    if s == 0:
                        pe.wait_ge(wmat_ready, 2)
                    else:
                        pe.wait_ge(pe_edge_summed, s)
                for dy in range(3):
                    shift, row = divmod(r + dy - 1, R)
                    for dx in range(3):
                        m = nc.tensor.matmul(acc_bank[k][:, r, :],
                                             wmat[:, 9 * k + 3 * dy + dx, 1 + shift:1 + shift + P],
                                             gray_p[:, s, row, dx:dx + D],
                                             start=dy == dx == 0, stop=dy == dx == 2)
                if k == 1 and r == R - 1:
                    m.then_inc(pe_conv_done, 1)

            pe.wait_ge(const_loaded, 16 * 9)
            pe.wait_ge(masks_ready, 1)
            for ec in range(C):
                for kc in range(C):
                    m = nc.tensor.matmul(bank(0)[:, ec * D:(ec + 1) * D], wq_n[:, kc, ec * P:(ec + 1) * P],
                                         wk_n[:, kc, :], start=kc == 0, stop=kc == C - 1)
            for vc in range(C):
                for ec in range(C):
                    m = transpose(bank(1)[:, ec * D + vc * P:ec * D + (vc + 1) * P],
                              wv_n[:, vc, ec * P:(ec + 1) * P])
            m.then_inc(pe_setup, 1)
            conv(0, 0, 0)
            pe.wait_ge(dve_setup, 1)
            for c in range(C):
                for e in range(E):
                    m = transpose(bank(2 + 2 * c + e // 4)[:, e % 4 * P:(e % 4 + 1) * P],
                                  sn_n[:, e, c * P:(c + 1) * P])
            m.then_inc(pe_setup, 1)
            conv(0, 0, 1)
            pe.wait_ge(dve_setup, 2)
            pe.wait_ge(dve_setup, 3)
            transpose(bank(0)[:, D:D + E * J], b1_n[:, :])
            for c in range(C):
                m = transpose(bank(0)[:, c * P:(c + 1) * P], xc[:, c * P:(c + 1) * P])
            m.then_inc(pe_setup, 1)
            conv(0, 1, 0)
            pe.wait_ge(dve_setup, 4)
            for c in range(C):
                mm3(bank(1)[:, 0:D], xc_hi[:, c, :], xc_lo[:, c, :], wvT_hi[:, c, :], wvT_lo[:, c, :],
                    c == 0, c == C - 1)
            for c2 in range(C):
                for c in range(C):
                    m = mm3(bank(2)[:, c2 * P:(c2 + 1) * P], qk_hi[:, c, c2 * P:(c2 + 1) * P],
                            qk_lo[:, c, c2 * P:(c2 + 1) * P], xc_hi[:, c, :], xc_lo[:, c, :],
                            c == 0, c == C - 1)
            m.then_inc(pe_setup, 1)
            conv(0, 1, 1)
            pe.wait_ge(dve_setup, 5)
            for c in range(C):
                m = mm3(bank(3)[:, 0:P], gc_hi[:, c, :], gc_lo[:, c, :], xc_hi[:, c, :], xc_lo[:, c, :],
                        c == 0, c == C - 1)
            m.then_inc(pe_setup, 1)
            conv(1, 0, 0)
            pe.wait_ge(dve_setup, 6)
            for c in range(C):
                m = transpose(bank(0)[:, c * P:(c + 1) * P], yc[:, c * P:(c + 1) * P])
            m.then_inc(pe_setup, 1)
            conv(1, 0, 1)
            pe.wait_ge(dve_setup, 7)
            for half in range(2):
                for c in range(C):
                    mm3(bank(4 + half), yc_hi[:, c, :], yc_lo[:, c, :],
                        snT_hi[:, c, half * 512:(half + 1) * 512], snT_lo[:, c, half * 512:(half + 1) * 512],
                        c == 0, c == C - 1)
            for e in range(E):
                for c in range(C):
                    mm3(bank(2)[:, 2 * e:2 * e + 2], snT_hi[:, c, e * P:(e + 1) * P],
                        snT_lo[:, c, e * P:(e + 1) * P], yc_hi[:, c, 0:2], yc_lo[:, c, 0:2],
                        c == 0, c == C - 1)
            for c in range(C):
                m = transpose(bank(3)[0:3, c * P:(c + 1) * P], y3[:, c, :])
            m.then_inc(pe_setup, 1)
            conv(1, 1, 0)
            conv(1, 1, 1)
            pe.wait_ge(dve_setup, 9)

            def attn_xT(g, b):
                n = g * G + b
                pe.wait_ge(xhat_ready, n + 1)
                if b >= 2:
                    pe.wait_ge(xT_split, n - 1)
                for r in range(R):
                    for c in range(C):
                        m = transpose(bank(b % 2)[:, c * NQ + r * P:c * NQ + (r + 1) * P],
                                      xhat[:, b % 2, r, c * P:(c + 1) * P])
                m.then_inc(xT_ready, 1)

            def attn_g(g, b):
                n, k = g * G + b, b % 2
                pe.wait_ge(xT_split, n + 1)
                for c2 in range(C):
                    for c in range(C):
                        m = mm3(bank(2)[:, c2 * NQ:(c2 + 1) * NQ], qk_hi[:, c, c2 * P:(c2 + 1) * P],
                                qk_lo[:, c, c2 * P:(c2 + 1) * P], xT_hi[:, k, c, 0:NQ], xT_lo[:, k, c, 0:NQ],
                                c == 0, c == C - 1)
                m.then_inc(g_ready, 1)

            def attn_v(g, b):
                n, k = g * G + b, b % 2
                if b >= 1:
                    pe.wait_ge(v_split, n)
                for r in range(R):
                    for c in range(C):
                        m = mm3(bank(3)[:, r * D:(r + 1) * D], xT_hi[:, k, c, r * P:(r + 1) * P],
                                xT_lo[:, k, c, r * P:(r + 1) * P], wvT_hi[:, c, :], wvT_lo[:, c, :],
                                c == 0, c == C - 1)
                m.then_inc(v_ready, 1)

            def attn_scores(g, b):
                n, k = g * G + b, b % 2
                pe.wait_ge(g_split, n + 1)
                if b >= 1:
                    pe.wait_ge(scores_masked, n)
                for r in range(R):
                    for c in range(C):
                        m = mm3(bank(4 + r)[:, 0:NT], g_hi[:, c, r * P:(r + 1) * P],
                                g_lo[:, c, r * P:(r + 1) * P], xT_hi[:, k, c, :], xT_lo[:, k, c, :],
                                c == 0, c == C - 1)
                m.then_inc(scores_ready, 1)

            def attn_pT(g, b):
                n, k = g * G + b, b % 2
                pe.wait_ge(prob_ready, n + 1)
                for r in range(R):
                    for r2 in range(R):
                        m = transpose(bank(6)[:, r2 * NQ + r * P:r2 * NQ + (r + 1) * P],
                                      prob[:, k, r, r2 * P:(r2 + 1) * P])
                m.then_inc(pT_ready, 1)

            def attn_out(g, b):
                n, k = g * G + b, b % 2
                pe.wait_ge(pT_split, n + 1)
                pe.wait_ge(v_split, n + 1)
                if b >= 1:
                    pe.wait_ge(h_ready, n)
                for r in range(R):
                    for r2 in range(R):
                        m = mm3(bank(7)[:, r * D:(r + 1) * D], pT_hi[:, r2, r * P:(r + 1) * P],
                                pT_lo[:, r2, r * P:(r + 1) * P], v_hi[:, k, r2, :], v_lo[:, k, r2, :],
                                r2 == 0, r2 == R - 1)
                m.then_inc(attn_ready, 1)

            def disp_yT(g, b):
                n, i = g * G + b, g * IT + 2 * b
                pe.wait_ge(y_ready, n + 1)
                if b >= 1:
                    pe.wait_ge(lsb_ready, (i - 1) * R + 1)
                for r in range(R):
                    for c in range(C):
                        m = transpose(bank(0)[:, c * NQ + r * P:c * NQ + (r + 1) * P],
                                      y[:, b % 2, r, c * P:(c + 1) * P])
                m.then_inc(yT_ready, 1)

            def disp_logits(g, i):
                pe.wait_ge(yT_split, g * G + i // 2 + 1)
                if i >= 1:
                    pe.wait_ge(lsb_ready, (g * IT + i - 1) * R + R)
                h = slice(i % 2 * HM, (i % 2 + 1) * HM)
                for r in range(R):
                    if i >= 3 and r == 1:
                        pe.wait_ge(d3_copied, g * IT + i - 1)
                    for c in range(C):
                        m = mm3(bank(r), yT_hi[:, c, r * P:(r + 1) * P], yT_lo[:, c, r * P:(r + 1) * P],
                                snT_hi[:, c, h], snT_lo[:, c, h], c == 0, c == C - 1)
                    m.then_inc(logits_ready, 1)

            def disp_lT(g, i):
                pe.wait_ge(lsb_ready, (g * IT + i) * R + R)
                for a in range(HE):
                    if i >= 1 and a % 2 == 0:
                        pe.wait_ge(dT_exp, (g * IT + i - 1) * 2 + a // 2 + 1)
                    e = i % 2 * HE + a
                    for r in range(R):
                        m = transpose(bank(2 + a // 2)[:, a % 2 * NQ + r * P:a % 2 * NQ + (r + 1) * P],
                                      lsb[:, i // 2 % 2, r, e * P:(e + 1) * P])
                    if a % 2:
                        m.then_inc(lT_ready, 1)

            def disp_dT(g, i):
                if i >= 1:
                    pe.wait_ge(d_split, g * IT + i)
                for a in range(HE):
                    if a % 2 == 0:
                        pe.wait_ge(dT_scaled, (g * IT + i) * 2 + a // 2 + 1)
                    for r in range(R):
                        m = transpose(bank(4 + r)[:, a * P:(a + 1) * P],
                                      dT[:, i % 2 * HE + a, r * P:(r + 1) * P])
                m.then_inc(d_ready, 1)
                pe.wait_ge(dc3_ready, g * IT + i + 1)
                pe.wait_ge(lsb_ready, (g * IT + min(i + 1 + (i == 0), IT - 1)) * R + R)
                for a in range(HE):
                    m = transpose(bank(1)[0:3, a * P:(a + 1) * P], dc3[:, i % 2 * HE + a, :])
                m.then_inc(d3_ready, 1)

            def disp_slots(g, i):
                b, k = i // 2, i % 2
                pe.wait_ge(y_split, g * G + b + 1)
                pe.wait_ge(d_split, g * IT + i + 1)
                if i == 0:
                    pe.wait_ge(h_ready, (g + 1) * G)
                for c in range(C):
                    if i >= 1:
                        pe.wait_ge(slots_split, (g * IT + i - 1) * C + c + 1)
                    for r in range(R):
                        mm3(bank(6 + c), y_hi[:, b % 2, r, c * P:(c + 1) * P],
                            y_lo[:, b % 2, r, c * P:(c + 1) * P], d_hi[:, k, r, :], d_lo[:, k, r, :],
                            r == 0, False)
                    if c == 0:
                        pe.wait_ge(d3_copied, g * IT + i + 1)
                    nc.tensor.matmul(bank(6 + c), ycls3[:, c * P:(c + 1) * P], d3[:, :],
                                     start=False, stop=True).then_inc(slots_ready, 1)

            def hidden(g, e, j):
                k, jj = j // 2, slice(j % 2 * P, (j % 2 + 1) * P)
                if j % 2 == 0:
                    pe.wait_ge(w1_split, (g * E + e) * (J // 2) + j // 2 + 3)
                for c in range(C):
                    m = mm3(bank(j % RING), w1_hi[:, k, c, jj], w1_lo[:, k, c, jj],
                            slot_hi[:, e, c * W:(c + 1) * W], slot_lo[:, e, c * W:(c + 1) * W],
                            c == 0, c == C - 1)
                m.then_inc(hidden_ready, 1)

            def expert_out(g, e, j):
                t = (g * E + e) * J + j
                k = j % RING
                if j % 2 == 0:
                    pe.wait_ge(w2_split, (g * E + e) * (J // 2) + j // 2 + 3)
                pe.wait_ge(hT_split, t + 1)
                if j == 0:
                    pe.wait_ge(eo_summed, g * E + e + 1)
                for b in range(G):
                    o = bank(4 + b // 2)[:, b % 2 * D:(b % 2 + 1) * D]
                    m = mm3(o, hT_hi[:, k, b * P:(b + 1) * P], hT_lo[:, k, b * P:(b + 1) * P],
                            w2_hi[:, j // 2 % 2, j % 2, :], w2_lo[:, j // 2 % 2, j % 2, :],
                            j == 0 and b % 2 == 0, j == J - 1, shared=True)
                m.then_inc(tile_free, 1)

            def comb_cT(g, b, k):
                if b >= 1:
                    pe.wait_ge(cT_split, (g * G + b - 1) * E // 2 + k + 1)
                for e in (2 * k, 2 * k + 1):
                    for r in range(R):
                        m = transpose(bank(k)[:, e % 2 * NQ + r * P:e % 2 * NQ + (r + 1) * P],
                                      cexp[:, b, r, e * P:(e + 1) * P])
                m.then_inc(cT_ready, 1)

            def comb_out(g, b):
                n = g * G + b
                pe.wait_ge(cT_split, (n + 1) * E // 2)
                if b == 0:
                    pe.wait_ge(ccls_copied, g * 2 + 1)
                    pe.wait_ge(eo_split, (g + 1) * E - 1)
                if b == 1:
                    pe.wait_ge(ccls_copied, g * 2 + 2)
                if b >= 1:
                    pe.wait_ge(outT_copied, n * C)
                for c in range(C):
                    for e in range(E):
                        if b == 0 and c == 0 and e == E - 1:
                            pe.wait_ge(eo_split, (g + 1) * E)
                        o = b * D + c * P
                        m = mm3(bank(4 + c)[:, 0:NT], slot_hi[:, e, o:o + P], slot_lo[:, e, o:o + P],
                                cT_hi[b % 2][:, e, :], cT_lo[b % 2][:, e, :], e == 0, e == E - 1)
                    m.then_inc(outT_ready, 1)

            def comb_fin(g, b):
                n = g * G + b
                pe.wait_ge(outT_copied, n * C + C)
                if b >= 1:
                    pe.wait_ge(fin_done, n)
                for r in range(R):
                    for c in range(C):
                        m = transpose(bank(6)[:, r * D + c * P:r * D + (c + 1) * P],
                                      oT[:, b % 2, c, r * P:(r + 1) * P])
                m.then_inc(fin_ready, 1)

            attn_xT(0, 0)
            attn_xT(0, 1)

            def group(g, last):
                attn_g(g, 0)
                attn_v(g, 0)
                for b in range(G):
                    attn_scores(g, b)
                    if b >= 1:
                        attn_pT(g, b - 1)
                    if b < G - 1:
                        attn_g(g, b + 1)
                    if b >= 1:
                        attn_out(g, b - 1)
                    if b < G - 1:
                        attn_v(g, b + 1)
                    if b < G - 2:
                        attn_xT(g, b + 2)

                disp_yT(g, 0)
                attn_pT(g, G - 1)
                disp_logits(g, 0)
                attn_out(g, G - 1)
                disp_logits(g, 1)
                disp_lT(g, 0)
                disp_yT(g, 1)
                disp_logits(g, 2)
                disp_lT(g, 1)
                disp_dT(g, 0)
                for i in range(IT - 1):
                    disp_slots(g, i)
                    if i % 2 and i + 3 < IT:
                        disp_yT(g, (i + 3) // 2)
                    if i + 2 < IT:
                        disp_lT(g, i + 2)
                    disp_dT(g, i + 1)
                    if i + 3 < IT:
                        disp_logits(g, i + 3)

                pe.wait_ge(slots_split, (g * IT + IT - 1) * C)
                pe.wait_ge(d3_copied, (g + 1) * IT)
                pe.wait_ge(dT_exp, (g + 1) * IT * 2)
                hidden(g, 0, 0)
                hidden(g, 0, 1)
                disp_slots(g, IT - 1)
                for j in range(2, AHEAD):
                    hidden(g, 0, j)
                with pe.Fori(0, E - 1) as e:
                    for j in range(J):
                        if j < J - AHEAD:
                            hidden(g, e, j + AHEAD)
                        else:
                            if j + AHEAD == J:
                                pe.wait_ge(slots_split, (g + 1) * IT * C)
                            hidden(g, e + 1, j + AHEAD - J)
                        expert_out(g, e, j)
                for j in range(J):
                    if j < J - AHEAD:
                        hidden(g, E - 1, j + AHEAD)
                    expert_out(g, E - 1, j)
                    if j >= RING:
                        comb_cT(g, 0, j - RING)

                for b in range(G):
                    for k in range(E // 2):
                        if b < G - 1:
                            comb_cT(g, b + 1, k)
                    comb_out(g, b)
                    if b >= 1:
                        comb_fin(g, b - 1)
                if not last:
                    pe.wait_ge(cT_split, (g + 1) * G * E // 2)
                    attn_xT(g + 1, 0)
                    attn_xT(g + 1, 1)
                comb_fin(g, G - 1)
                for c in range(C):
                    m = transpose(bank(7)[0:G, c * P:(c + 1) * P], ocls[:, c, :])
                m.then_inc(fcls_ready, 1)

            over_groups(pe, group)

        @block.scalar
        def _(act):
            copy = lambda o, i, **k: nc.scalar.activation(o, i, ACT.Copy, **k)

            def gray_start(t, acc):
                act.wait_ge(x_loaded, 16 * t + 16)
                copy(acc[0], xrow[:, 0, :].rearrange("p (r w) -> p r w", r=R), scale=GRAY_W[0])\
                    .then_inc(gray_first, 1)

            def edge_abs(t, b, acc):
                act.wait_ge(conv_done, t + 1)
                nc.scalar.activation(edge[:, b, :, :], acc[0], ACT.Abs)
                nc.scalar.activation(acc[1], acc[1], ACT.Abs).then_inc(abs_done, 1)

            def pe_gray_start(s):
                act.wait_ge(pe_x_loaded, 16 * s + 16)
                copy(first_p[:, s, :], x_p[:, 0, :], scale=GRAY_W[0]).then_inc(pe_gray_first, 1)

            def pe_edge_abs(s):
                act.wait_ge(pe_conv_done, s + 1)
                nc.scalar.activation(edge[:, 2 * s, :, :], acc_bank[0], ACT.Abs)
                nc.scalar.activation(acc_bank[1], acc_bank[1], ACT.Abs).then_inc(pe_abs_done, 1)

            pe_gray_start(0)
            gray_start(0, acc_sbuf[0])
            act.wait_ge(const_loaded, 16 * 9)
            for e in range(E):
                nc.scalar.activation(junk[:, 0:D], sn_n[:, e, :], ACT.Square, accum_out=ssq[:, e:e + 1])\
                  .then_inc(square_link, 1)
                act.wait_ge(square_link, e + 1)
            act.sem_inc(act_setup, 1)
            nc.scalar.activation(snorm[:, :], ssq[:, :], ACT.Sqrt).then_inc(act_setup, 1)
            act.wait_ge(halo_zero, 2)
            nc.scalar.activation(csq[:, 0:1], cve[:, 0:1], ACT.Sqrt).then_inc(act_setup, 1)
            act.wait_ge(pe_setup, 1)
            copy(qk_hi[:, :, :], bank(0).rearrange("p (c n) -> p c n", c=C)).then_inc(act_setup, 1)
            copy(wvT_hi[:, :, :], bank(1).rearrange("p (c n) -> p c n", c=C)).then_inc(act_setup, 1)
            act.wait_ge(pe_setup, 2)
            act.wait_ge(dve_setup, 1)
            for c in range(C):
                copy(snT_hi[:, c, :], bank(2 + 2 * c, 2), scale=gg[:, c:c + 1]).then_inc(act_setup, 1)
            act.wait_ge(pe_setup, 3)
            copy(b1T[:, :], bank(0)[:, D:D + E * J])
            copy(xc_hi[:, :, :], bank(0)[:, 0:D].rearrange("p (c n) -> p c n", c=C)).then_inc(act_setup, 1)
            pe_gray_start(1)
            act.wait_ge(pe_setup, 4)
            copy(vcls_b[:, :], bank(1)[:, 0:D]).then_inc(act_setup, 1)
            copy(gc_hi[:, :, :], bank(2)[:, 0:D].rearrange("p (c n) -> p c n", c=C)).then_inc(act_setup, 1)
            pe_edge_abs(0)
            act.wait_ge(halo_zero, 3)
            nc.scalar.activation(csq[:, 2:4], cve[:, 2:4], ACT.Sqrt).then_inc(act_setup, 1)
            gray_start(1, acc_sbuf[1])
            act.wait_ge(pe_setup, 6)
            copy(yc_hi[:, :, :], bank(0)[:, 0:D].rearrange("p (c n) -> p c n", c=C)).then_inc(act_setup, 1)
            act.wait_ge(dve_setup, 8)
            nc.scalar.activation(junk[:, :], bank(4, 2), ACT.Exp, bias=cnegm[:, 0:1],
                                 accum_out=csumc[:, 0:1]).then_inc(act_setup, 1)
            nc.scalar.activation(cexpT[:, :], lclsT[:, :], ACT.Exp, bias=cnegm[:, 0:1])\
              .then_inc(act_setup, 1)
            act.wait_ge(act_setup, 14)
            copy(ccls_hi[:, :, 0], cexpT[:, :]).then_inc(act_setup, 1)
            copy(ycls3[:, :], bank(3)[0:3, 0:D]).then_inc(act_setup, 1)
            edge_abs(0, 1, acc_sbuf[0])
            pe_edge_abs(1)
            edge_abs(1, 3, acc_sbuf[1])

            def attn_front(g, b):
                n, k = g * G + b, b % 2
                act.wait_ge(xT_ready, n + 1)
                if b >= 2:
                    act.wait_ge(scores_ready, n - 1)
                copy(xT_hi[:, k, :, 0:NQ], bank(k).rearrange("p (c n) -> p c n", c=C)).then_inc(xT_rounded, 1)

            def attn_g(g, b):
                n = g * G + b
                act.wait_ge(g_ready, n + 1)
                if b >= 1:
                    act.wait_ge(scores_ready, n)
                copy(g_hi[:, :, :], bank(2).rearrange("p (c n) -> p c n", c=C), scale=SCALE)\
                    .then_inc(g_rounded, 1)

            def attn_v(g, b):
                n, k = g * G + b, b % 2
                act.wait_ge(v_ready, n + 1)
                if b >= 2:
                    act.wait_ge(attn_ready, n - 1)
                copy(v_hi[:, k, :, :], bank(3).rearrange("p (r n) -> p r n", r=R)).then_inc(v_rounded, 1)

            def attn_exp(g, b):
                n, k = g * G + b, b % 2
                act.wait_ge(negm_ready, n + 1)
                if b >= 2:
                    act.wait_ge(pT_ready, n - 1)
                    act.wait_ge(h_ready, n - 1)
                for r in range(R):
                    m = nc.scalar.activation(prob[:, k, r, :], sm[:, r, :], ACT.Exp, bias=negm[:, r:r + 1],
                                             accum_out=asum[:, k, r:r + 1])
                m.then_inc(prob_ready, 1)

            def attn_pT(g, b):
                n = g * G + b
                act.wait_ge(pT_ready, n + 1)
                if b >= 1:
                    act.wait_ge(attn_ready, n)
                copy(pT_hi[:, :, :], bank(6).rearrange("p (r n) -> p r n", r=R)).then_inc(pT_rounded, 1)

            def attn_cls(g, b):
                n = g * G + b
                act.wait_ge(arinv_ready, n + 1)
                if b >= 1:
                    act.wait_ge(h_ready, n)
                for r in range(R):
                    m = copy(base[:, r, :], vcls_b[:, :], scale=pcls[:, b % 2, r:r + 1])
                m.then_inc(clsv_ready, 1)

            def disp_sqrt(g, half):
                act.wait_ge(ve2_ready, g * 2 + half + 1)
                q = slice(half * G * R // 2, (half + 1) * G * R // 2)
                nc.scalar.activation(sq2[:, :, q], ve2[:, :, q], ACT.Sqrt).then_inc(sq2_ready, 1)

            def disp_yT(g, b):
                n = g * G + b
                act.wait_ge(yT_ready, n + 1)
                if b >= 1:
                    act.wait_ge(logits_ready, (g * IT + 2 * b) * R)
                else:
                    act.wait_ge(scores_ready, (g + 1) * G)
                copy(yT_hi[:, :, :], bank(0).rearrange("p (c n) -> p c n", c=C)).then_inc(yT_rounded, 1)

            def disp_y(g, b):
                n, k = g * G + b, b % 2
                act.wait_ge(y_ready, n + 1)
                if b >= 2:
                    act.wait_ge(slots_ready, (g * IT + 2 * b - 2) * C)
                copy(y_hi[:, k, :, :], y[:, k, :, :]).then_inc(y_rounded, 1)

            def disp_lsb(g, i):
                b = i // 2
                if b >= 2:
                    act.wait_ge(lT_ready, (g * IT + i - 3) * 2)
                    act.wait_ge(cexp_ready, (g * G + b - 1) * R)
                if b == 1:
                    act.wait_ge(attn_ready, (g + 1) * G)
                for r in range(R):
                    act.wait_ge(logits_ready, (g * IT + i) * R + r + 1)
                    copy(lsb[:, b % 2, r, i % 2 * HM:(i % 2 + 1) * HM], bank(r)).then_inc(lsb_ready, 1)

            def disp_cexp(g, b, rs=range(R)):
                n = g * G + b
                for r in rs:
                    act.wait_ge(cneg_ready, n * R + r + 1)
                    nc.scalar.activation(cexp[:, b, r, :], lsb[:, b % 2, r, :], ACT.Exp,
                                         bias=cneg[:, r:r + 1],
                                         accum_out=csum[:, b * R + r:b * R + r + 1]).then_inc(cexp_ready, 1)

            def disp_exp(g, i):
                if i == 0:
                    act.wait_ge(h_ready, (g + 1) * G)
                if i >= 2:
                    act.wait_ge(d_ready, g * IT + i - 1)
                for q in range(2):
                    act.wait_ge(tneg_ready, g * IT + i + 1)
                    e0 = i % 2 * HE + 2 * q
                    for a in range(2):
                        nc.scalar.activation(dT[:, e0 + a, :], bank(2 + q)[:, a * NQ:(a + 1) * NQ], ACT.Exp,
                                             bias=tneg[:, e0 + a:e0 + a + 1],
                                             accum_out=dsum[:, e0 + a:e0 + a + 1])
                    nc.scalar.activation(ecls[:, e0:e0 + 2], tdl[:, e0:e0 + 2], ACT.Exp).then_inc(dT_exp, 1)

            def disp_d(g, i):
                if i >= 2:
                    act.wait_ge(slots_ready, (g * IT + i - 1) * C)
                act.wait_ge(d_ready, g * IT + i + 1)
                copy(d_hi[:, i % 2, :, :], bank(4, 2).rearrange("p (r n) -> p r n", r=R)).then_inc(d_rounded, 1)
                act.wait_ge(d3_ready, g * IT + i + 1)
                if i >= 1:
                    act.wait_ge(slots_ready, (g * IT + i) * C)
                copy(d3[:, :], bank(1)[0:3, :]).then_inc(d3_copied, 1)

            def slot_view(t, i, c):
                e = slice(i % 2 * HE, (i % 2 + 1) * HE)
                return t[:, e, c * W + i // 2 * P:c * W + (i // 2 + 1) * P]

            def disp_slots(g, i):
                for c in range(C):
                    act.wait_ge(slots_ready, (g * IT + i) * C + c + 1)
                    copy(slot_view(slot_hi, i, c), bank(6 + c).rearrange("p (e m) -> p e m", m=P),
                         scale=gam[:, c:c + 1]).then_inc(slots_rounded, 1)

            def gelu(g, e, j):
                t = (g * E + e) * J + j
                k = j % RING
                act.wait_ge(hidden_ready, t + 1)
                nc.scalar.activation(bank(k), bank(k), ACT.Gelu, bias=b1T[:, bass.ds(e * J + j, 1)])\
                  .then_inc(gelu_done, 1)
                act.wait_ge(gelu_done, t + 1)
                act.wait_ge(tile_free, t + 1)
                copy(hT_hi[:, k, :], bank(k)).then_inc(hT_rounded, 1)

            def round_w1(g, e, q):
                n, k = (g * E + e) * 2 + q // 2, q % 2
                act.wait_ge(w1_loaded[k], 16 * n + 16)
                copy(w1_hi[:, q, :, :], w1_in[:, k, :, :]).then_inc(w1_rounded, 1)

            def expert_hi(g, e):
                act.wait_ge(eo_summed, g * E + e + 2)
                copy(slot_hi[:, e, :], eo_f[:, :]).then_inc(eo_rounded, 1)

            def comb_cT(g, b):
                n = g * G + b
                for k in range(E // 2):
                    act.wait_ge(cT_ready, n * E // 2 + k + 1)
                    if b >= 2:
                        act.wait_ge(outT_ready, (n - 1) * C)
                    copy(cT_hi[b % 2][:, 2 * k:2 * k + 2, 0:NQ],
                         bank(k).rearrange("p (e n) -> p e n", e=2)).then_inc(cT_rounded, 1)

            def comb_oT(g, b):
                n = g * G + b
                for c in range(C):
                    act.wait_ge(outT_ready, n * C + c + 1)
                    if b >= 2:
                        act.wait_ge(fin_ready, n - 1)
                    copy(ocls[:, c, b:b + 1], bank(4 + c)[:, NQ:NQ + 1])
                    copy(oT[:, b % 2, c, :], bank(4 + c)[:, 0:NT]).then_inc(outT_copied, 1)

            def root1(g):
                act.wait_ge(ve1_ready, g + 1)
                nc.scalar.activation(sd1[:, :], ve1[:, :], ACT.Sqrt).then_inc(sd1_ready, 1)

            root1(0)
            attn_front(0, 0)
            attn_front(0, 1)

            def group(g, last):
                attn_g(g, 0)
                attn_v(g, 0)
                for b in range(G):
                    if b >= 1:
                        attn_pT(g, b - 1)
                        attn_cls(g, b - 1)
                    if b < G - 1:
                        attn_g(g, b + 1)
                    if b == G - 1:
                        disp_sqrt(g, 0)
                    attn_exp(g, b)
                    if b < G - 1:
                        attn_v(g, b + 1)
                    if b < G - 2:
                        attn_front(g, b + 2)

                disp_yT(g, 0)
                attn_pT(g, G - 1)
                attn_cls(g, G - 1)
                disp_lsb(g, 0)
                disp_lsb(g, 1)
                disp_yT(g, 1)
                disp_exp(g, 0)
                disp_y(g, 0)
                disp_lsb(g, 2)
                disp_d(g, 0)
                disp_exp(g, 1)
                disp_cexp(g, 0)
                for i in range(IT):
                    if i == IT - 1:
                        gelu(g, 0, 0)
                    disp_slots(g, i)
                    if i % 2 and i + 3 < IT:
                        disp_yT(g, (i + 3) // 2)
                    if i + 1 < IT:
                        disp_d(g, i + 1)
                    if i == 0:
                        disp_sqrt(g, 1)
                    if i == IT - 2:
                        round_w1(g, 0, 2)
                    if i == IT - 3:
                        disp_cexp(g, G - 2, [1])
                        act.wait_ge(y_split, (g + 1) * G)
                        act.wait_ge(lT_ready, (g + 1) * IT * 2)
                        act.wait_ge(cexp_ready, (g * G + G - 1) * R)
                        round_w1(g, 0, 0)
                        round_w1(g, 0, 1)
                    if i + 2 < IT:
                        disp_exp(g, i + 2)
                    if i == 3:
                        disp_cexp(g, 1, [1])
                    if i + 3 < IT:
                        disp_lsb(g, i + 3)
                    if i % 2 == 0 and i // 2 + 1 < G:
                        disp_y(g, i // 2 + 1)
                    if i == 2 or i == 4:
                        disp_cexp(g, i // 2, [0])
                    if i == IT - 2:
                        disp_cexp(g, G - 1)

                def tile(e, j, final):
                    gelu(g, e, j)
                    if j == 1:
                        round_w1(g, e, 3)
                    if j in (3, 5, 7) and not final:
                        round_w1(g, e + 1, j // 2 - 1)

                def experts(pair, final):
                    for odd in range(2):
                        e = pair * 2 + odd
                        for j in range(2, J + 2):
                            if j < J:
                                tile(e, j, final and odd)
                            elif not (final and odd):
                                tile(e + 1, j - J, False)
                            if j == 2 and not odd and not last:
                                act.wait_ge(edge_done, g * G + G + pair)
                                act.wait_ge(halo_zero, 4 + g)
                                gray_start(g * G + 2 + pair, acc_bank)
                            if j == 7 and odd and not last:
                                edge_abs(g * G + 2 + pair, pair, acc_bank)
                        if final and odd:
                            comb_cT(g, 0)
                        expert_hi(g, e)

                tile(0, 1, False)
                with act.Fori(0, E // 2 - 1) as pair:
                    experts(pair, False)
                experts(E // 2 - 1, True)

                for b in range(G):
                    if b < G - 1:
                        comb_cT(g, b + 1)
                    if b == 0 and not last:
                        root1(g + 1)
                    comb_oT(g, b)
                if not last:
                    attn_front(g + 1, 0)
                    attn_front(g + 1, 1)

            over_groups(act, group)

        @block.vector
        def _(dve):
            STT = nc.vector.scalar_tensor_tensor
            f = lambda t: t.bitcast(f32)

            def lo(o, value, hi):
                return nc.vector.tensor_tensor(o, value, f(hi), ALU.subtract)

            class Link:
                def __init__(self, s, base):
                    self.s, self.base, self.n = s, base, 0

                def mark(self, ins):
                    self.n += 1
                    ins.then_inc(self.s, 1)

                def wait(self):
                    dve.wait_ge(self.s, self.base + self.n)

                def __call__(self, ins):
                    self.mark(ins)
                    self.wait()

            T_LINKS = 13

            def gray_sum(o, first, px, link):
                link(STT(first, px[:, 1, :].rearrange("p (r w) -> p r w", r=R), GRAY_W[1], first,
                         ALU.mult, ALU.add))
                return STT(o, px[:, 2, :].rearrange("p (r w) -> p r w", r=R), GRAY_W[2], first,
                           ALU.mult, ALU.add)

            def gray_rest(t, acc, link):
                dve.wait_ge(gray_first, t + 1)
                gray_sum(gray[:, 1:R + 1, 1:D + 1], acc[0], xrow, link).then_inc(gray_done, 1)

            def pe_gray_rest(s, link):
                dve.wait_ge(pe_gray_first, s + 1)
                gray_sum(gray_p[:, s, :, 1:D + 1], first_p[:, s, :].rearrange("p (r w) -> p r w", r=R),
                         x_p, link).then_inc(pe_gray_done, 1)

            def conv_tap(t, tap, accs, link):
                dy, dx = divmod(tap, 3)
                if tap == 0:
                    dve.wait_ge(halo_loaded, 64 * t + 64)
                    dve.wait_ge(gray_done, t + 1)
                src = gray[:, dy:dy + R, dx:dx + D]
                for k, acc in enumerate(accs):
                    w = taps[:, 9 * k + tap:9 * k + tap + 1]
                    if tap == 0:
                        m = nc.vector.tensor_scalar(acc, src, w, None, ALU.mult)
                    else:
                        m = STT(acc, src, w, acc, ALU.mult, ALU.add)
                if tap == 8:
                    m.then_inc(conv_done, 1)
                else:
                    link(m)

            def edge_sum(t, b, acc, link):
                dve.wait_ge(abs_done, t + 1)
                e = edge[:, b, :, :]
                link(nc.vector.tensor_tensor(e, acc[1], e, ALU.add))

            def pe_edge_sum(s, link):
                dve.wait_ge(pe_abs_done, s + 1)
                e = edge[:, 2 * s, :, :]
                nc.vector.tensor_tensor(e, acc_bank[1], e, ALU.add).then_inc(pe_edge_summed, 1)
                dve.wait_ge(pe_edge_summed, s + 1)

            def edge_stats(b, link):
                for r in range(R):
                    link(nc.vector.bn_stats(st1[:, r, :], edge[:, b, r, :]))
                apart(dve)
                for r in range(R):
                    m = nc.vector.bn_aggr(mv1_b[:, r, :], st1[:, r, :])
                link(m)
                nc.vector.tensor_copy(mv1[:, bass.ds(b * R, R), :], mv1_b[:, :, :]).then_inc(edge_done, 1)

            link = Link(disp_link, 0)
            tokens = Link(token_link, 0)
            nc.vector.memset(gray_p[:, :, :, :], 0.0).then_inc(pe_gray_zero, 1)
            nc.vector.memset(wide_id[:, :], 0.0).then_inc(wmat_ready, 1)
            nc.vector.memset(gray[:, :, :], 0.0).then_inc(halo_zero, 1)
            nc.vector.memset(xcls_hi[:, :, :].bitcast(f32), 0.0)
            nc.vector.memset(xcls_lo[:, :, :].bitcast(f32), 0.0)
            nc.vector.memset(ccls_hi[:, :, :].bitcast(f32), 0.0)
            nc.vector.memset(ccls_lo[:, :, :].bitcast(f32), 0.0)
            dve.wait_ge(const_loaded, 16 * 9)
            dve.wait_ge(masks_ready, 1 + 2 * R)
            link(nc.vector.tensor_scalar(taps[:, :], taps[:, :], 0.5, None, ALU.mult))
            dve.wait_ge(wmat_ready, 1)
            link(nc.vector.tensor_copy(wide_id[:, 1:P + 1], ident[:, :]))
            dve.wait_ge(pe_gray_zero, 1)
            nc.vector.tensor_tensor(
                wmat[:, :, :], wide_id[:, :].rearrange("p (a n) -> p a n", a=1).to_broadcast([P, 18, P + 2]),
                taps[:, :].rearrange("p (a b) -> p a b", b=1).to_broadcast([P, 18, P + 2]), ALU.mult)\
              .then_inc(wmat_ready, 1)
            pe_gray_rest(0, tokens)
            dve.wait_ge(halo_zero, 1)
            gray_rest(0, acc_sbuf[0], tokens)
            link(nc.vector.tensor_tensor(gg[:, :], gam[:, :], sgam[:, :], ALU.mult))
            link(nc.vector.bn_stats(cst[:, 0, :], clsrow[:, :]))
            link(nc.vector.bn_aggr(cmv[:, 0, :], cst[:, 0, :]))
            nc.vector.tensor_scalar(cve[:, 0:1], cmv[:, 0, 1:2], EPS, None, ALU.add).then_inc(halo_zero, 1)
            dve.wait_ge(act_setup, 2)
            link(nc.vector.tensor_scalar(snorm[:, :], snorm[:, :], 1e-12, None, ALU.max))
            link(nc.vector.reciprocal(srin[:, :], snorm[:, :]))
            for e in range(E):
                m = nc.vector.tensor_scalar(sn_n[:, e, :], sn_n[:, e, :], srin[:, e:e + 1], RMS, ALU.mult, ALU.mult)
            m.then_inc(dve_setup, 1)
            dve.wait_ge(act_setup, 3)
            link(nc.vector.reciprocal(csc[:, 0:1], csq[:, 0:1]))
            nc.vector.tensor_scalar(xc[:, :], clsrow[:, :], cmv[:, 0, 0:1], csc[:, 0:1], ALU.subtract, ALU.mult)\
              .then_inc(dve_setup, 1)
            for tap in range(0, 2):
                conv_tap(0, tap, acc_sbuf[0], tokens)
            dve.wait_ge(act_setup, 4)
            lo(qk_lo[:, :, :], bank(0).rearrange("p (c n) -> p c n", c=C), qk_hi[:, :, :])
            dve.wait_ge(act_setup, 5)
            lo(wvT_lo[:, :, :], bank(1).rearrange("p (c n) -> p c n", c=C), wvT_hi[:, :, :])
            for c in range(C):
                dve.wait_ge(act_setup, 6 + c)
                m = STT(snT_lo[:, c, :], bank(2 + 2 * c, 2), gg[:, c:c + 1], f(snT_hi[:, c, :]),
                        ALU.mult, ALU.subtract)
            m.then_inc(dve_setup, 1)
            for tap in range(2, 4):
                conv_tap(0, tap, acc_sbuf[0], tokens)
            dve.wait_ge(act_setup, 8)
            link(lo(xc_lo[:, :, :], bank(0)[:, 0:D].rearrange("p (c n) -> p c n", c=C), xc_hi[:, :, :]))
            nc.vector.tensor_copy(xcls_hi[:, :, 0:1], xc_hi[:, :, 0:1])
            nc.vector.tensor_copy(xcls_lo[:, :, 0:1], xc_lo[:, :, 0:1]).then_inc(dve_setup, 1)
            for tap in range(4, 6):
                conv_tap(0, tap, acc_sbuf[0], tokens)
            dve.wait_ge(act_setup, 10)
            lo(gc_lo[:, :, :], bank(2)[:, 0:D].rearrange("p (c n) -> p c n", c=C), gc_hi[:, :, :])\
                .then_inc(dve_setup, 1)
            pe_gray_rest(1, tokens)
            pe_edge_sum(0, tokens)
            edge_stats(0, tokens)
            dve.wait_ge(pe_setup, 5)
            link(nc.vector.tensor_scalar(cf[:, 0:1], bank(3)[:, 0:1], 0.0, None, ALU.not_equal))
            link(nc.vector.reciprocal(cf[:, 1:2], cf[:, 0:1]))
            link(nc.vector.tensor_tensor(cf[:, 2:3], cf[:, 0:1], cf[:, 1:2], ALU.mult))
            link(STT(hcls_b[:, :], vcls_b[:, :], cf[:, 2:3], clsrow[:, :], ALU.mult, ALU.add))
            link(nc.vector.bn_stats(cst[:, 1, :], hcls_b[:, :]))
            link(nc.vector.bn_aggr(cmv[:, 1, :], cst[:, 1, :]))
            nc.vector.tensor_scalar(cve[:, 2:3], cmv[:, 1, 1:2], EPS, None, ALU.add)
            nc.vector.tensor_scalar(cve[:, 3:4], cmv[:, 1, 1:2], float(D), None, ALU.mult).then_inc(halo_zero, 1)
            for tap in range(6, 9):
                conv_tap(0, tap, acc_sbuf[0], tokens)
            dve.wait_ge(act_setup, 11)
            link(nc.vector.reciprocal(csc[:, 2:3], csq[:, 2:3]))
            link(nc.vector.tensor_tensor(csc[:, 3:4], csc[:, 2:3], csq[:, 3:4], ALU.mult))
            link(nc.vector.tensor_scalar(csc[:, 4:5], csc[:, 3:4], 1e-12, None, ALU.max))
            link(nc.vector.reciprocal(csc[:, 5:6], csc[:, 4:5]))
            link(STT(csc[:, 6:7], csc[:, 5:6], RMS, csc[:, 2:3], ALU.mult, ALU.mult))
            nc.vector.tensor_scalar(yc[:, :], hcls_b[:, :], cmv[:, 1, 0:1], csc[:, 6:7], ALU.subtract, ALU.mult)\
              .then_inc(dve_setup, 1)
            gray_rest(1, acc_sbuf[1], tokens)
            dve.wait_ge(act_setup, 12)
            link(lo(yc_lo[:, :, :], bank(0)[:, 0:D].rearrange("p (c n) -> p c n", c=C), yc_hi[:, :, :]))
            for k, t in enumerate((yc_hi, yc_lo, yc_hi)):
                m = nc.vector.tensor_copy(y3[:, :, k:k + 1], f(t[:, :, 0:1]))
            m.then_inc(dve_setup, 1)
            for tap in range(0, 7):
                conv_tap(1, tap, acc_sbuf[1], tokens)
            dve.wait_ge(pe_setup, 7)
            lcls = bank(2)[:, 0:2 * E].rearrange("p (e k) -> p e k", k=2)[:, :, 0]
            nc.vector.tensor_copy(lclsT[:, :], lcls)
            nc.vector.tensor_scalar(nlclsT[:, :], lcls, -1.0, None, ALU.mult)
            link(nc.vector.reduce_max(cmax[:, :], bank(4, 2), axis=AX.X))
            nc.vector.tensor_scalar(cnegm[:, :], cmax[:, :], -1.0, None, ALU.mult).then_inc(dve_setup, 1)
            dve.wait_ge(act_setup, 13)
            nc.vector.reciprocal(rcls[:, :], csumc[:, :])
            dve.wait_ge(act_setup, 16)
            lo(ccls_lo[:, :, 0], cexpT[:, :], ccls_hi[:, :, 0]).then_inc(dve_setup, 1)
            dve.wait_ge(dve_setup, 9)
            SETUP_LINKS = link.n
            edge_sum(0, 1, acc_sbuf[0], tokens)
            edge_stats(1, tokens)
            for tap in range(7, 9):
                conv_tap(1, tap, acc_sbuf[1], tokens)
            pe_edge_sum(1, tokens)
            edge_stats(2, tokens)
            edge_sum(1, 3, acc_sbuf[1], tokens)
            edge_stats(3, tokens)
            TOKEN_LINKS = tokens.n

            A_LINKS = 25

            def attn_xhat(g, b, link):
                n = g * G + b
                if b >= 2:
                    dve.wait_ge(xT_ready, n - 1)
                for r in range(R):
                    q = b * R + r
                    m = nc.vector.tensor_scalar(xhat[:, b % 2, r, :], edge[:, b, r, :], mv1[:, q, 0:1],
                                                rstd1[:, q:q + 1], ALU.subtract, ALU.mult)
                m.then_inc(xhat_ready, 1)

            def attn_front(g, b):
                n, k = g * G + b, b % 2
                dve.wait_ge(xT_rounded, n + 1)
                lo(xT_lo[:, k, :, 0:NQ], bank(k).rearrange("p (c n) -> p c n", c=C), xT_hi[:, k, :, 0:NQ])\
                    .then_inc(xT_split, 1)

            def attn_g(g, b):
                dve.wait_ge(g_rounded, g * G + b + 1)
                STT(g_lo[:, :, :], bank(2).rearrange("p (c n) -> p c n", c=C), SCALE, f(g_hi[:, :, :]),
                    ALU.mult, ALU.subtract).then_inc(g_split, 1)

            def attn_v(g, b):
                k = b % 2
                dve.wait_ge(v_rounded, g * G + b + 1)
                lo(v_lo[:, k, :, :], bank(3).rearrange("p (r n) -> p r n", r=R), v_hi[:, k, :, :])\
                    .then_inc(v_split, 1)

            def attn_mask(g, b, link):
                n = g * G + b
                dve.wait_ge(scores_ready, n + 1)
                s = bank(4, 2).rearrange("p (r n) -> p r n", r=R)[:, :, 0:NT]
                link(STT(masked[:, :, :], s, 0.0, upper[:, :, :], ALU.is_equal, ALU.max))
                if b >= 1:
                    dve.wait_ge(prob_ready, n)
                STT(sm[:, :, :], masked[:, :, :], -BIG, s, ALU.mult, ALU.add).then_inc(scores_masked, 1)
                dve.wait_ge(scores_masked, n + 1)
                link(nc.vector.reduce_max(mx[:, :], sm[:, :, :], axis=AX.X))
                nc.vector.tensor_scalar(negm[:, :], mx[:, :], -1.0, BIG / 10, ALU.mult, ALU.min)\
                  .then_inc(negm_ready, 1)

            def attn_pT(g, b):
                dve.wait_ge(pT_rounded, g * G + b + 1)
                lo(pT_lo[:, :, :], bank(6).rearrange("p (r n) -> p r n", r=R), pT_hi[:, :, :]).then_inc(pT_split, 1)

            def attn_rinv(g, b, link):
                k = b % 2
                dve.wait_ge(prob_ready, g * G + b + 1)
                link(nc.vector.reciprocal(arinv[:, k, :], asum[:, k, :]))
                nc.vector.tensor_tensor(pcls[:, k, :], prob[:, k, :, NQ], arinv[:, k, :], ALU.mult)\
                  .then_inc(arinv_ready, 1)

            def attn_res(g, b, link):
                n, k = g * G + b, b % 2
                if b == 0:
                    dve.wait_ge(out_stored, 16 * G * g + 1)
                dve.wait_ge(base_ready, n + 1)
                dve.wait_ge(attn_ready, n + 1)
                for r in range(R):
                    m = STT(hres[:, b, r, :], bank(7)[:, r * D:(r + 1) * D], arinv[:, k, r:r + 1],
                            base[:, r, :], ALU.mult, ALU.add)
                m.then_inc(h_ready, 1)
                dve.wait_ge(h_ready, n + 1)
                for r in range(R):
                    m = nc.vector.bn_stats(st2[:, r, :], hres[:, b, r, :])
                link(m)
                apart(dve)
                for r in range(R):
                    m = nc.vector.bn_aggr(mv2[:, b * R + r, :], st2[:, r, :])
                link(m)

            L_LINKS = 61

            def disp_norm(g, half, link):
                q = slice(half * G * R // 2, (half + 1) * G * R // 2)
                dve.wait_ge(sq2_ready, g * 2 + half + 1)
                link(nc.vector.reciprocal(rr2[:, q], sq2[:, 0, q]))
                link(nc.vector.tensor_tensor(nn2[:, q], rr2[:, q], sq2[:, 1, q], ALU.mult))
                link(nc.vector.tensor_scalar(nn2[:, q], nn2[:, q], 1e-12, None, ALU.max))
                link(nc.vector.reciprocal(rn2[:, q], nn2[:, q]))
                link(STT(s2[:, q], rn2[:, q], RMS, rr2[:, q], ALU.mult, ALU.mult))

            def disp_vars(g, half):
                q = slice(half * G * R // 2, (half + 1) * G * R // 2)
                nc.vector.tensor_scalar(ve2[:, 0, q], mv2[:, q, 1], EPS, None, ALU.add)
                nc.vector.tensor_scalar(ve2[:, 1, q], mv2[:, q, 1], float(D), None, ALU.mult)\
                  .then_inc(ve2_ready, 1)

            def disp_y(g, b):
                n, k = g * G + b, b % 2
                if b >= 2:
                    dve.wait_ge(yT_ready, n - 1)
                    dve.wait_ge(y_split, n - 1)
                else:
                    dve.wait_ge(xT_ready, (g + 1) * G)
                for r in range(R):
                    q = b * R + r
                    m = nc.vector.tensor_scalar(y[:, k, r, :], hres[:, b, r, :], mv2[:, q, 0:1], s2[:, q:q + 1],
                                                ALU.subtract, ALU.mult)
                m.then_inc(y_ready, 1)

            def disp_split_y(g, b):
                n, k = g * G + b, b % 2
                dve.wait_ge(y_rounded, n + 1)
                lo(y_lo[:, k, :, :], y[:, k, :, :], y_hi[:, k, :, :]).then_inc(y_split, 1)

            def disp_yT(g, b):
                dve.wait_ge(yT_rounded, g * G + b + 1)
                lo(yT_lo[:, :, :], bank(0).rearrange("p (c n) -> p c n", c=C), yT_hi[:, :, :])\
                    .then_inc(yT_split, 1)

            def disp_max(g, b, link, rs=range(R)):
                n = g * G + b
                for r in rs:
                    dve.wait_ge(lsb_ready, (g * IT + 2 * b + 1) * R + r + 1)
                    if b >= 1:
                        dve.wait_ge(cexp_ready, n * R)
                    link(nc.vector.reduce_max(cmx[:, r:r + 1], lsb[:, b % 2, r, :], axis=AX.X))
                    nc.vector.tensor_scalar(cneg[:, r:r + 1], cmx[:, r:r + 1], -1.0, None, ALU.mult)\
                      .then_inc(cneg_ready, 1)

            def disp_maxT(g, i, link):
                for q in range(2):
                    e0 = i % 2 * HE + 2 * q
                    dve.wait_ge(lT_ready, (g * IT + i) * 2 + q + 1)
                    m = nc.vector.reduce_max(tmx[:, e0:e0 + 2], bank(2 + q).rearrange("p (e n) -> p e n", e=2),
                                             axis=AX.X)
                link(m)
                s = slice(i % 2 * HE, (i % 2 + 1) * HE)
                link(STT(tneg[:, s], tmx[:, s], -1.0, nlclsT[:, s], ALU.mult, ALU.min))
                nc.vector.tensor_tensor(tdl[:, s], lclsT[:, s], tneg[:, s], ALU.add).then_inc(tneg_ready, 1)

            def disp_scale(g, i, link):
                e0 = i % 2 * HE
                s = slice(e0, e0 + HE)
                dve.wait_ge(dT_exp, (g * IT + i) * 2 + 2)
                link(nc.vector.tensor_tensor(dtot[:, s], dsum[:, s], ecls[:, s], ALU.add))
                link(nc.vector.reciprocal(drinv[:, s], dtot[:, s]))
                link.mark(nc.vector.tensor_tensor(dcls[:, s], ecls[:, s], drinv[:, s], ALU.mult))
                for q in range(2):
                    for e in (e0 + 2 * q, e0 + 2 * q + 1):
                        m = nc.vector.tensor_scalar(dT[:, e, :], dT[:, e, :], drinv[:, e:e + 1], None, ALU.mult)
                    m.then_inc(dT_scaled, 1)
                    if q == 0:
                        link.wait()
                        link.mark(nc.vector.tensor_copy(dclsh[:, s], dcls[:, s]))
                link.wait()
                if i >= 2:
                    dve.wait_ge(d3_ready, g * IT + i - 1)
                nc.vector.tensor_copy(dc3[:, s, 0], f(dclsh[:, s]))
                nc.vector.tensor_copy(dc3[:, s, 1], f(dclsh[:, s]))
                lo(dc3[:, s, 2], dcls[:, s], dclsh[:, s]).then_inc(dc3_ready, 1)

            def disp_d(g, i):
                dve.wait_ge(d_rounded, g * IT + i + 1)
                lo(d_lo[:, i % 2, :, :], bank(4, 2).rearrange("p (r n) -> p r n", r=R), d_hi[:, i % 2, :, :])\
                    .then_inc(d_split, 1)

            def slot_view(t, i, c):
                e = slice(i % 2 * HE, (i % 2 + 1) * HE)
                return t[:, e, c * W + i // 2 * P:c * W + (i // 2 + 1) * P]

            def disp_slots(g, i):
                for c in range(C):
                    dve.wait_ge(slots_rounded, (g * IT + i) * C + c + 1)
                    STT(slot_view(slot_lo, i, c), bank(6 + c).rearrange("p (e m) -> p e m", m=P),
                        gam[:, c:c + 1], f(slot_view(slot_hi, i, c)), ALU.mult, ALU.subtract)\
                        .then_inc(slots_split, 1)

            def split_hidden(g, e, j):
                dve.wait_ge(hT_rounded, (g * E + e) * J + j + 1)
                lo(hT_lo[:, j % RING, :], bank(j % RING), hT_hi[:, j % RING, :]).then_inc(hT_split, 1)

            def round_w2(g, e, q):
                n, k = (g * E + e) * 2 + q // 2, q % 2
                dve.wait_ge(w2_loaded[k], 16 * n + 16)
                dve.wait_ge(tile_free, (g * E + e) * J + 2 * q - 2 + RING)
                nc.vector.tensor_copy(w2_hi[:, k, :, :], w2_in[:, k, :, :]).then_inc(w2_rounded, 1)

            def expert_sum(g, e):
                dve.wait_ge(tile_free, (g * E + e + 1) * J + RING)
                dve.wait_ge(b2_loaded, 16 * (g * E + e) + 16)
                o = bank(4, 2).rearrange("p (b d) -> p b d", b=G)
                nc.vector.tensor_tensor(eo_f[:, :].rearrange("p (b d) -> p b d", b=G), o,
                                        b2_b[:, :].rearrange("p (a d) -> p a d", a=1).to_broadcast([P, G, D]),
                                        ALU.add).then_inc(eo_summed, 1)

            def expert_lo(g, e):
                dve.wait_ge(eo_rounded, g * E + e + 1)
                lo(slot_lo[:, e, :], eo_f[:, :], slot_hi[:, e, :]).then_inc(eo_split, 1)

            def comb_cT(g, b):
                n = g * G + b
                for k in range(E // 2):
                    dve.wait_ge(cT_rounded, n * E // 2 + k + 1)
                    lo(cT_lo[b % 2][:, 2 * k:2 * k + 2, 0:NQ], bank(k).rearrange("p (e n) -> p e n", e=2),
                       cT_hi[b % 2][:, 2 * k:2 * k + 2, 0:NQ]).then_inc(cT_split, 1)

            def comb_cls(k):
                nc.vector.tensor_copy(cT_hi[k][:, :, NQ:NT], ccls_hi[:, :, :])
                nc.vector.tensor_copy(cT_lo[k][:, :, NQ:NT], ccls_lo[:, :, :]).then_inc(ccls_copied, 1)

            def comb_fin(g, b):
                n = g * G + b
                dve.wait_ge(fin_ready, n + 1)
                for r in range(R):
                    q = b * R + r
                    m = STT(hres[:, b, r, :], bank(6)[:, r * D:(r + 1) * D], crinv[:, q:q + 1], hres[:, b, r, :],
                            ALU.mult, ALU.add)
                m.then_inc(fin_done, 1)

            def first_tokens(g, link):
                dve.wait_ge(edge_done, (g + 1) * G)
                nc.vector.tensor_scalar(ve1[:, :], mv1[:, :, 1], EPS, None, ALU.add).then_inc(ve1_ready, 1)
                for k in range(2):
                    nc.vector.tensor_copy(xT_hi[:, k, :, NQ:NT], xcls_hi[:, :, :])
                    nc.vector.tensor_copy(xT_lo[:, k, :, NQ:NT], xcls_lo[:, :, :])
                dve.wait_ge(sd1_ready, g + 1)
                nc.vector.reciprocal(rstd1[:, :], sd1[:, :]).then_inc(rstd1_ready, 1)
                dve.wait_ge(rstd1_ready, g + 1)
                attn_xhat(g, 0, link)
                attn_xhat(g, 1, link)

            first_tokens(0, None)
            attn_front(0, 0)
            attn_front(0, 1)

            def group(g, last):
                link = Link(attn_link, g * A_LINKS)
                attn_g(g, 0)
                attn_v(g, 0)
                attn_xhat(g, 2, link)
                for b in range(G):
                    if b >= 1:
                        attn_rinv(g, b - 1, link)
                        attn_pT(g, b - 1)
                    attn_mask(g, b, link)
                    if b < G - 1:
                        attn_g(g, b + 1)
                    else:
                        disp_norm(g, 0, link)
                        disp_y(g, 0)
                        disp_yT(g, 0)
                    if b >= 1:
                        attn_res(g, b - 1, link)
                    if b == G - 2:
                        disp_vars(g, 0)
                    if b < G - 1:
                        attn_v(g, b + 1)
                    if b < G - 2:
                        attn_front(g, b + 2)
                    if b < G - 3:
                        attn_xhat(g, b + 3, link)

                attn_rinv(g, G - 1, link)
                attn_pT(g, G - 1)
                disp_y(g, 1)
                attn_res(g, G - 1, link)
                disp_vars(g, 1)
                assert link.n == A_LINKS

                link = Link(disp_link, SETUP_LINKS + g * L_LINKS)
                disp_maxT(g, 0, link)
                disp_yT(g, 1)
                disp_scale(g, 0, link)
                disp_split_y(g, 0)
                disp_maxT(g, 1, link)
                disp_d(g, 0)
                disp_max(g, 0, link)
                disp_scale(g, 1, link)
                for i in range(IT):
                    if i == 2:
                        disp_y(g, 3)
                    if i % 2 and i // 2 + 1 < G:
                        disp_split_y(g, i // 2 + 1)
                    if i % 2 and i + 3 < IT:
                        disp_yT(g, (i + 3) // 2)
                    if i == IT - 3:
                        disp_slots(g, i)
                        disp_d(g, i + 1)
                        disp_maxT(g, i + 2, link)
                    elif i + 2 < IT:
                        disp_maxT(g, i + 2, link)
                        disp_d(g, i + 1)
                    if i == IT - 1:
                        dve.wait_ge(slots_ready, (g + 1) * IT * C)
                        round_w2(g, 0, 0)
                        split_hidden(g, 0, 0)
                    if i != IT - 3:
                        disp_slots(g, i)
                    if i == 0:
                        disp_norm(g, 1, link)
                        disp_y(g, 2)
                    if i == IT - 2:
                        disp_d(g, i + 1)
                    if i + 2 < IT:
                        disp_scale(g, i + 2, link)
                    if 0 < i < IT - 3:
                        disp_max(g, (i + 1) // 2, link, [1 - i % 2])
                    if i == IT - 2:
                        disp_max(g, G - 1, link)
                assert link.n == L_LINKS

                def experts(pair, final):
                    t = g * G + 2 + pair
                    link = Link(token_link, TOKEN_LINKS + (t - 2) * T_LINKS)
                    for odd in range(2):
                        e = pair * 2 + odd
                        for j in range(2, J + 2):
                            if j < J:
                                split_hidden(g, e, j)
                            elif not (final and odd):
                                split_hidden(g, e + 1, j - J)
                            if j in (3, 5):
                                round_w2(g, e, j // 2 + 1)
                            if j == 7 and not (final and odd):
                                round_w2(g, e + 1, 0)
                            step = odd * J + j - 2
                            if last:
                                continue
                            if step == 1:
                                gray_rest(t, acc_bank, link)
                            if step in (4, 5):
                                conv_tap(t, step - 4, acc_bank, link)
                            if 8 <= step < 13:
                                conv_tap(t, step - 4, acc_bank, link)
                            if step == 14:
                                edge_sum(t, pair, acc_bank, link)
                        expert_sum(g, e)
                        if final and odd:
                            comb_cls(0)
                            comb_cT(g, 0)
                        else:
                            round_w2(g, e + 1, 1)
                        if not last and not odd:
                            conv_tap(t, 2, acc_bank, link)
                        expert_lo(g, e)
                        if not last and not odd:
                            conv_tap(t, 3, acc_bank, link)
                        if not last and odd:
                            edge_stats(pair, link)
                    assert last or link.n == T_LINKS

                split_hidden(g, 0, 1)
                round_w2(g, 0, 1)
                if not last:
                    nc.vector.memset(gray[:, :, :], 0.0).then_inc(halo_zero, 1)
                with dve.Fori(0, E // 2 - 1) as pair:
                    experts(pair, False)
                experts(E // 2 - 1, True)

                comb_cls(1)
                nc.vector.reciprocal(crinv[:, :], csum[:, :]).then_inc(crinv_ready, 1)
                dve.wait_ge(crinv_ready, g + 1)
                for b in range(G):
                    if b < G - 1:
                        comb_cT(g, b + 1)
                    if b == 0 and not last:
                        first_tokens(g + 1, None)
                    if b >= 1:
                        comb_fin(g, b - 1)
                if not last:
                    attn_front(g + 1, 0)
                    attn_front(g + 1, 1)
                comb_fin(g, G - 1)
                dve.wait_ge(fcls_ready, g + 1)
                dve.wait_ge(cls_stored, 16 * g + 1)
                STT(fcls[:, :], ps[0:G, 512 * 7:512 * 7 + D], rcls[0:G, :], hcls_b[0:G, :], ALU.mult, ALU.add)\
                    .then_inc(fcls_done, 1)

            over_groups(dve, group)


_INS = ['x', 'cls_tok', 'L0_tok_scharr', 'L0_attn_WQ', 'L0_attn_WK', 'L0_attn_WV', 'L0_ffn_norm_gamma',
        'L0_ffn_slot_norm_gamma', 'L0_ffn_slot_embeds', 'L0_ffn_w1', 'L0_ffn_b1', 'L0_ffn_w2', 'L0_ffn_b2']
_OUTS = [((16, 257, 256), 'float32')]


def kernel(**inputs):
    import numpy as _np
    import concourse.bacc as _bacc
    from concourse import mybir as _mybir
    from concourse.bass_utils import run_bass_kernel_spmd as _run

    nc = _bacc.Bacc("TRN2", target_bir_lowering=False, num_devices=1)
    arrays, args = {}, []
    for name in _INS:
        a = _np.ascontiguousarray(inputs[name])
        arrays[f"in_{name}_dram"] = a
        args.append(nc.dram_tensor(f"in_{name}_dram", a.shape, _mybir.dt.from_np(a.dtype), kind="ExternalInput").ap())
    for i, (shape, dtype) in enumerate(_OUTS):
        dt = _mybir.dt.from_np(_np.dtype(dtype))
        args.append(nc.dram_tensor(f"out_{i}_dram", shape, dt, kind="ExternalOutput").ap())
    vit_tower(nc, *args)
    r = _run(nc, [arrays], core_ids=[0])
    got = tuple(r.results[0][f"out_{i}_dram"] for i in range(len(_OUTS)))
    return got[0]
```
